# Optimizing a Trainium2 kernel written in Bass

```python
import numpy as np
import jax
import jax.numpy as jnp

def _softmax(x, axis=-1):
    return jax.nn.softmax(x, axis=axis)

def _gelu(x):
    return jax.nn.gelu(x, approximate=True)

def _silu(x):
    return jax.nn.silu(x)

def _sigmoid(x):
    return jax.nn.sigmoid(x)

def _layernorm(x, axis=-1, eps=1e-05):
    m = jnp.mean(x, axis=axis, keepdims=True)
    v = jnp.var(x, axis=axis, keepdims=True)
    return (x - m) / jnp.sqrt(v + eps)

def _scatter_add(tgt, idx, src, axis=0):
    return tgt.at[idx].add(src)

def _segment_sum(src, seg, n):
    return jax.ops.segment_sum(src, seg, n)
kernel_name = 'mk_vit_tower_cls_d2_tok_img1024_r4_af2195'

def setup_inputs(seed: int=0):
    np.random.seed(seed)
    _w = jnp.asarray

    def _rec_inputs():
        import jax
        import jax.numpy as jnp
        _rk = jax.random.key(seed)
        x = -0.00016672 + 0.999947 * jax.random.normal(jax.random.fold_in(_rk, 1), (32, 3, 96, 96), jnp.float32)
        cls_tok = 0.02 * jax.random.normal(jax.random.fold_in(_rk, 5), (1, 1, 256), jnp.float32)
        return (x, cls_tok)
    x, cls_tok = _rec_inputs()

    def _L0_tok_setup():
        import jax, jax.numpy as jnp
        import numpy as np
        B, C, H, W_IMG = (64, 3, 96, 96)
        P = 16
        EMBED = 256
        PATCH_DIM = C * P * P
        key = jax.random.key(seed)
        k1, k2 = jax.random.split(key)
        x = jax.random.normal(k1, (B, C, H, W_IMG), dtype=jnp.float32)
        W = jax.random.normal(k2, (PATCH_DIM, EMBED), dtype=jnp.float32) * (1.0 / np.sqrt(PATCH_DIM))
        b = jnp.zeros((EMBED,), dtype=jnp.float32)
        return {'x': x, 'W': W, 'b': b}
    _L0_tok_all = _L0_tok_setup()
    _L0_tok_in = {k: v for k, v in _L0_tok_all.items() if k in ('W', 'b')}
    del _L0_tok_all

    def _L0_attn_setup():
        import jax, jax.numpy as jnp
        import numpy as np
        H = 16
        E = 256
        D = E // H
        M = 256
        EPS = 1e-12
        key = jax.random.key(seed)
        ks = jax.random.split(key, 12)
        s = 0.02
        B, S = (8, 256)
        return {'hidden_states': jax.random.normal(ks[0], (B, S, E), jnp.float32), 'Wq': jax.random.normal(ks[1], (E, E), jnp.float32) * s, 'bq': jnp.zeros((E,), jnp.float32), 'Wk': jax.random.normal(ks[2], (E, E), jnp.float32) * s, 'bk': jnp.zeros((E,), jnp.float32), 'Wv': jax.random.normal(ks[3], (E, E), jnp.float32) * s, 'bv': jnp.zeros((E,), jnp.float32), 'dist_emb': jax.random.normal(ks[4], (2 * M - 1, D), jnp.float32) * s, 'Wo': jax.random.normal(ks[5], (E, E), jnp.float32) * s, 'bo': jnp.zeros((E,), jnp.float32), 'ln_gamma': jnp.ones((E,), jnp.float32), 'ln_beta': jnp.zeros((E,), jnp.float32)}
    _L0_attn_all = _L0_attn_setup()
    _L0_attn_in = {k: v for k, v in _L0_attn_all.items() if k in ('Wq', 'bq', 'Wk', 'bk', 'Wv', 'bv', 'dist_emb', 'Wo', 'bo', 'ln_gamma', 'ln_beta')}
    del _L0_attn_all

    def _L0_ffn_setup():
        import jax, jax.numpy as jnp
        import numpy as np
        EPS = 1e-05
        N_HEADS = 16
        TOP_K = 2

        def _ln(x, g, b):
            m = x.mean(-1, keepdims=True)
            v = ((x - m) ** 2).mean(-1, keepdims=True)
            return (x - m) / jnp.sqrt(v + EPS) * g + b

        def _block_fwd(x, ln1_g, ln1_b, ln2_g, ln2_b, Wq, bq, Wk, bk, Wv, bv, Wo, bo, Wr, br, e_w1, e_b1, e_w2, e_b2):
            B, S, D = x.shape
            H = N_HEADS
            hd = D // H
            h = _ln(x, ln1_g, ln1_b)
            q = (h @ Wq + bq).reshape(B, S, H, hd).transpose(0, 2, 1, 3)
            k = (h @ Wk + bk).reshape(B, S, H, hd).transpose(0, 2, 1, 3)
            v = (h @ Wv + bv).reshape(B, S, H, hd).transpose(0, 2, 1, 3)
            scores = jnp.einsum('bhqd,bhkd->bhqk', q, k) / hd ** 0.5
            causal = jnp.tril(jnp.ones((S, S), dtype=bool))
            scores = jnp.where(causal, scores, -jnp.inf)
            attn = jax.nn.softmax(scores, axis=-1)
            o = jnp.einsum('bhqk,bhkd->bhqd', attn, v).transpose(0, 2, 1, 3).reshape(B, S, D)
            a = o @ Wo + bo + x
            h2 = _ln(a, ln2_g, ln2_b)
            logits = h2 @ Wr + br
            topv = jax.lax.top_k(logits, TOP_K)[0]
            kmask = logits >= topv[..., -1:]
            w = jax.nn.softmax(jnp.where(kmask, logits, -jnp.inf), axis=-1)
            mid = jax.nn.gelu(jnp.einsum('bsd,edf->bsef', h2, e_w1) + e_b1, approximate=False)
            eo = jnp.einsum('bsef,efd->bsed', mid, e_w2) + e_b2
            moe = jnp.einsum('bse,bsed->bsd', w, eo)
            return moe + a
        key = jax.random.key(seed)
        B, S, D, E = (1, 512, 256, 8)
        F = 4 * D
        ks = jax.random.split(key, 8)

        def n(k, shape):
            return jax.random.normal(k, shape, jnp.float32) * 0.02
        return dict(x=jax.random.normal(ks[0], (B, S, D), jnp.float32), ln1_g=jnp.ones((D,), jnp.float32), ln1_b=jnp.zeros((D,), jnp.float32), ln2_g=jnp.ones((D,), jnp.float32), ln2_b=jnp.zeros((D,), jnp.float32), Wq=n(ks[1], (D, D)), bq=jnp.zeros((D,), jnp.float32), Wk=n(ks[2], (D, D)), bk=jnp.zeros((D,), jnp.float32), Wv=n(ks[3], (D, D)), bv=jnp.zeros((D,), jnp.float32), Wo=n(ks[4], (D, D)), bo=jnp.zeros((D,), jnp.float32), Wr=n(ks[5], (D, E)), br=jnp.zeros((E,), jnp.float32), e_w1=n(ks[6], (E, D, F)), e_b1=jnp.zeros((E, F), jnp.float32), e_w2=n(ks[7], (E, F, D)), e_b2=jnp.zeros((E, D), jnp.float32))
    _L0_ffn_all = _L0_ffn_setup()
    _L0_ffn_in = {k: v for k, v in _L0_ffn_all.items() if k in ('ln1_g', 'ln1_b', 'ln2_g', 'ln2_b', 'Wq', 'bq', 'Wk', 'bk', 'Wv', 'bv', 'Wo', 'bo', 'Wr', 'br', 'e_w1', 'e_b1', 'e_w2', 'e_b2')}
    del _L0_ffn_all

    def _L1_attn_setup():
        import jax, jax.numpy as jnp
        import numpy as np
        FEATS = 256
        HEAD = 16
        HEAD_DIM = FEATS // HEAD
        EPS = 1e-12

        def _l2norm(t):
            n = jnp.sqrt(jnp.sum(t * t, axis=-1, keepdims=True))
            return t / jnp.maximum(n, EPS)
        key = jax.random.key(seed)
        ks = jax.random.split(key, 10)
        s = 0.02
        inp = {'x': jax.random.normal(ks[0], (4, 512, FEATS), dtype=jnp.float32), 'Wq': jax.random.normal(ks[1], (FEATS, FEATS), dtype=jnp.float32) * s, 'bq': jnp.zeros((FEATS,), dtype=jnp.float32), 'Wk': jax.random.normal(ks[2], (FEATS, FEATS), dtype=jnp.float32) * s, 'bk': jnp.zeros((FEATS,), dtype=jnp.float32), 'Wv': jax.random.normal(ks[3], (FEATS, FEATS), dtype=jnp.float32) * s, 'bv': jnp.zeros((FEATS,), dtype=jnp.float32), 'Wo': jax.random.normal(ks[4], (FEATS, FEATS), dtype=jnp.float32) * s, 'bo': jnp.zeros((FEATS,), dtype=jnp.float32), 'm': jnp.full((HEAD,), 0.5, dtype=jnp.float32)}
        return inp
    _L1_attn_all = _L1_attn_setup()
    _L1_attn_in = {k: v for k, v in _L1_attn_all.items() if k in ('Wq', 'bq', 'Wk', 'bk', 'Wv', 'bv', 'Wo', 'bo', 'm')}
    del _L1_attn_all

    def _L1_ffn_setup():
        import jax, jax.numpy as jnp
        import numpy as np
        D_MODEL = 256
        N_HEADS = 16
        N_KV = 4
        NUM_REP = N_HEADS // N_KV
        HEAD_DIM = D_MODEL // N_HEADS
        N_EXPERTS = 8
        TOP_K = 2
        CAP_FACTOR = 1.25
        EPS_NORM = 1e-06

        def _rmsnorm(x, w):
            var = jnp.mean(x * x, axis=-1, keepdims=True)
            return w * (x * jax.lax.rsqrt(var + EPS_NORM))

        def _gqa(x, qw, qb, kw, kb, vw, vb, ow, ob):
            B, S, D = x.shape
            q = (x @ qw + qb).reshape(B, S, N_HEADS, HEAD_DIM).transpose(0, 2, 1, 3)
            k = (x @ kw + kb).reshape(B, S, N_KV, HEAD_DIM).transpose(0, 2, 1, 3)
            v = (x @ vw + vb).reshape(B, S, N_KV, HEAD_DIM).transpose(0, 2, 1, 3)
            k = jnp.repeat(k, NUM_REP, axis=1)
            v = jnp.repeat(v, NUM_REP, axis=1)
            scores = jnp.einsum('bhqd,bhkd->bhqk', q, k) / np.sqrt(HEAD_DIM).astype(np.float32)
            attn = jax.nn.softmax(scores, axis=-1)
            out = jnp.einsum('bhqk,bhkd->bhqd', attn, v)
            out = out.transpose(0, 2, 1, 3).reshape(B, S, D)
            return out @ ow + ob

        def _moe(x, gate_w, w1, w2):
            B, S, D = x.shape
            T = B * S
            x_flat = x.reshape(T, D)
            capacity = int(CAP_FACTOR * T * TOP_K / N_EXPERTS)
            logits = x_flat @ gate_w
            probs = jax.nn.sigmoid(logits)
            _, sel = jax.lax.top_k(probs, TOP_K)
            w_topk = jnp.take_along_axis(probs, sel, axis=1)
            w_topk = w_topk / (jnp.sum(w_topk, axis=-1, keepdims=True) + 1e-06)
            flat_sel = sel.reshape(-1)
            em = jax.nn.one_hot(flat_sel, N_EXPERTS, dtype=jnp.int32)
            ranks = jnp.take_along_axis(jnp.cumsum(em, axis=0), flat_sel[:, None], axis=1)[:, 0] - 1
            valid = ranks < capacity
            slot = flat_sel * capacity + ranks
            scatter_idx = jnp.where(valid, slot, N_EXPERTS * capacity)
            x_rep = jnp.repeat(x_flat, TOP_K, axis=0)
            padded = jnp.zeros((N_EXPERTS * capacity + 1, D), x.dtype).at[scatter_idx].set(x_rep)
            padded_x = padded[:N_EXPERTS * capacity].reshape(N_EXPERTS, capacity, D)
            h = jax.nn.gelu(jnp.einsum('ecd,edf->ecf', padded_x, w1), approximate=False)
            out_padded = jnp.einsum('ecf,efd->ecd', h, w2).reshape(N_EXPERTS * capacity, D)
            gather_idx = jnp.where(valid, slot, 0)
            out_rep = jnp.where(valid[:, None], out_padded[gather_idx], 0.0)
            out_w = out_rep * w_topk.reshape(-1)[:, None]
            return out_w.reshape(T, TOP_K, D).sum(axis=1).reshape(B, S, D)
        key = jax.random.key(seed)
        ks = jax.random.split(key, 12)
        s = 0.02
        return {'x': jax.random.normal(ks[0], (4, 256, D_MODEL), jnp.float32), 'qw': jax.random.normal(ks[1], (D_MODEL, D_MODEL), jnp.float32) * s, 'qb': jnp.zeros((D_MODEL,), jnp.float32), 'kw': jax.random.normal(ks[2], (D_MODEL, N_KV * HEAD_DIM), jnp.float32) * s, 'kb': jnp.zeros((N_KV * HEAD_DIM,), jnp.float32), 'vw': jax.random.normal(ks[3], (D_MODEL, N_KV * HEAD_DIM), jnp.float32) * s, 'vb': jnp.zeros((N_KV * HEAD_DIM,), jnp.float32), 'ow': jax.random.normal(ks[4], (D_MODEL, D_MODEL), jnp.float32) * s, 'ob': jnp.zeros((D_MODEL,), jnp.float32), 'gate_w': jax.random.normal(ks[5], (D_MODEL, N_EXPERTS), jnp.float32) * s, 'w1': jax.random.normal(ks[6], (N_EXPERTS, D_MODEL, 512), jnp.float32) * s, 'w2': jax.random.normal(ks[7], (N_EXPERTS, 512, D_MODEL), jnp.float32) * s, 'norm1_w': jnp.ones((D_MODEL,), jnp.float32), 'norm2_w': jnp.ones((D_MODEL,), jnp.float32)}
    _L1_ffn_all = _L1_ffn_setup()
    _L1_ffn_in = {k: v for k, v in _L1_ffn_all.items() if k in ('qw', 'qb', 'kw', 'kb', 'vw', 'vb', 'ow', 'ob', 'gate_w', 'w1', 'w2', 'norm1_w', 'norm2_w')}
    del _L1_ffn_all
    return {'x': x, 'cls_tok': cls_tok, 'L0_tok_W': _L0_tok_in['W'], 'L0_tok_b': _L0_tok_in['b'], 'L0_attn_Wq': _L0_attn_in['Wq'], 'L0_attn_bq': _L0_attn_in['bq'], 'L0_attn_Wk': _L0_attn_in['Wk'], 'L0_attn_bk': _L0_attn_in['bk'], 'L0_attn_Wv': _L0_attn_in['Wv'], 'L0_attn_bv': _L0_attn_in['bv'], 'L0_attn_dist_emb': _L0_attn_in['dist_emb'], 'L0_attn_Wo': _L0_attn_in['Wo'], 'L0_attn_bo': _L0_attn_in['bo'], 'L0_attn_ln_gamma': _L0_attn_in['ln_gamma'], 'L0_attn_ln_beta': _L0_attn_in['ln_beta'], 'L0_ffn_ln1_g': _L0_ffn_in['ln1_g'], 'L0_ffn_ln1_b': _L0_ffn_in['ln1_b'], 'L0_ffn_ln2_g': _L0_ffn_in['ln2_g'], 'L0_ffn_ln2_b': _L0_ffn_in['ln2_b'], 'L0_ffn_Wq': _L0_ffn_in['Wq'], 'L0_ffn_bq': _L0_ffn_in['bq'], 'L0_ffn_Wk': _L0_ffn_in['Wk'], 'L0_ffn_bk': _L0_ffn_in['bk'], 'L0_ffn_Wv': _L0_ffn_in['Wv'], 'L0_ffn_bv': _L0_ffn_in['bv'], 'L0_ffn_Wo': _L0_ffn_in['Wo'], 'L0_ffn_bo': _L0_ffn_in['bo'], 'L0_ffn_Wr': _L0_ffn_in['Wr'], 'L0_ffn_br': _L0_ffn_in['br'], 'L0_ffn_e_w1': _L0_ffn_in['e_w1'], 'L0_ffn_e_b1': _L0_ffn_in['e_b1'], 'L0_ffn_e_w2': _L0_ffn_in['e_w2'], 'L0_ffn_e_b2': _L0_ffn_in['e_b2'], 'L1_attn_Wq': _L1_attn_in['Wq'], 'L1_attn_bq': _L1_attn_in['bq'], 'L1_attn_Wk': _L1_attn_in['Wk'], 'L1_attn_bk': _L1_attn_in['bk'], 'L1_attn_Wv': _L1_attn_in['Wv'], 'L1_attn_bv': _L1_attn_in['bv'], 'L1_attn_Wo': _L1_attn_in['Wo'], 'L1_attn_bo': _L1_attn_in['bo'], 'L1_attn_m': _L1_attn_in['m'], 'L1_ffn_qw': _L1_ffn_in['qw'], 'L1_ffn_qb': _L1_ffn_in['qb'], 'L1_ffn_kw': _L1_ffn_in['kw'], 'L1_ffn_kb': _L1_ffn_in['kb'], 'L1_ffn_vw': _L1_ffn_in['vw'], 'L1_ffn_vb': _L1_ffn_in['vb'], 'L1_ffn_ow': _L1_ffn_in['ow'], 'L1_ffn_ob': _L1_ffn_in['ob'], 'L1_ffn_gate_w': _L1_ffn_in['gate_w'], 'L1_ffn_w1': _L1_ffn_in['w1'], 'L1_ffn_w2': _L1_ffn_in['w2'], 'L1_ffn_norm1_w': _L1_ffn_in['norm1_w'], 'L1_ffn_norm2_w': _L1_ffn_in['norm2_w']}

def reference(x, cls_tok, L0_tok_W, L0_tok_b, L0_attn_Wq, L0_attn_bq, L0_attn_Wk, L0_attn_bk, L0_attn_Wv, L0_attn_bv, L0_attn_dist_emb, L0_attn_Wo, L0_attn_bo, L0_attn_ln_gamma, L0_attn_ln_beta, L0_ffn_ln1_g, L0_ffn_ln1_b, L0_ffn_ln2_g, L0_ffn_ln2_b, L0_ffn_Wq, L0_ffn_bq, L0_ffn_Wk, L0_ffn_bk, L0_ffn_Wv, L0_ffn_bv, L0_ffn_Wo, L0_ffn_bo, L0_ffn_Wr, L0_ffn_br, L0_ffn_e_w1, L0_ffn_e_b1, L0_ffn_e_w2, L0_ffn_e_b2, L1_attn_Wq, L1_attn_bq, L1_attn_Wk, L1_attn_bk, L1_attn_Wv, L1_attn_bv, L1_attn_Wo, L1_attn_bo, L1_attn_m, L1_ffn_qw, L1_ffn_qb, L1_ffn_kw, L1_ffn_kb, L1_ffn_vw, L1_ffn_vb, L1_ffn_ow, L1_ffn_ob, L1_ffn_gate_w, L1_ffn_w1, L1_ffn_w2, L1_ffn_norm1_w, L1_ffn_norm2_w):
    import jax
    import jax.numpy as jnp

    def _L0_tok_ref(x, W, b):
        import jax, jax.numpy as jnp
        import numpy as np
        B, C, H, W_IMG = (64, 3, 96, 96)
        P = 16
        EMBED = 256
        PATCH_DIM = C * P * P
        Bn, Cn, Hn, Wn = x.shape
        gh, gw = (Hn // P, Wn // P)
        patches = x.reshape(Bn, Cn, gh, P, gw, P)
        patches = patches.transpose(0, 2, 4, 1, 3, 5)
        patches = patches.reshape(Bn, gh * gw, Cn * P * P)
        return jnp.einsum('bnd,de->bne', patches, W) + b

    def _L0_attn_ref(hidden_states, Wq, bq, Wk, bk, Wv, bv, dist_emb, Wo, bo, ln_gamma, ln_beta):
        import jax, jax.numpy as jnp
        import numpy as np
        H = 16
        E = 256
        D = E // H
        M = 256
        EPS = 1e-12
        B, S, _ = hidden_states.shape

        def heads(x):
            return x.reshape(B, S, H, D).transpose(0, 2, 1, 3)
        q = heads(hidden_states @ Wq + bq)
        k = heads(hidden_states @ Wk + bk)
        v = heads(hidden_states @ Wv + bv)
        scores = jnp.einsum('bhqd,bhkd->bhqk', q, k)
        pos_l = jnp.arange(S)[:, None]
        pos_r = jnp.arange(S)[None, :]
        dist_idx = pos_l - pos_r + M - 1
        pos_emb = dist_emb[dist_idx]
        rel_q = jnp.einsum('bhld,lrd->bhlr', q, pos_emb)
        rel_k = jnp.einsum('bhrd,lrd->bhlr', k, pos_emb)
        scores = (scores + rel_q + rel_k) / jnp.sqrt(jnp.asarray(D, scores.dtype))
        probs = jax.nn.softmax(scores, axis=-1)
        ctx = jnp.einsum('bhqk,bhkd->bhqd', probs, v)
        ctx = ctx.transpose(0, 2, 1, 3).reshape(B, S, E)
        h = ctx @ Wo + bo + hidden_states
        mu = jnp.mean(h, axis=-1, keepdims=True)
        var = jnp.mean(jnp.square(h - mu), axis=-1, keepdims=True)
        out = (h - mu) * jax.lax.rsqrt(var + EPS) * ln_gamma + ln_beta
        return out

    def _L0_ffn_ref(x, ln1_g, ln1_b, ln2_g, ln2_b, Wq, bq, Wk, bk, Wv, bv, Wo, bo, Wr, br, e_w1, e_b1, e_w2, e_b2):
        import jax, jax.numpy as jnp
        import numpy as np
        EPS = 1e-05
        N_HEADS = 16
        TOP_K = 2

        def _ln(x, g, b):
            m = x.mean(-1, keepdims=True)
            v = ((x - m) ** 2).mean(-1, keepdims=True)
            return (x - m) / jnp.sqrt(v + EPS) * g + b

        def _block_fwd(x, ln1_g, ln1_b, ln2_g, ln2_b, Wq, bq, Wk, bk, Wv, bv, Wo, bo, Wr, br, e_w1, e_b1, e_w2, e_b2):
            B, S, D = x.shape
            H = N_HEADS
            hd = D // H
            h = _ln(x, ln1_g, ln1_b)
            q = (h @ Wq + bq).reshape(B, S, H, hd).transpose(0, 2, 1, 3)
            k = (h @ Wk + bk).reshape(B, S, H, hd).transpose(0, 2, 1, 3)
            v = (h @ Wv + bv).reshape(B, S, H, hd).transpose(0, 2, 1, 3)
            scores = jnp.einsum('bhqd,bhkd->bhqk', q, k) / hd ** 0.5
            causal = jnp.tril(jnp.ones((S, S), dtype=bool))
            scores = jnp.where(causal, scores, -jnp.inf)
            attn = jax.nn.softmax(scores, axis=-1)
            o = jnp.einsum('bhqk,bhkd->bhqd', attn, v).transpose(0, 2, 1, 3).reshape(B, S, D)
            a = o @ Wo + bo + x
            h2 = _ln(a, ln2_g, ln2_b)
            logits = h2 @ Wr + br
            topv = jax.lax.top_k(logits, TOP_K)[0]
            kmask = logits >= topv[..., -1:]
            w = jax.nn.softmax(jnp.where(kmask, logits, -jnp.inf), axis=-1)
            mid = jax.nn.gelu(jnp.einsum('bsd,edf->bsef', h2, e_w1) + e_b1, approximate=False)
            eo = jnp.einsum('bsef,efd->bsed', mid, e_w2) + e_b2
            moe = jnp.einsum('bse,bsed->bsd', w, eo)
            return moe + a
        return _block_fwd(x, ln1_g, ln1_b, ln2_g, ln2_b, Wq, bq, Wk, bk, Wv, bv, Wo, bo, Wr, br, e_w1, e_b1, e_w2, e_b2)

    def _L1_attn_ref(x, Wq, bq, Wk, bk, Wv, bv, Wo, bo, m):
        import jax, jax.numpy as jnp
        import numpy as np
        FEATS = 256
        HEAD = 16
        HEAD_DIM = FEATS // HEAD
        EPS = 1e-12

        def _l2norm(t):
            n = jnp.sqrt(jnp.sum(t * t, axis=-1, keepdims=True))
            return t / jnp.maximum(n, EPS)
        b, n, f = x.shape

        def proj(W, bias):
            y = x @ W + bias
            return y.reshape(b, n, HEAD, HEAD_DIM).transpose(0, 2, 1, 3)
        q = _l2norm(proj(Wq, bq))
        k = _l2norm(proj(Wk, bk))
        v = proj(Wv, bv)
        sim = jnp.einsum('bhid,bhjd->bhij', q, k)
        sigma_m = jax.nn.sigmoid(m).reshape(1, HEAD, 1, 1)
        scaling = jnp.asarray(n, dtype=x.dtype) ** sigma_m
        attn = sim / scaling
        out = jnp.einsum('bhij,bhjd->bhid', attn, v)
        out = out.transpose(0, 2, 1, 3).reshape(b, n, f)
        return out @ Wo + bo

    def _L1_ffn_ref(x, qw, qb, kw, kb, vw, vb, ow, ob, gate_w, w1, w2, norm1_w, norm2_w):
        import jax, jax.numpy as jnp
        import numpy as np
        D_MODEL = 256
        N_HEADS = 16
        N_KV = 4
        NUM_REP = N_HEADS // N_KV
        HEAD_DIM = D_MODEL // N_HEADS
        N_EXPERTS = 8
        TOP_K = 2
        CAP_FACTOR = 1.25
        EPS_NORM = 1e-06

        def _rmsnorm(x, w):
            var = jnp.mean(x * x, axis=-1, keepdims=True)
            return w * (x * jax.lax.rsqrt(var + EPS_NORM))

        def _gqa(x, qw, qb, kw, kb, vw, vb, ow, ob):
            B, S, D = x.shape
            q = (x @ qw + qb).reshape(B, S, N_HEADS, HEAD_DIM).transpose(0, 2, 1, 3)
            k = (x @ kw + kb).reshape(B, S, N_KV, HEAD_DIM).transpose(0, 2, 1, 3)
            v = (x @ vw + vb).reshape(B, S, N_KV, HEAD_DIM).transpose(0, 2, 1, 3)
            k = jnp.repeat(k, NUM_REP, axis=1)
            v = jnp.repeat(v, NUM_REP, axis=1)
            scores = jnp.einsum('bhqd,bhkd->bhqk', q, k) / np.sqrt(HEAD_DIM).astype(np.float32)
            attn = jax.nn.softmax(scores, axis=-1)
            out = jnp.einsum('bhqk,bhkd->bhqd', attn, v)
            out = out.transpose(0, 2, 1, 3).reshape(B, S, D)
            return out @ ow + ob

        def _moe(x, gate_w, w1, w2):
            B, S, D = x.shape
            T = B * S
            x_flat = x.reshape(T, D)
            capacity = int(CAP_FACTOR * T * TOP_K / N_EXPERTS)
            logits = x_flat @ gate_w
            probs = jax.nn.sigmoid(logits)
            _, sel = jax.lax.top_k(probs, TOP_K)
            w_topk = jnp.take_along_axis(probs, sel, axis=1)
            w_topk = w_topk / (jnp.sum(w_topk, axis=-1, keepdims=True) + 1e-06)
            flat_sel = sel.reshape(-1)
            em = jax.nn.one_hot(flat_sel, N_EXPERTS, dtype=jnp.int32)
            ranks = jnp.take_along_axis(jnp.cumsum(em, axis=0), flat_sel[:, None], axis=1)[:, 0] - 1
            valid = ranks < capacity
            slot = flat_sel * capacity + ranks
            scatter_idx = jnp.where(valid, slot, N_EXPERTS * capacity)
            x_rep = jnp.repeat(x_flat, TOP_K, axis=0)
            padded = jnp.zeros((N_EXPERTS * capacity + 1, D), x.dtype).at[scatter_idx].set(x_rep)
            padded_x = padded[:N_EXPERTS * capacity].reshape(N_EXPERTS, capacity, D)
            h = jax.nn.gelu(jnp.einsum('ecd,edf->ecf', padded_x, w1), approximate=False)
            out_padded = jnp.einsum('ecf,efd->ecd', h, w2).reshape(N_EXPERTS * capacity, D)
            gather_idx = jnp.where(valid, slot, 0)
            out_rep = jnp.where(valid[:, None], out_padded[gather_idx], 0.0)
            out_w = out_rep * w_topk.reshape(-1)[:, None]
            return out_w.reshape(T, TOP_K, D).sum(axis=1).reshape(B, S, D)
        src = x + _gqa(x, qw, qb, kw, kb, vw, vb, ow, ob)
        src = _rmsnorm(src, norm1_w)
        src = src + _moe(src, gate_w, w1, w2)
        return _rmsnorm(src, norm2_w)
    h = _L0_tok_ref(x, L0_tok_W, L0_tok_b)
    h = jnp.concatenate([jnp.broadcast_to(cls_tok, (h.shape[0], 1, h.shape[2])), h], axis=1)
    h = h + _L0_attn_ref(_layernorm(h, axis=-1), L0_attn_Wq, L0_attn_bq, L0_attn_Wk, L0_attn_bk, L0_attn_Wv, L0_attn_bv, L0_attn_dist_emb, L0_attn_Wo, L0_attn_bo, L0_attn_ln_gamma, L0_attn_ln_beta)
    h = h + _L0_ffn_ref(_layernorm(h, axis=-1), L0_ffn_ln1_g, L0_ffn_ln1_b, L0_ffn_ln2_g, L0_ffn_ln2_b, L0_ffn_Wq, L0_ffn_bq, L0_ffn_Wk, L0_ffn_bk, L0_ffn_Wv, L0_ffn_bv, L0_ffn_Wo, L0_ffn_bo, L0_ffn_Wr, L0_ffn_br, L0_ffn_e_w1, L0_ffn_e_b1, L0_ffn_e_w2, L0_ffn_e_b2)
    h = h + _L1_attn_ref(_layernorm(h, axis=-1), L1_attn_Wq, L1_attn_bq, L1_attn_Wk, L1_attn_bk, L1_attn_Wv, L1_attn_bv, L1_attn_Wo, L1_attn_bo, L1_attn_m)
    h = h + _L1_ffn_ref(_layernorm(h, axis=-1), L1_ffn_qw, L1_ffn_qb, L1_ffn_kw, L1_ffn_kb, L1_ffn_vw, L1_ffn_vb, L1_ffn_ow, L1_ffn_ob, L1_ffn_gate_w, L1_ffn_w1, L1_ffn_w2, L1_ffn_norm1_w, L1_ffn_norm2_w)
    return h

_drawn_inputs = setup_inputs


def setup_inputs(seed=0):
    import zlib

    import numpy as np

    out = dict(_drawn_inputs(seed))
    spreads = {'L0_tok_b': (0.0, 0.1),
     'L0_attn_bq': (0.0, 0.8),
     'L0_attn_bk': (0.0, 0.8),
     'L0_attn_bv': (0.0, 0.458),
     'L0_attn_bo': (0.0, 0.1),
     'L0_attn_ln_gamma': (1.0, 0.2),
     'L0_attn_ln_beta': (0.0, 0.1),
     'L0_ffn_ln1_g': (1.0, 0.6),
     'L0_ffn_ln1_b': (0.0, 0.8),
     'L0_ffn_ln2_g': (1.0, 0.6),
     'L0_ffn_ln2_b': (0.0, 0.725),
     'L0_ffn_bq': (0.0, 0.8),
     'L0_ffn_bk': (0.0, 0.8),
     'L0_ffn_bv': (0.0, 0.701),
     'L0_ffn_bo': (0.0, 0.1),
     'L0_ffn_br': (0.0, 0.303),
     'L0_ffn_e_b1': (0.0, 0.8),
     'L0_ffn_e_b2': (0.0, 0.346),
     'L1_attn_bq': (0.0, 0.8),
     'L1_attn_bk': (0.0, 0.8),
     'L1_attn_bv': (0.0, 0.8),
     'L1_attn_bo': (0.0, 0.1),
     'L1_attn_m': (0.5, 0.6),
     'L1_ffn_qb': (0.0, 0.8),
     'L1_ffn_kb': (0.0, 0.8),
     'L1_ffn_vb': (0.0, 0.8),
     'L1_ffn_ob': (0.0, 0.354),
     'L1_ffn_norm1_w': (1.0, 0.2),
     'L1_ffn_norm2_w': (1.0, 0.2)}
    factors = {'L0_attn_Wq': 8.0,
     'L0_attn_Wk': 8.0,
     'L0_attn_Wv': 5.351,
     'L0_attn_dist_emb': 8.0,
     'L0_attn_Wo': 2.754,
     'L0_ffn_Wq': 8.0,
     'L0_ffn_Wk': 8.0,
     'L0_ffn_Wv': 4.048,
     'L0_ffn_Wo': 3.142,
     'L1_attn_Wq': 8.0,
     'L1_attn_Wk': 8.0,
     'L1_attn_Wv': 8.0,
     'L1_attn_Wo': 7.992,
     'L1_ffn_qw': 8.0,
     'L1_ffn_kw': 8.0,
     'L1_ffn_vw': 8.0,
     'L1_ffn_ow': 4.999,
     'L1_ffn_gate_w': 4.533,
     'L1_ffn_w1': 4.044,
     'L1_ffn_w2': 3.94}
    for name, (base, spread) in spreads.items():
        noise = np.random.default_rng([zlib.crc32(name.encode()), seed]).standard_normal(out[name].shape)
        drawn = base * np.exp(spread * noise) if base else spread * noise
        out[name] = jnp.asarray(drawn.astype(out[name].dtype))
    for name, factor in factors.items():
        out[name] = (out[name] * factor).astype(out[name].dtype)
    return out
```

```python
from contextlib import ExitStack

import numpy as np

import concourse.bass as bass
from concourse import mybir

F32 = mybir.dt.float32
ALU = mybir.AluOpType
ACT = mybir.ActivationFunctionType
AX = mybir.AxisListType

IMAGES, PER = 32, 3
GROUPS = -(-IMAGES // PER)
PATCH, SIDE = 16, 6
SEQ = SIDE * SIDE + 1
TOK = PER * SEQ
E, HEADS, HD = 256, 16, 16
CT = E // 128
HC = HEADS // CT
PK = 3 * PATCH * PATCH // 128
K0, K1 = (SEQ + 1) // 2, SEQ // 2
HS = SEQ * HEADS
REL = 2 * SEQ - 1
REL_CUTS = (0, 25, 49, 73)
HPC = 3
CHUNKS = -(-HEADS // HPC)
EXPERTS = 8
F0, F1 = 1024, 512
CAPACITY = int(1.25 * IMAGES * SEQ * 2 / EXPERTS)
SPANS = ((0, 4), (4, 8), (8, 11))
EPS, EPS_A, EPS_R = 1e-5, 1e-12, 1e-6
MASKED = -1e30

ROWS = ["a_bo", "a_g", "a_b", "f_bo", "l_bq", "l_bk", "l_bv", "l_bo", "g_ob", "g_n1", "g_n2"]
COLS = ["a_bq", "a_bk", "a_bv", "f_g1", "f_b1", "f_g2", "f_b2", "f_bq", "f_bk", "f_bv",
        "g_qb", "g_kb", "g_vb", "l_m"]
MATS = ["a_Wq", "a_Wk", "a_Wv", "a_Wo", "f_Wq", "f_Wk", "f_Wv", "f_Wo", "l_Wq", "l_Wk", "l_Wv",
        "l_Wo", "g_Wq", "g_Wk", "g_Wv", "g_Wo"]


def build_tower(nc, A):
    ctx = ExitStack()
    with ctx:
        def sb(name, shape):
            return ctx.enter_context(nc.sbuf_tensor("sb_" + name, shape, F32))

        def sem(name):
            return ctx.enter_context(nc.semaphore(name))

        bank = [ctx.enter_context(nc.psum_tensor(f"bank{i}", [128, 512], F32)) for i in range(8)]

        ident = sb("ident", [128, 128])
        head_of_row = sb("head_of_row", [128, HC])
        third_of_head = sb("third_of_head", [TOK, HEADS])
        causal = sb("causal", [TOK, SEQ])
        of_image = sb("of_image", [TOK, PER])
        same_head = sb("same_head", [128, 128])
        before = sb("before", [TOK, TOK])
        ones = sb("ones", [TOK, TOK])
        half = sb("half", [TOK, 1])
        idle = sb("idle", [1, 64])
        eps = sb("eps", [TOK, 3])
        rev8 = sb("rev8", [TOK, EXPERTS])
        rows = sb("rows", [TOK, len(ROWS), E])
        cols = sb("cols", [128, len(COLS), CT])
        mats = sb("mats", [128, len(MATS), CT, E])
        wtok = sb("wtok", [128, PK, E])
        base = sb("base", [TOK, E])
        relq = sb("relq", [128, REL, HC])
        relk = sb("relk", [128, REL, HC])
        wr0 = sb("wr0", [128, CT, EXPERTS])
        wr1 = sb("wr1", [128, CT, EXPERTS])
        br0 = sb("br0", [TOK, EXPERTS])
        b_up = [sb(f"b_up{i}", [128, F0 // 128]) for i in range(2)]
        eb2 = sb("eb2", [EXPERTS, E])
        inv_scale = sb("inv_scale", [128, 2, CT])

        def row(name):
            return rows[:, ROWS.index(name), :]

        def col(name, c):
            return cols[:, COLS.index(name), c:c + 1]

        def mat(name, c, lo=0, hi=E):
            return mats[:, MATS.index(name), c, lo:hi]

        H = sb("H", [TOK, GROUPS * E])
        SRC_all = sb("SRC", [128, GROUPS * E])
        SRC = SRC_all[0:TOK, :]
        XT = sb("XT", [128, CT, GROUPS * TOK])
        LOGITS = sb("LOGITS", [TOK, GROUPS, EXPERTS])
        GATE = sb("GATE", [TOK, GROUPS, EXPERTS])
        GATE_E = sb("GATE_E", [TOK, EXPERTS * GROUPS])
        w_up = [sb(f"w_up{i}", [128, CT * F0]) for i in range(2)]
        w_dn = [sb(f"w_dn{i}", [128, F0 // 128 * E]) for i in range(2)]
        mid_flat = sb("mid", [128, F0 // 128 * 4 * TOK])
        mid = mid_flat[:, :].rearrange("p (f t) -> p f t", t=4 * TOK)
        rel_scratch = {n: nc.dram_tensor("scratch_" + n, [2, TOK, REL * HEADS], F32, kind="Internal").ap()
                       for n in ("q", "k")}

        def of_group(t, g, width=E):
            return t[:, bass.ds(g * width, width)]

        DVE_LINKS = {"rel": 10, "causal": 7, "gqa": 8}
        POOL_LINKS = {"rel": 2, "causal": 2, "gqa": 2}

        def attention(tag, banks, same_buffers=None):
            L = dict(tag=tag, b=banks, at=0, dve_at=0, pool_at=0)
            if same_buffers:
                L.update(same_buffers)
                L["tag"], L["at"] = tag, GROUPS
                L["dve_at"], L["pool_at"] = (GROUPS * k[same_buffers["tag"]] for k in (DVE_LINKS, POOL_LINKS))
                return L
            for n, shape in dict(
                    xin=[TOK, E], res=[TOK, E], hold=[TOK, E], work=[TOK, E], work2=[TOK, E],
                    xT=[128, CT, TOK], qT=[128, CT, TOK], kT=[128, CT, TOK], qM=[128, CT, PER, TOK],
                    kB=[128, CT, TOK, HC], vB=[TOK, PER, E], sc=[TOK, HS], pr=[TOK, HS],
                    mx=[TOK, HEADS], sm=[TOK, HEADS], pT=[128, CHUNKS, TOK], cx=[SEQ, PER, E],
                    cT=[128, CT, TOK], st=[TOK, 6], mv=[TOK, 2], va=[TOK, 2], rs=[TOK, 2],
                    st2=[TOK, 6], mv2=[TOK, 2], va2=[TOK, 1], rs2=[TOK, 1]).items():
                L[n] = sb(f"{tag}_{n}", shape)
            L["x3"] = L["pT"][:].rearrange("p t q -> p (t q)").rearrange("p (c j r k) -> p c j (r k)", c=CT, j=PER, r=HPC)
            for n in ("x3", "xin", "xT_psum", "xT", "qk_psum", "v_psum", "qT", "kT", "qM", "kB", "vB", "s_psum",
                      "shifted", "exped", "probs", "pT_psum", "pT", "c_psum", "cx", "cT_psum", "cT", "o_psum",
                      "stat", "rstd", "stat2", "rstd2", "in2", "bias_in", "done", "dve", "pool"):
                L["s_" + n] = sem(f"{tag}_{n}")
            return L

        a1 = attention("rel", bank[0:4])
        a2 = attention("causal", bank[4:8])
        a3 = attention("gqa", bank[4:8], same_buffers=a2)
        s_zeroed = sem("s_zeroed")

        patches = SRC_all[:, 0:PK * TOK].rearrange("p (k t) -> p k t", t=TOK)
        qe = mid_flat[0:TOK, 0:2 * REL * HEADS].rearrange("p (i r) -> p i r", i=2)
        relb = mid_flat[0:TOK, 2 * REL * HEADS:2 * REL * HEADS + 2 * HS].rearrange("p (i r) -> p i r", i=2)
        nT = sb("nT", [128, CT, TOK])
        gT = sb("gT", [128, CT, TOK])

        ln = dict(b=bank[0:4])
        kb_flat = a1["kB"][:].rearrange("p c t h -> p (c t h)")
        ln.update(xin=a1["xin"], hold=a1["hold"], xT=a1["xT"], q=a1["vB"], qT=a1["qT"], cT=a1["cT"],
                           sq=a1["sc"][:, 0:2 * E].rearrange("p (i e) -> p i e", i=2),
                           km=kb_flat[0:TOK, 0:PER * E].rearrange("p (j e) -> p j e", j=PER),
                           kv=kb_flat[:, PER * E:2 * PER * E].rearrange("p (c j d) -> p c j d", c=CT, j=PER))
        for n, shape in dict(ss=[TOK, 2, HEADS], ri=[TOK, 2, HEADS], st=[TOK, 6], mv=[TOK, 2],
                             va=[TOK, 1], rs=[TOK, 1]).items():
            ln[n] = sb("cos_" + n, shape)
        for n in ("stat", "rstd", "xin", "xT_psum", "xT", "qkv_psum", "qkv", "squares", "norm2", "norm", "qn",
                  "km", "qT_psum", "qT", "kv_psum", "kv", "cT_psum", "cT", "o_psum", "bias_in", "done", "dve",
                  "act", "pool"):
            ln["s_" + n] = sem("cos_" + n)
        LN_LINKS = 3

        s_const = sem("s_const")
        s_patch = sem("s_patch")
        s_tok = sem("s_tok")
        s_qe_psum = sem("s_qe_psum")
        s_qe = sem("s_qe")
        s_qe_out = [sem(f"s_qe_out{i}") for i in range(2)]
        s_rel_in = sem("s_rel_in")
        s_relsum = sem("s_relsum")
        s_nT_psum = sem("s_nT_psum")
        s_nT = sem("s_nT")
        s_log = sem("s_log")
        s_lg = sem("s_lg")
        s_XT = sem("s_XT")
        s_scale = sem("s_scale")
        s_scale2 = sem("s_scale2")
        s_gT_psum = sem("s_gT_psum")
        s_gT = sem("s_gT")
        s_glog = sem("s_glog")
        s_glg = sem("s_glg")
        s_GXT = sem("s_GXT")

        def mixture(tag):
            M = dict(tag=tag)
            for n in ("gate", "gT_psum", "gT", "b_psum", "b_add", "w0", "w1", "up", "act", "down",
                      "acc", "dve", "probs", "rank_psum", "exp"):
                M["s_" + n] = sem(f"{tag}_{n}")
            return M

        m0, m1 = mixture("moe0"), mixture("moe1")
        RING = 4
        tmp8 = [sb(f"tmp8_{i}", [TOK, GROUPS, EXPERTS]) for i in range(6)]
        tmp1 = [sb(f"tmp1_{i}", [TOK, GROUPS]) for i in range(3)]
        top8 = sb("top8", [TOK, GROUPS, 8])
        gateT = SRC_all[0:EXPERTS, PK * TOK:PK * TOK + GROUPS * TOK].rearrange("p (g t) -> p g t", t=TOK)
        s_fin_stat = sem("s_fin_stat")
        s_fin_rstd = sem("s_fin_rstd")
        s_fin = sem("s_fin")
        s_out = sem("s_out")
        s_fin_dve = sem("s_fin_dve")
        s_fin_pool = sem("s_fin_pool")
        fin = dict(st=sb("fin_st", [TOK, GROUPS, 6]), mv=sb("fin_mv", [TOK, GROUPS, 2]),
                              va=sb("fin_va", [TOK, GROUPS]), rs=sb("fin_rs", [TOK, GROUPS]))

        loads = [(ident, A["c_ident"]), (head_of_row, A["c_head_of_row"]), (third_of_head, A["c_third"]),
                 (causal, A["c_causal"]), (of_image, A["c_of_image"]), (same_head, A["c_same_head"]),
                 (before, A["c_before"]), (rev8, A["c_rev8"]), (base, A["base"]), (wtok, A["wtok"]),
                 (cols, A["cols"]), (relq, A["relq"]), (relk, A["relk"]), (wr0, A["wr0"]), (wr1, A["wr1"]),
                 (eb2, A["eb2"]), (mats, A["mats"])]
        N_LOADS = len(loads) + 2

        carriers = [0]

        def idle_element():
            carriers[0] += 1
            return idle[0:1, carriers[0] - 1:carriers[0]]

        def carry_dve():
            nc.vector.memset(idle_element(), 0.0)

        def carry_pool():
            nc.gpsimd.tensor_tensor(idle_element(), half[0:1, :], half[0:1, :], ALU.add)

        def carry_pe(free):
            nc.tensor.matmul(free[0:1, 0:1], ident[:, 0:1], ident[:, 0:1], start=True, stop=True)

        block = ctx.enter_context(nc.Block())

        @block.sync
        def _(sp):
            for dst, src in loads:
                sp.dma_start(dst[:], src[:]).then_inc(s_const, 16)
            sp.dma_start(rows[:].rearrange("p r e -> p (r e)"),
                         A["rows"].rearrange("r e -> (r e)").partition_broadcast(TOK)).then_inc(s_const, 16)
            sp.dma_start(br0[:], A["br0"].partition_broadcast(TOK)).then_inc(s_const, 16)

            def load_pair(M, up, down, width, i=0, wait=False):
                for b in range(2):
                    e = 2 * i + b
                    if wait:
                        sp.wait_ge(M["s_down"], (e - 1) * GROUPS)
                    done = M["s_w1"] if b else M["s_w0"]
                    if M is m0:
                        sp.dma_start(b_up[b][:], A["eb1"][bass.ds(e, 1)].rearrange("o p n -> p (o n)"))\
                            .then_inc(done, 16)
                    sp.dma_start(w_up[b][:, 0:CT * width], up[bass.ds(e, 1)].rearrange("o p n -> p (o n)"))\
                        .then_inc(done, 16)
                    sp.dma_start(w_dn[b][:, 0:width // 128 * E],
                                 down[bass.ds(e, 1)].rearrange("o p n -> p (o n)")).then_inc(done, 16)

            def load_rest(M, up, down, width):
                with sp.Fori(1, EXPERTS // 2) as i:
                    load_pair(M, up, down, width, i, True)

            def send_relative(n):
                for i, way in enumerate(("q", "k")):
                    sp.wait_ge(s_qe, 6 * n + 3 * i + 3)
                    dst = rel_scratch[way][0]
                    sp.dma_start(dst, qe[:, i, :]).then_inc(s_qe_out[i], 16)
                for i, way in enumerate(("q", "k")):
                    sp.wait_ge(s_qe_out[i], 16 * (n + 1))
                    src = rel_scratch[way]
                    wide = REL * HEADS
                    for j in range(PER):
                        at = src.offset + j * SEQ * wide + (SEQ - 1) * HEADS
                        if way == "q":
                            ap = [[wide - HEADS, SEQ], [1, HS]]
                        else:
                            ap = [[HEADS, SEQ], [wide - HEADS, SEQ], [1, HEADS]]
                        dst = relb[j * SEQ:(j + 1) * SEQ, i, :]
                        if way == "k":
                            dst = dst.rearrange("p (r h) -> p r h", h=HEADS)
                        sp.dma_start(dst, bass.AP(tensor=src.tensor, offset=at, ap=ap)).then_inc(s_rel_in, 16)

            sp.dma_start(patches, A["xT"][0]).then_inc(s_patch, 16)
            load_pair(m0, A["e_w1"], A["e_w2"], F0)
            send_relative(0)
            with sp.Fori(1, GROUPS) as n:
                sp.wait_ge(s_tok, n)
                sp.dma_start(patches, A["xT"][bass.ds(n, 1)].rearrange("o p k t -> p (o k) t"))\
                    .then_inc(s_patch, 16)
                send_relative(n)

            load_rest(m0, A["e_w1"], A["e_w2"], F0)
            sp.wait_ge(m0["s_down"], EXPERTS * GROUPS)
            load_pair(m1, A["g_w1"], A["g_w2"], F1)
            load_rest(m1, A["g_w1"], A["g_w2"], F1)
            sp.wait_ge(s_fin, GROUPS)
            sp.dma_start(A["out"], H[:]).then_inc(s_out, 16)
            sp.wait_ge(s_out, 16)

        @block.tensor
        def _(pe):
            def transpose_in(L, n):
                pe.wait_ge(L["s_xin"], L["at"] + n + 1)
                for c in range(CT):
                    last = nc.tensor.transpose(L["b"][0][:, c * TOK:(c + 1) * TOK], L["xin"][:, c * 128:(c + 1) * 128],
                                               ident[0:TOK, 0:TOK])
                last.then_inc(L["s_xT_psum"], 1)

            def project(L, n, p):
                pe.wait_ge(L["s_xT"], L["at"] + n + 1)
                for w, dst in (("q", L["b"][1]), ("k", L["b"][2])):
                    for m in range(CT):
                        for c in range(CT):
                            last = nc.tensor.matmul(dst[:, m * TOK:(m + 1) * TOK],
                                                    mat(f"{p}_W{w}", c, m * 128, (m + 1) * 128), L["xT"][:, c, :],
                                                    start=(c == 0), stop=(c == CT - 1))
                last.then_inc(L["s_qk_psum"], 1)
                pe.wait_ge(L["s_x3"], L["at"] + n + 1)
                for j in range(PER):
                    dst = (L["b"][0][0:TOK, j * E:(j + 1) * E] if j < 2 else L["b"][3][0:TOK, 0:E])
                    for c in range(CT):
                        last = nc.tensor.matmul(dst, L["x3"][:, c, j, :], mat(f"{p}_Wv", c), start=(c == 0), stop=(c == CT - 1))
                last.then_inc(L["s_v_psum"], 1)

            def scores(L, n):
                pe.wait_ge(L["s_kB"], L["at"] + n + 1)
                pe.wait_ge(L["s_qM"], L["at"] + n + 1)
                for b, (lo, hi) in enumerate(((0, K0), (K0, SEQ))):
                    dst = L["b"][1 + b][0:TOK, 0:(hi - lo) * HEADS].rearrange("p (k h) -> p k h", h=HEADS)
                    for j in range(PER):
                        for c in range(CT):
                            last = nc.tensor.matmul(dst[:, :, c * HC:(c + 1) * HC], L["qM"][:, c, j, :],
                                                    L["kB"][:, c, j * SEQ + lo:j * SEQ + hi, :],
                                                    start=(j == 0 and c == 0), stop=(j == PER - 1 and c == CT - 1),
                                                    skip_group_check=True)
                last.then_inc(L["s_s_psum"], 1)

            def transpose_probs(L, n):
                pe.wait_ge(L["s_probs"], L["at"] + n + 1)
                for t in range(CHUNKS):
                    w = min(HPC * SEQ, HS - t * HPC * SEQ)
                    dst = L["b"][0 if t < 3 else 3][0:w, (t % 3) * TOK:(t % 3 + 1) * TOK]
                    last = nc.tensor.transpose(dst, L["pr"][:, t * HPC * SEQ:t * HPC * SEQ + w], ident[0:TOK, 0:TOK])
                last.then_inc(L["s_pT_psum"], 1)

            def contexts(L, n):
                pe.wait_ge(L["s_pT"], L["at"] + n + 1)
                for j in range(PER):
                    dst = L["b"][1][0:SEQ, j * E:(j + 1) * E] if j < 2 else L["b"][2][0:SEQ, 0:E]
                    for t in range(CHUNKS):
                        h = min(HPC, HEADS - t * HPC)
                        at = t * HPC * HD
                        last = nc.tensor.matmul(dst[:, at:at + h * HD],
                                                L["pT"][0:h * SEQ, t, j * SEQ:(j + 1) * SEQ],
                                                L["vB"][0:h * SEQ, j, at:at + h * HD],
                                                start=True, stop=True)
                last.then_inc(L["s_c_psum"], 1)

            def transpose_ctx(L, n):
                pe.wait_ge(L["s_cx"], L["at"] + n + 1)
                carry_pe(L["b"][0])
                for c in range(CT):
                    for j in range(PER):
                        at = c * TOK + j * SEQ
                        last = nc.tensor.transpose(L["b"][0][:, at:at + SEQ], L["cx"][:, j, c * 128:(c + 1) * 128],
                                                   ident[0:SEQ, 0:SEQ])
                last.then_inc(L["s_cT_psum"], 1)

            def output(L, n, p):
                pe.wait_ge(L["s_cT"], L["at"] + n + 1)
                for c in range(CT):
                    last = nc.tensor.matmul(L["b"][3][0:TOK, 0:E], L["cT"][:, c, :], mat(f"{p}_Wo", c),
                                            start=(c == 0), stop=(c == CT - 1))
                last.then_inc(L["s_o_psum"], 1)

            def embed(n, first=False):
                pe.wait_ge(s_patch, 16 * (n + 1))
                if not first:
                    pe.wait_ge(a1["s_done"], n)
                for k in range(PK):
                    last = nc.tensor.matmul(bank[1][0:TOK, 0:E], patches[:, k, :], wtok[:, k, :],
                                            start=(k == 0), stop=(k == PK - 1))
                last.then_inc(s_tok, 1)

            def distances(n):
                pe.wait_ge(a1["s_qT"], n + 1)
                pe.wait_ge(a1["s_kT"], n + 1)
                pe.wait_ge(a1["s_vB"], n + 1)
                for i, (x, table) in enumerate(((a1["qT"], relq), (a1["kT"], relk))):
                    for part in range(3):
                        u = 3 * i + part
                        lo, hi = REL_CUTS[part], REL_CUTS[part + 1]
                        if u >= 2:
                            pe.wait_ge(s_qe, 6 * n + u - 1)
                        dst = a1["b"][0 if u % 2 == 0 else 3][0:TOK, 0:(hi - lo) * HEADS]
                        dst = dst.rearrange("p (r h) -> p r h", h=HEADS)
                        for c in range(CT):
                            last = nc.tensor.matmul(dst[:, :, c * HC:(c + 1) * HC], x[:, c, :],
                                                    table[:, lo:hi, :], start=(c == 0), stop=(c == CT - 1),
                                                    skip_group_check=True)
                        last.then_inc(s_qe_psum, 1)

            def router(L, n, s_in, src, s_psum, s_T, dstT, w, s_logit):
                pe.wait_ge(s_in, L["at"] + n + 1)
                for c in range(CT):
                    last = nc.tensor.transpose(L["b"][0][:, c * TOK:(c + 1) * TOK], src[:, c * 128:(c + 1) * 128],
                                               ident[0:TOK, 0:TOK])
                last.then_inc(s_psum, 1)
                pe.wait_ge(s_T, n + 1)
                for c in range(CT):
                    last = nc.tensor.matmul(L["b"][1][0:TOK, 0:EXPERTS], dstT[:, c, :], w[:, c, :],
                                            start=(c == 0), stop=(c == CT - 1))
                last.then_inc(s_logit, 1)

            def rel_first(n, first=False):
                embed(n, first)
                transpose_in(a1, n)
                project(a1, n, "a")

            def rel_block(n, first=False):
                rel_first(n, first)
                distances(n)
                scores(a1, n)
                transpose_probs(a1, n)
                contexts(a1, n)
                transpose_ctx(a1, n)
                output(a1, n, "a")

            def causal_block(n):
                transpose_in(a2, n)
                project(a2, n, "f")
                scores(a2, n)
                transpose_probs(a2, n)
                contexts(a2, n)
                transpose_ctx(a2, n)
                output(a2, n, "f")
                router(a2, n, a2["s_in2"], a2["work2"], s_nT_psum, s_nT, nT, wr0, s_log)

            pe.wait_ge(s_const, 16 * N_LOADS)
            rel_block(0, first=True)
            with pe.Fori(1, GROUPS) as n:
                embed(n)
                transpose_in(a2, n - 1)
                transpose_in(a1, n)
                project(a2, n - 1, "f")
                project(a1, n, "a")
                scores(a2, n - 1)
                distances(n)
                scores(a1, n)
                transpose_probs(a2, n - 1)
                contexts(a2, n - 1)
                transpose_ctx(a2, n - 1)
                transpose_probs(a1, n)
                output(a2, n - 1, "f")
                contexts(a1, n)
                router(a2, n - 1, a2["s_in2"], a2["work2"], s_nT_psum, s_nT, nT, wr0, s_log)
                transpose_ctx(a1, n)
                output(a1, n, "a")
            causal_block(GROUPS - 1)

            def gates_transposed(M):
                pe.wait_ge(M["s_gate"], 1)
                for g in range(GROUPS):
                    last = nc.tensor.transpose(bank[g // 4][0:EXPERTS, (g % 4) * TOK:(g % 4 + 1) * TOK],
                                               GATE[:, g, :], ident[0:TOK, 0:TOK])
                last.then_inc(M["s_gT_psum"], 1)
                pe.wait_ge(M["s_gT"], 1)
                for g in range(GROUPS):
                    if g >= 4:
                        pe.wait_ge(M["s_b_add"], g - 3)
                    nc.tensor.matmul(bank[4 + g % 4][0:TOK, 0:E], gateT[:, g, :], eb2[:, :],
                                     start=True, stop=True).then_inc(M["s_b_psum"], 1)

            def experts(M, width, loads_each):
                nf = width // 128
                with pe.Fori(0, EXPERTS // 2) as i:
                    for b in range(2):
                        e = 2 * i + b
                        pe.wait_ge(M["s_w1"] if b else M["s_w0"], 16 * loads_each * (i + 1))
                        for s, (lo, hi) in enumerate(SPANS):
                            cols_ = (hi - lo) * TOK
                            u = e * (len(SPANS) * nf) + s * nf
                            for f in range(nf):
                                pe.wait_ge(M["s_act"], RING + u + f - 3)
                                for c in range(CT):
                                    at = c * width + f * 128
                                    last = nc.tensor.matmul(bank[f % 4][:, 0:cols_], w_up[b][:, at:at + 128],
                                                            XT[:, c, lo * TOK:hi * TOK],
                                                            start=(c == 0), stop=(c == CT - 1))
                                last.then_inc(M["s_up"], 1)
                            pe.wait_ge(M["s_act"], RING + u + nf)
                            for g in range(lo, hi):
                                t = e * GROUPS + g
                                pe.wait_ge(M["s_acc"], RING + t - (3 if g >= 3 else 2))
                                for f in range(nf):
                                    last = nc.tensor.matmul(bank[4 + g % 4][0:TOK, 0:E],
                                                            mid[:, f, (g - lo) * TOK:(g - lo + 1) * TOK],
                                                            w_dn[b][:, f * E:(f + 1) * E],
                                                            start=(f == 0), stop=(f == nf - 1))
                                last.then_inc(M["s_down"], 1)

            gates_transposed(m0)
            pe.wait_ge(m0["s_b_add"], GROUPS)
            pe.wait_ge(s_XT, GROUPS)
            experts(m0, F0, 3)
            pe.wait_ge(m0["s_acc"], RING + EXPERTS * GROUPS)

            def cos_block_1(n):
                pe.wait_ge(ln["s_xin"], n + 1)
                for c in range(CT):
                    last = nc.tensor.transpose(ln["b"][0][:, c * TOK:(c + 1) * TOK], ln["xin"][:, c * 128:(c + 1) * 128],
                                               ident[0:TOK, 0:TOK])
                last.then_inc(ln["s_xT_psum"], 1)

            def cos_block_2(n):
                pe.wait_ge(ln["s_xT"], n + 1)
                for i, w in enumerate("qkv"):
                    for c in range(CT):
                        last = nc.tensor.matmul(ln["b"][1 + i][0:TOK, 0:E], ln["xT"][:, c, :], mat(f"l_W{w}", c),
                                                start=(c == 0), stop=(c == CT - 1))
                last.then_inc(ln["s_qkv_psum"], 1)

            def cos_block_3(n):
                pe.wait_ge(ln["s_qn"], n + 1)
                for c in range(CT):
                    last = nc.tensor.transpose(ln["b"][0][:, c * TOK:(c + 1) * TOK], ln["q"][:, 0, c * 128:(c + 1) * 128],
                                               ident[0:TOK, 0:TOK])
                last.then_inc(ln["s_qT_psum"], 1)
                pe.wait_ge(ln["s_km"], n + 1)
                for c in range(CT):
                    for j in range(PER):
                        last = nc.tensor.matmul(ln["b"][1 + c][:, j * 128:(j + 1) * 128],
                                                ln["km"][:, j, c * 128:(c + 1) * 128],
                                                ln["q"][:, 2, c * 128:(c + 1) * 128], start=True, stop=True)
                last.then_inc(ln["s_kv_psum"], 1)

            def cos_block_4(n):
                pe.wait_ge(ln["s_qT"], n + 1)
                pe.wait_ge(ln["s_kv"], n + 1)
                for c in range(CT):
                    for j in range(PER):
                        at = c * TOK + j * SEQ
                        last = nc.tensor.matmul(ln["b"][3][:, at:at + SEQ], ln["kv"][:, c, j, :],
                                                ln["qT"][:, c, j * SEQ:(j + 1) * SEQ], start=True, stop=True)
                last.then_inc(ln["s_cT_psum"], 1)

            def cos_block_5(n):
                pe.wait_ge(ln["s_cT"], n + 1)
                for c in range(CT):
                    last = nc.tensor.matmul(ln["b"][0][0:TOK, 0:E], ln["cT"][:, c, :], mat("l_Wo", c),
                                            start=(c == 0), stop=(c == CT - 1))
                last.then_inc(ln["s_o_psum"], 1)

            cos_block_1(0)
            cos_block_2(0)
            cos_block_3(0)
            cos_block_4(0)
            cos_block_5(0)
            with pe.Fori(1, GROUPS) as n:
                transpose_in(a3, n - 1)
                cos_block_1(n)
                project(a3, n - 1, "g")
                cos_block_2(n)
                scores(a3, n - 1)
                cos_block_3(n)
                transpose_probs(a3, n - 1)
                cos_block_4(n)
                contexts(a3, n - 1)
                cos_block_5(n)
                transpose_ctx(a3, n - 1)
                output(a3, n - 1, "g")
                router(a3, n - 1, a3["s_in2"], a3["work2"], s_gT_psum, s_gT, gT, wr1, s_glog)
            n = GROUPS - 1
            transpose_in(a3, n)
            project(a3, n, "g")
            scores(a3, n)
            transpose_probs(a3, n)
            contexts(a3, n)
            transpose_ctx(a3, n)
            output(a3, n, "g")
            router(a3, n, a3["s_in2"], a3["work2"], s_gT_psum, s_gT, gT, wr1, s_glog)

            pe.wait_ge(m1["s_probs"], 1)
            flat = "p g e -> p (g e)"
            nc.tensor.matmul(bank[0][0:TOK, 0:GROUPS * EXPERTS], before[:, :], tmp8[1][:].rearrange(flat),
                             start=True, stop=False)
            nc.tensor.matmul(bank[0][0:TOK, 0:GROUPS * EXPERTS], ones[:, :], tmp8[2][:].rearrange(flat),
                             start=False, stop=True).then_inc(m1["s_rank_psum"], 1)
            pe.wait_ge(m1["s_gate"], 1)
            pe.wait_ge(s_GXT, GROUPS)
            experts(m1, F1, 2)

        @block.scalar
        def _(act):
            def copy_scaled(L, n, p=None):
                act.wait_ge(L["s_xT_psum"], L["at"] + n + 1)
                if p is None:
                    nc.scalar.activation(L["xT"][:].rearrange("p c t -> p (c t)"), L["b"][0][:, 0:CT * TOK], ACT.Copy)\
                        .then_inc(L["s_xT"], 1)
                    return
                for c in range(CT):
                    last = nc.scalar.activation(L["xT"][:, c, :], L["b"][0][:, c * TOK:(c + 1) * TOK], ACT.Identity,
                                                bias=col(p + "_b1", c), scale=col(p + "_g1", c))
                last.then_inc(L["s_xT"], 1)

            def queries_keys(L, n, bq, bk):
                act.wait_ge(L["s_qk_psum"], L["at"] + n + 1)
                for src, dst, bias, s in ((L["b"][1], L["qT"], bq, L["s_qT"]), (L["b"][2], L["kT"], bk, L["s_kT"])):
                    for c in range(CT):
                        last = nc.scalar.activation(dst[:, c, :], src[:, c * TOK:(c + 1) * TOK], ACT.Identity,
                                                    bias=col(bias, c))
                    last.then_inc(s, 1)

            def exps(L, n):
                act.wait_ge(L["s_shifted"], L["at"] + n + 1)
                nc.scalar.activation(L["pr"][:].rearrange("p (h k) -> p k h", h=HEADS),
                                     L["sc"][:].rearrange("p (k h) -> p k h", h=HEADS), ACT.Exp, scale=HD ** -0.5)\
                    .then_inc(L["s_exped"], 1)

            def probs_T(L, n):
                act.wait_ge(L["s_pT_psum"], L["at"] + n + 1)
                full = HPC * SEQ
                nc.scalar.activation(L["pT"][0:full, 0:3, :].rearrange("p t q -> p (t q)"), L["b"][0][0:full, 0:3 * TOK], ACT.Copy)
                nc.scalar.activation(L["pT"][0:full, 3:5, :].rearrange("p t q -> p (t q)"), L["b"][3][0:full, 0:2 * TOK], ACT.Copy)
                nc.scalar.activation(L["pT"][0:SEQ, 5, :], L["b"][3][0:SEQ, 2 * TOK:3 * TOK], ACT.Copy)\
                    .then_inc(L["s_pT"], 1)

            def ctx_out(L, n):
                act.wait_ge(L["s_c_psum"], L["at"] + n + 1)
                nc.scalar.activation(L["cx"][:, 0:2, :].rearrange("p j e -> p (j e)"), L["b"][1][0:SEQ, 0:2 * E], ACT.Copy)
                nc.scalar.activation(L["cx"][:, 2, :], L["b"][2][0:SEQ, 0:E], ACT.Copy).then_inc(L["s_cx"], 1)

            def ctx_T(L, n, bv):
                act.wait_ge(L["s_cT_psum"], L["at"] + n + 1)
                for c in range(CT):
                    last = nc.scalar.activation(L["cT"][:, c, :], L["b"][0][:, c * TOK:(c + 1) * TOK], ACT.Identity,
                                                bias=col(bv, c))
                last.then_inc(L["s_cT"], 1)

            def distances(n):
                for i in range(2):
                    for part in range(3):
                        u = 3 * i + part
                        lo, hi = REL_CUTS[part], REL_CUTS[part + 1]
                        act.wait_ge(s_qe_psum, 6 * n + u + 1)
                        nc.scalar.activation(qe[:, i, lo * HEADS:hi * HEADS],
                                             a1["b"][0 if u % 2 == 0 else 3][0:TOK, 0:(hi - lo) * HEADS], ACT.Copy)\
                            .then_inc(s_qe, 1)

            def normed_T(n, first=False):
                act.wait_ge(s_nT_psum, n + 1)
                for c in range(CT):
                    last = nc.scalar.activation(nT[:, c, :], a2["b"][0][:, c * TOK:(c + 1) * TOK], ACT.Identity,
                                                bias=col("f_b2", c), scale=col("f_g2", c))
                last.then_inc(s_nT, 1)

            act.wait_ge(s_const, 16 * N_LOADS)
            copy_scaled(a1, 0)
            queries_keys(a1, 0, "a_bq", "a_bk")
            distances(0)
            exps(a1, 0)
            probs_T(a1, 0)
            ctx_out(a1, 0)
            ctx_T(a1, 0, "a_bv")
            with act.Fori(1, GROUPS) as n:
                m = n - 1
                copy_scaled(a2, m, "f")
                copy_scaled(a1, n)
                queries_keys(a2, m, "f_bq", "f_bk")
                queries_keys(a1, n, "a_bq", "a_bk")
                distances(n)
                exps(a2, m)
                probs_T(a2, m)
                ctx_out(a2, m)
                exps(a1, n)
                ctx_T(a2, m, "f_bv")
                probs_T(a1, n)
                ctx_out(a1, n)
                normed_T(m)
                ctx_T(a1, n, "a_bv")
            m = GROUPS - 1
            copy_scaled(a2, m, "f")
            queries_keys(a2, m, "f_bq", "f_bk")
            exps(a2, m)
            probs_T(a2, m)
            ctx_out(a2, m)
            ctx_T(a2, m, "f_bv")
            normed_T(m)

            act.wait_ge(m0["s_probs"], 1)
            nc.scalar.activation(tmp8[1][:], tmp8[0][:], ACT.Exp).then_inc(m0["s_exp"], 1)
            act.wait_ge(m0["s_gT_psum"], 1)
            for b in range(3):
                hi = min(4 * (b + 1), GROUPS)
                last = nc.scalar.activation(gateT[:, 4 * b:hi, :].rearrange("p g t -> p (g t)"),
                                            bank[b][0:EXPERTS, 0:(hi - 4 * b) * TOK], ACT.Copy)
            last.then_inc(m0["s_gT"], 1)

            def gelus(M, width, bias):
                nf = width // 128
                act.sem_inc(M["s_act"], RING)
                with act.Fori(0, EXPERTS // 2) as i:
                    for b in range(2):
                        e = 2 * i + b
                        for s, (lo, hi) in enumerate(SPANS):
                            u = e * (len(SPANS) * nf) + s * nf
                            for f in range(nf):
                                act.wait_ge(M["s_up"], u + f + 1)
                                kw = dict(bias=b_up[b][:, f:f + 1]) if bias else {}
                                nc.scalar.activation(mid[:, f, 0:(hi - lo) * TOK],
                                                     bank[f % 4][:, 0:(hi - lo) * TOK], ACT.Gelu, **kw)\
                                    .then_inc(M["s_act"], 1)

            gelus(m0, F0, True)

            nc.scalar.activation(inv_scale[:, 0, :], cols[:, COLS.index("l_m"), :], ACT.Sigmoid)\
                .then_inc(s_scale, 1)
            act.wait_ge(s_scale, 1)
            nc.scalar.activation(inv_scale[:, 1, :], inv_scale[:, 0, :], ACT.Exp, scale=-float(np.log(SEQ)))\
                .then_inc(s_scale2, 1)

            def cos_1(n):
                act.wait_ge(ln["s_xT_psum"], n + 1)
                nc.scalar.activation(ln["xT"][:].rearrange("p c t -> p (c t)"), ln["b"][0][:, 0:CT * TOK], ACT.Copy)\
                    .then_inc(ln["s_xT"], 1)

            def cos_2(n):
                act.wait_ge(ln["s_norm2"], n + 1)
                nc.scalar.activation(ln["ri"][:], ln["ss"][:], ACT.Ln).then_inc(ln["s_act"], 1)
                act.wait_ge(ln["s_act"], n + 1)
                nc.scalar.activation(ln["ss"][:], ln["ri"][:], ACT.Exp, scale=0.5).then_inc(ln["s_norm"], 1)

            def cos_3(n):
                act.wait_ge(ln["s_qT_psum"], n + 1)
                nc.scalar.activation(ln["qT"][:].rearrange("p c t -> p (c t)"), ln["b"][0][:, 0:CT * TOK], ACT.Copy)\
                    .then_inc(ln["s_qT"], 1)

            def cos_4(n):
                act.wait_ge(ln["s_cT_psum"], n + 1)
                nc.scalar.activation(ln["cT"][:].rearrange("p c t -> p (c t)"), ln["b"][3][:, 0:CT * TOK], ACT.Copy)\
                    .then_inc(ln["s_cT"], 1)

            def src_T(n):
                act.wait_ge(s_gT_psum, n + 1)
                nc.scalar.activation(gT[:].rearrange("p c t -> p (c t)"), a3["b"][0][:, 0:CT * TOK], ACT.Copy)\
                    .then_inc(s_gT, 1)

            for st in (cos_1, cos_2, cos_3, cos_4):
                st(0)
            with act.Fori(1, GROUPS) as n:
                m = n - 1
                copy_scaled(a3, m)
                cos_1(n)
                queries_keys(a3, m, "g_qb", "g_kb")
                cos_2(n)
                exps(a3, m)
                cos_3(n)
                probs_T(a3, m)
                cos_4(n)
                ctx_out(a3, m)
                ctx_T(a3, m, "g_vb")
                src_T(m)
            m = GROUPS - 1
            copy_scaled(a3, m)
            queries_keys(a3, m, "g_qb", "g_kb")
            exps(a3, m)
            probs_T(a3, m)
            ctx_out(a3, m)
            ctx_T(a3, m, "g_vb")
            src_T(m)
            act.wait_ge(s_glg, GROUPS)
            nc.scalar.activation(tmp8[0][:], LOGITS[:], ACT.Sigmoid).then_inc(m1["s_exp"], 1)
            gelus(m1, F1, False)

        @block.vector
        def _(dve):
            link_no = {}

            def link(L, n, ins):
                k = link_no[L["tag"]] = link_no.get(L["tag"], 0) + 1
                ins.then_inc(L["s_dve"], 1)
                dve.wait_ge(L["s_dve"], L["dve_at"] + n * DVE_LINKS[L["tag"]] + k)

            def end_links(L):
                assert link_no[L["tag"]] == DVE_LINKS[L["tag"]], (L["tag"], link_no[L["tag"]])
                link_no[L["tag"]] = 0

            def normed(out, x, mean, rstd):
                return nc.vector.tensor_scalar(out, x, mean, rstd, ALU.subtract, ALU.mult)

            def rel_pre(n, first=False):
                dve.wait_ge(s_tok, n + 1)
                link(a1, n, nc.vector.tensor_tensor(a1["hold"][:], bank[1][0:TOK, 0:E], base[:], ALU.add))
                link(a1, n, nc.vector.bn_stats(a1["st"][:], a1["hold"][:]))
                carry_dve()
                nc.vector.bn_aggr(a1["mv"][:], a1["st"][:]).then_inc(a1["s_stat"], 1)
                dve.wait_ge(a1["s_rstd"], n + 1)
                normed(a1["xin"][:], a1["hold"][:], a1["mv"][:, 0:1], a1["rs"][:, 0:1]).then_inc(a1["s_xin"], 1)

            def causal_pre(n, first=False):
                dve.wait_ge(a1["s_done"], n + 1)
                link(a2, n, nc.vector.bn_stats(a2["st"][:], of_group(H, n)))
                carry_dve()
                nc.vector.bn_aggr(a2["mv"][:], a2["st"][:]).then_inc(a2["s_stat"], 1)
                dve.wait_ge(a2["s_rstd"], n + 1)
                normed(a2["xin"][:], of_group(H, n), a2["mv"][:, 0:1], a2["rs"][:, 1:2])
                normed(a2["res"][:], of_group(H, n), a2["mv"][:, 0:1], a2["rs"][:, 0:1]).then_inc(a2["s_xin"], 1)

            def keys(L, n):
                dve.wait_ge(L["s_kT"], L["at"] + n + 1)
                k = L["kT"][:].rearrange("p c t -> p (c t)")
                nc.vector.tensor_tensor(
                    L["kB"][:].rearrange("p c t h -> p (c t) h"), k[:, :, None].to_broadcast([128, CT * TOK, HC]),
                    head_of_row[:, None, :].to_broadcast([128, CT * TOK, HC]), ALU.mult).then_inc(L["s_kB"], 1)

            def values(L, n):
                dve.wait_ge(L["s_v_psum"], L["at"] + n + 1)
                for lo, hi, src in ((0, 2, L["b"][0]), (2, 3, L["b"][3])):
                    w = (hi - lo)
                    v = src[0:TOK, 0:w * E].rearrange("p (j h d) -> p j h d", j=w, h=HEADS)
                    m_ = third_of_head[:, None, :, None].to_broadcast([TOK, w, HEADS, HD])
                    last = nc.vector.tensor_tensor(L["vB"][:, lo:hi, :].rearrange("p j (h d) -> p j h d", h=HEADS),
                                                   v, m_, ALU.mult)
                last.then_inc(L["s_vB"], 1)

            def shift(L, n, extra):
                dve.wait_ge(L["s_s_psum"], L["at"] + n + 1)
                for b, (lo, hi) in enumerate(((0, K0), (K0, SEQ))):
                    s = L["b"][1 + b][0:TOK, 0:(hi - lo) * HEADS].rearrange("p (k h) -> p k h", h=HEADS)
                    o = L["sc"][:, lo * HEADS:hi * HEADS].rearrange("p (k h) -> p k h", h=HEADS)
                    if extra == "rel":
                        ins = nc.vector.tensor_tensor(o, s, relb[:, 0, lo * HEADS:hi * HEADS]
                                                      .rearrange("p (k h) -> p k h", h=HEADS), ALU.add)
                    elif extra == "causal":
                        ins = nc.vector.tensor_tensor(o, s, causal[:, lo:hi, None].to_broadcast(
                            [TOK, hi - lo, HEADS]), ALU.add)
                    else:
                        ins = nc.vector.tensor_copy(o, s)
                link(L, n, ins)
                link(L, n, nc.vector.tensor_reduce(L["mx"][:], L["sc"][:].rearrange("p (k h) -> p h k", h=HEADS),
                                                   AX.X, ALU.max))
                s = L["sc"][:].rearrange("p (k h) -> p k h", h=HEADS)
                nc.vector.tensor_tensor(s, s, L["mx"][:, None, :].to_broadcast([TOK, SEQ, HEADS]), ALU.subtract)\
                    .then_inc(L["s_shifted"], 1)

            def normalise(L, n):
                dve.wait_ge(L["s_exped"], L["at"] + n + 1)
                p = L["pr"][:].rearrange("p (h k) -> p h k", h=HEADS)
                link(L, n, nc.vector.tensor_reduce(L["sm"][:], p, AX.X, ALU.add))
                link(L, n, nc.vector.reciprocal(L["sm"][:], L["sm"][:]))
                nc.vector.tensor_tensor(p, p, L["sm"][:, :, None].to_broadcast([TOK, HEADS, SEQ]), ALU.mult)\
                    .then_inc(L["s_probs"], 1)

            def rel_post(n):
                dve.wait_ge(a1["s_o_psum"], n + 1)
                dve.wait_ge(a1["s_bias_in"], n + 1)
                link(a1, n, nc.vector.tensor_tensor(a1["work"][:], a1["b"][3][0:TOK, 0:E], a1["res"][:], ALU.add))
                link(a1, n, nc.vector.bn_stats(a1["st2"][:], a1["work"][:]))
                carry_dve()
                nc.vector.bn_aggr(a1["mv2"][:], a1["st2"][:]).then_inc(a1["s_stat2"], 1)
                dve.wait_ge(a1["s_rstd2"], n + 1)
                link(a1, n, normed(a1["work2"][:], a1["work"][:], a1["mv2"][:, 0:1], a1["rs2"][:, 0:1]))
                link(a1, n, nc.vector.tensor_tensor(a1["work2"][:], a1["work2"][:], row("a_g"), ALU.mult))
                nc.vector.tensor_tensor(of_group(H, n), a1["work2"][:], a1["hold"][:], ALU.add).then_inc(a1["s_done"], 1)
                end_links(a1)

            def causal_post(n):
                dve.wait_ge(a2["s_o_psum"], n + 1)
                dve.wait_ge(a2["s_bias_in"], n + 1)
                link(a2, n, nc.vector.tensor_tensor(a2["work"][:], a2["b"][3][0:TOK, 0:E], a2["hold"][:], ALU.add))

            def gqa_pre(n, first=False):
                dve.wait_ge(ln["s_done"], n + 1)
                link(a3, n, nc.vector.bn_stats(a3["st"][:], of_group(H, n)))
                carry_dve()
                nc.vector.bn_aggr(a3["mv"][:], a3["st"][:]).then_inc(a3["s_stat"], 1)
                dve.wait_ge(a3["s_rstd"], a3["at"] + n + 1)
                normed(a3["xin"][:], of_group(H, n), a3["mv"][:, 0:1], a3["rs"][:, 0:1]).then_inc(a3["s_xin"], 1)

            def logits_in(n, s_in, s_done_, src, bias):
                dve.wait_ge(s_in, n + 1)
                dst = LOGITS[:].rearrange("p g e -> p (g e)")[:, bass.ds(n * EXPERTS, EXPERTS)]
                if bias:
                    nc.vector.tensor_tensor(dst, src[0:TOK, 0:EXPERTS], br0[:], ALU.add).then_inc(s_done_, 1)
                else:
                    nc.vector.tensor_copy(dst, src[0:TOK, 0:EXPERTS]).then_inc(s_done_, 1)

            def causal_norm(n):
                link(a2, n, nc.vector.bn_stats(a2["st2"][:], a2["work"][:]))
                carry_dve()
                nc.vector.bn_aggr(a2["mv2"][:], a2["st2"][:]).then_inc(a2["s_stat2"], 1)
                nc.vector.tensor_tensor(of_group(H, n), of_group(H, n), a2["work"][:], ALU.add).then_inc(a2["s_done"], 1)
                dve.wait_ge(a2["s_rstd2"], n + 1)
                normed(a2["work2"][:], a2["work"][:], a2["mv2"][:, 0:1], a2["rs2"][:, 0:1]).then_inc(a2["s_in2"], 1)
                end_links(a2)

            def gqa_post(n):
                dve.wait_ge(a3["s_o_psum"], a3["at"] + n + 1)
                dve.wait_ge(a3["s_bias_in"], a3["at"] + n + 1)
                link(a3, n, nc.vector.tensor_tensor(a3["work"][:], a3["b"][3][0:TOK, 0:E], a3["hold"][:], ALU.add))
                link(a3, n, nc.vector.bn_stats(a3["st2"][:], a3["work"][:]))
                carry_dve()
                link(a3, n, nc.vector.bn_aggr(a3["mv2"][:], a3["st2"][:]))
                nc.vector.scalar_tensor_tensor(a3["va2"][:], a3["mv2"][:, 0:1], a3["mv2"][:, 0:1], a3["mv2"][:, 1:2],
                                               ALU.mult, ALU.add).then_inc(a3["s_stat2"], 1)
                dve.wait_ge(a3["s_rstd2"], a3["at"] + n + 1)
                nc.vector.scalar_tensor_tensor(a3["work2"][:], a3["work"][:], a3["rs2"][:, 0:1], row("g_n1"),
                                               ALU.mult, ALU.mult).then_inc(a3["s_in2"], 1)
                dve.wait_ge(a3["s_in2"], a3["at"] + n + 1)
                nc.vector.tensor_copy(of_group(SRC, n), a3["work2"][:]).then_inc(a3["s_done"], 1)
                end_links(a3)

            dve.wait_ge(s_const, 16 * N_LOADS)
            rel_pre(0, True)
            keys(a1, 0)
            values(a1, 0)
            dve.wait_ge(s_relsum, 1)
            shift(a1, 0, "rel")
            normalise(a1, 0)
            rel_post(0)
            with dve.Fori(1, GROUPS) as n:
                m = n - 1
                rel_pre(n)
                causal_pre(m)
                keys(a2, m)
                values(a2, m)
                keys(a1, n)
                values(a1, n)
                shift(a2, m, "causal")
                normalise(a2, m)
                dve.wait_ge(s_relsum, n + 1)
                shift(a1, n, "rel")
                normalise(a1, n)
                causal_post(m)
                causal_norm(m)
                logits_in(m, s_log, s_lg, a2["b"][1], True)
                rel_post(n)
            m = GROUPS - 1
            causal_pre(m)
            keys(a2, m)
            values(a2, m)
            shift(a2, m, "causal")
            normalise(a2, m)
            causal_post(m)
            causal_norm(m)
            logits_in(m, s_log, s_lg, a2["b"][1], True)

            moe_links = {"moe0": 0, "moe1": 0}

            def mlink(M, ins):
                moe_links[M["tag"]] += 1
                ins.then_inc(M["s_dve"], 1)
                dve.wait_ge(M["s_dve"], moe_links[M["tag"]])

            def wide1(x):
                return x[:, :, None].to_broadcast([TOK, GROUPS, EXPERTS])

            dve.wait_ge(s_lg, GROUPS)
            for g in range(GROUPS):
                last = nc.vector.max(top8[:, g, :], LOGITS[:, g, :])
            mlink(m0, last)
            nc.vector.tensor_tensor(tmp8[0][:], LOGITS[:], top8[:, :, 0:1].to_broadcast([TOK, GROUPS, EXPERTS]),
                                    ALU.subtract).then_inc(m0["s_probs"], 1)
            mlink(m0, nc.vector.tensor_tensor(tmp8[2][:], LOGITS[:],
                                              top8[:, :, 1:2].to_broadcast([TOK, GROUPS, EXPERTS]), ALU.is_ge))
            dve.wait_ge(m0["s_exp"], 1)
            mlink(m0, nc.vector.tensor_tensor(tmp8[3][:], tmp8[1][:], tmp8[2][:], ALU.mult))
            mlink(m0, nc.vector.tensor_reduce(tmp1[0][:], tmp8[3][:], AX.X, ALU.add))
            mlink(m0, nc.vector.reciprocal(tmp1[0][:], tmp1[0][:]))
            mlink(m0, nc.vector.tensor_tensor(GATE[:], tmp8[3][:], wide1(tmp1[0]), ALU.mult))
            nc.vector.tensor_copy(GATE_E[:].rearrange("p (e g) -> p g e", e=EXPERTS), GATE[:])\
                .then_inc(m0["s_gate"], 1)
            for g in range(GROUPS):
                dve.wait_ge(m0["s_b_psum"], g + 1)
                nc.vector.tensor_tensor(H[:, g * E:(g + 1) * E], H[:, g * E:(g + 1) * E],
                                        bank[4 + g % 4][0:TOK, 0:E], ALU.add).then_inc(m0["s_b_add"], 1)

            def accumulate(M, acc):
                dve.wait_ge(M["s_gate"], 1)
                dve.sem_inc(M["s_acc"], RING)
                with dve.Fori(0, EXPERTS // 2) as i:
                    for b in range(2):
                        e = 2 * i + b
                        for g in range(GROUPS):
                            dve.wait_ge(M["s_down"], e * GROUPS + g + 1)
                            if g == 0:
                                dve.wait_ge(M["s_acc"], RING + e * GROUPS)
                            a = acc[:, g * E:(g + 1) * E]
                            ins = nc.vector.scalar_tensor_tensor(a, bank[4 + g % 4][0:TOK, 0:E],
                                                                 GATE_E[:, bass.ds(e * GROUPS + g, 1)], a,
                                                                 ALU.mult, ALU.add)
                            ins.then_inc(M["s_acc"], 1)
                dve.wait_ge(M["s_acc"], RING + EXPERTS * GROUPS)

            dve.wait_ge(m0["s_b_add"], GROUPS)
            accumulate(m0, H)

            def cos_pre(n, first=False):
                if not first:
                    dve.wait_ge(ln["s_done"], n)
                nc.vector.bn_stats(ln["st"][:], of_group(H, n)).then_inc(ln["s_dve"], 1)
                dve.wait_ge(ln["s_dve"], n * LN_LINKS + 1)
                carry_dve()
                nc.vector.bn_aggr(ln["mv"][:], ln["st"][:]).then_inc(ln["s_stat"], 1)
                dve.wait_ge(ln["s_rstd"], n + 1)
                normed(ln["xin"][:], of_group(H, n), ln["mv"][:, 0:1], ln["rs"][:, 0:1]).then_inc(ln["s_xin"], 1)

            def cos_qkv(n):
                dve.wait_ge(ln["s_qkv_psum"], n + 1)
                for i, b in enumerate(("l_bq", "l_bk", "l_bv")):
                    last = nc.vector.tensor_tensor(ln["q"][:, i, :], ln["b"][1 + i][0:TOK, 0:E], row(b), ALU.add)
                last.then_inc(ln["s_qkv"], 1)
                dve.wait_ge(ln["s_squares"], n + 1)
                nc.vector.tensor_reduce(ln["ss"][:], ln["sq"][:].rearrange("p i (h d) -> p i h d", h=HEADS), AX.X, ALU.add)\
                    .then_inc(ln["s_norm2"], 1)

            def cos_norm(n):
                dve.wait_ge(ln["s_norm"], n + 1)
                nc.vector.tensor_scalar(ln["ri"][:], ln["ss"][:], EPS_A, None, ALU.max).then_inc(ln["s_dve"], 1)
                dve.wait_ge(ln["s_dve"], n * LN_LINKS + 2)
                nc.vector.reciprocal(ln["ri"][:], ln["ri"][:]).then_inc(ln["s_dve"], 1)
                dve.wait_ge(ln["s_dve"], n * LN_LINKS + 3)
                qk = ln["q"][:, 0:2, :].rearrange("p i (h d) -> p i h d", h=HEADS)
                nc.vector.tensor_tensor(qk, qk, ln["ri"][:, :, :, None].to_broadcast([TOK, 2, HEADS, HD]), ALU.mult)\
                    .then_inc(ln["s_qn"], 1)
                dve.wait_ge(ln["s_qn"], n + 1)
                nc.vector.tensor_tensor(ln["km"][:], ln["q"][:, 1:2, :].to_broadcast([TOK, PER, E]),
                                        of_image[:, :, None].to_broadcast([TOK, PER, E]), ALU.mult)\
                    .then_inc(ln["s_km"], 1)

            def cos_kv(n):
                dve.wait_ge(ln["s_kv_psum"], n + 1)
                for c in range(CT):
                    last = nc.vector.scalar_tensor_tensor(
                        ln["kv"][:, c, :, :], ln["b"][1 + c][:, 0:PER * 128].rearrange("p (j d) -> p j d", j=PER),
                        inv_scale[:, 1, c:c + 1], same_head[:, None, :].to_broadcast([128, PER, 128]),
                        ALU.mult, ALU.mult)
                last.then_inc(ln["s_kv"], 1)

            def cos_post(n):
                dve.wait_ge(ln["s_o_psum"], n + 1)
                dve.wait_ge(ln["s_bias_in"], n + 1)
                nc.vector.tensor_tensor(of_group(H, n), ln["b"][0][0:TOK, 0:E], ln["hold"][:], ALU.add).then_inc(ln["s_done"], 1)

            dve.wait_ge(s_scale2, 1)
            cos_pre(0, True)
            cos_qkv(0)
            cos_norm(0)
            cos_kv(0)
            cos_post(0)

            with dve.Fori(1, GROUPS) as n:
                m = n - 1
                gqa_pre(m)
                cos_pre(n)
                keys(a3, m)
                cos_qkv(n)
                values(a3, m)
                cos_norm(n)
                shift(a3, m, "none")
                cos_kv(n)
                normalise(a3, m)
                cos_post(n)
                gqa_post(m)
                logits_in(m, s_glog, s_glg, a3["b"][1], False)
            m = GROUPS - 1
            gqa_pre(m)
            keys(a3, m)
            values(a3, m)
            shift(a3, m, "none")
            normalise(a3, m)
            gqa_post(m)
            logits_in(m, s_glog, s_glg, a3["b"][1], False)

            p, left, first, eq, chosen, score = tmp8[0], tmp8[3], tmp8[4], tmp8[5], tmp8[1], tmp8[2]
            dve.wait_ge(m1["s_exp"], 1)
            rev = rev8[:, None, :].to_broadcast([TOK, GROUPS, EXPERTS])

            def pick(src, out):
                mlink(m1, nc.vector.tensor_reduce(tmp1[0][:], src[:], AX.X, ALU.max))
                mlink(m1, nc.vector.tensor_tensor(eq[:], src[:], wide1(tmp1[0]), ALU.is_ge))
                mlink(m1, nc.vector.tensor_tensor(score[:], eq[:], rev, ALU.mult))
                mlink(m1, nc.vector.tensor_reduce(tmp1[1][:], score[:], AX.X, ALU.max))
                mlink(m1, nc.vector.tensor_tensor(out[:], score[:], wide1(tmp1[1]), ALU.is_equal))

            pick(p, first)
            mlink(m1, nc.vector.scalar_tensor_tensor(left[:], first[:], -2.0, p[:], ALU.mult, ALU.add))
            pick(left, chosen)
            mlink(m1, nc.vector.tensor_tensor(chosen[:], chosen[:], first[:], ALU.add))
            mlink(m1, nc.vector.memset(tmp8[2][:, 0, :], 0.0))
            for g in range(1, GROUPS):
                mlink(m1, nc.vector.tensor_tensor(tmp8[2][:, g, :], tmp8[2][:, g - 1, :], chosen[:, g - 1, :], ALU.add))
            mlink(m1, nc.vector.tensor_tensor(left[:], p[:], chosen[:], ALU.mult))
            mlink(m1, nc.vector.tensor_reduce(tmp1[0][:], left[:], AX.X, ALU.add))
            mlink(m1, nc.vector.tensor_scalar(tmp1[0][:], tmp1[0][:], EPS_R, None, ALU.add))
            nc.vector.reciprocal(tmp1[1][:], tmp1[0][:]).then_inc(m1["s_probs"], 1)
            dve.wait_ge(m1["s_probs"], 1)
            mlink(m1, nc.vector.tensor_tensor(left[:], left[:], wide1(tmp1[1]), ALU.mult))
            dve.wait_ge(m1["s_rank_psum"], 1)
            mlink(m1, nc.vector.tensor_scalar(eq[:].rearrange("p g e -> p (g e)"), bank[0][0:TOK, 0:GROUPS * EXPERTS],
                                              float(CAPACITY), None, ALU.is_lt))
            nc.vector.tensor_tensor(GATE_E[:].rearrange("p (e g) -> p g e", e=EXPERTS), left[:], eq[:], ALU.mult)\
                .then_inc(m1["s_gate"], 1)
            accumulate(m1, SRC)

            for g in range(GROUPS):
                last = nc.vector.bn_stats(fin["st"][:, g, :], SRC[:, g * E:(g + 1) * E])
            last.then_inc(s_fin_dve, 1)
            dve.wait_ge(s_fin_dve, 1)
            for g in range(GROUPS):
                last = nc.vector.bn_aggr(fin["mv"][:, g, :], fin["st"][:, g, :])
            last.then_inc(s_fin_dve, 1)
            dve.wait_ge(s_fin_dve, 2)
            nc.vector.tensor_tensor(fin["va"][:], fin["mv"][:, :, 0], fin["mv"][:, :, 0], ALU.mult).then_inc(s_fin_dve, 1)
            dve.wait_ge(s_fin_dve, 3)
            nc.vector.tensor_tensor(fin["va"][:], fin["va"][:], fin["mv"][:, :, 1], ALU.add).then_inc(s_fin_stat, 1)
            dve.wait_ge(s_fin_rstd, 1)
            for g in range(GROUPS):
                s = SRC[:, g * E:(g + 1) * E]
                nc.vector.scalar_tensor_tensor(s, s, fin["rs"][:, g:g + 1], row("g_n2"), ALU.mult, ALU.mult)\
                    .then_inc(s_fin_dve, 1)
            for g in range(GROUPS):
                h = H[:, g * E:(g + 1) * E]
                dve.wait_ge(s_fin_dve, 4 + g)
                nc.vector.tensor_tensor(h, h, SRC[:, g * E:(g + 1) * E], ALU.add).then_inc(s_fin, 1)

        @block.gpsimd
        def _(pool):
            link_no = {}

            def link(L, n, ins):
                k = link_no[L["tag"]] = link_no.get(L["tag"], 0) + 1
                ins.then_inc(L["s_pool"], 1)
                pool.wait_ge(L["s_pool"], L["pool_at"] + n * POOL_LINKS[L["tag"]] + k)

            def end_links(L):
                assert link_no[L["tag"]] == POOL_LINKS[L["tag"]], (L["tag"], link_no[L["tag"]])
                link_no[L["tag"]] = 0

            def pow_half(out, x):
                return nc.gpsimd.tensor_tensor(out, x, half[:, 0:1], ALU.pow)

            def rel_rstd(n):
                pool.wait_ge(a1["s_stat"], n + 1)
                link(a1, n, nc.gpsimd.tensor_tensor(a1["va"][:, 0:1], a1["mv"][:, 1:2], eps[:, 0:1], ALU.add))
                pow_half(a1["rs"][:, 0:1], a1["va"][:, 0:1]).then_inc(a1["s_rstd"], 1)
                pool.wait_ge(a1["s_xin"], n + 1)
                nc.gpsimd.tensor_tensor(a1["res"][:], a1["xin"][:], row("a_bo"), ALU.add)
                nc.gpsimd.tensor_tensor(a1["hold"][:], a1["hold"][:], row("a_b"), ALU.add).then_inc(a1["s_bias_in"], 1)

            def triple(L, n):
                pool.wait_ge(L["s_xT"], L["at"] + n + 1)
                carry_pool()
                nc.gpsimd.tensor_copy(
                    L["x3"].rearrange("p c j (r k) -> p (c j) r k", r=HPC),
                    L["xT"][:].rearrange("p c (j k) -> p (c j) k", j=PER)[:, :, None, :]
                    .to_broadcast([128, CT * PER, HPC, SEQ])).then_inc(L["s_x3"], 1)

            def spread_queries(L, n):
                pool.wait_ge(L["s_qT"], L["at"] + n + 1)
                carry_pool()
                for j in range(PER):
                    last = nc.gpsimd.tensor_copy(L["qM"][:, :, j, j * SEQ:(j + 1) * SEQ],
                                                 L["qT"][:, :, j * SEQ:(j + 1) * SEQ])
                last.then_inc(L["s_qM"], 1)

            def rel_sum(n):
                pool.wait_ge(s_rel_in, 96 * (n + 1))
                nc.gpsimd.tensor_tensor(relb[:, 0, :], relb[:, 0, :], relb[:, 1, :], ALU.add).then_inc(s_relsum, 1)

            def rel_rstd2(n):
                pool.wait_ge(a1["s_stat2"], n + 1)
                link(a1, n, nc.gpsimd.tensor_tensor(a1["va2"][:], a1["mv2"][:, 1:2], eps[:, 1:2], ALU.add))
                pow_half(a1["rs2"][:], a1["va2"][:]).then_inc(a1["s_rstd2"], 1)

            def causal_rstd(n):
                pool.wait_ge(a2["s_stat"], n + 1)
                nc.gpsimd.tensor_tensor(a2["va"][:, 0:1], a2["mv"][:, 1:2], eps[:, 0:1], ALU.add)
                link(a2, n, nc.gpsimd.tensor_scalar(a2["va"][:, 1:2], a2["mv"][:, 1:2], 1.0 + EPS, EPS * EPS,
                                                    ALU.mult, ALU.add))
                nc.gpsimd.tensor_tensor(a2["rs"][:], a2["va"][:], half[:, 0:1].to_broadcast([TOK, 2]), ALU.pow)\
                    .then_inc(a2["s_rstd"], 1)
                pool.wait_ge(a2["s_xin"], n + 1)
                nc.gpsimd.tensor_tensor(a2["hold"][:], a2["res"][:], row("f_bo"), ALU.add).then_inc(a2["s_bias_in"], 1)

            def causal_rstd2(n):
                pool.wait_ge(a2["s_stat2"], n + 1)
                link(a2, n, nc.gpsimd.tensor_tensor(a2["va2"][:], a2["mv2"][:, 1:2], eps[:, 0:1], ALU.add))
                pow_half(a2["rs2"][:], a2["va2"][:]).then_inc(a2["s_rstd2"], 1)

            def keep_T(n, s_in, src, s_done_):
                pool.wait_ge(s_in, n + 1)
                carry_pool()
                nc.gpsimd.tensor_copy(XT[:, :, bass.ds(n * TOK, TOK)], src[:]).then_inc(s_done_, 1)

            nc.gpsimd.memset(half[:], -0.5)
            for i, value in enumerate((EPS, EPS_A, EPS_R)):
                nc.gpsimd.memset(eps[:, i:i + 1], value)
            nc.gpsimd.memset(ones[:], 1.0)
            nc.gpsimd.memset(a2["qM"][:], 0.0)
            nc.gpsimd.memset(a1["qM"][:], 0.0).then_inc(s_zeroed, 1)
            pool.wait_ge(s_zeroed, 1)
            pool.wait_ge(s_const, 16 * N_LOADS)
            rel_rstd(0)
            triple(a1, 0)
            spread_queries(a1, 0)
            rel_sum(0)
            rel_rstd2(0)
            end_links(a1)
            with pool.Fori(1, GROUPS) as n:
                m = n - 1
                rel_rstd(n)
                causal_rstd(m)
                triple(a2, m)
                spread_queries(a2, m)
                triple(a1, n)
                spread_queries(a1, n)
                rel_sum(n)
                causal_rstd2(m)
                keep_T(m, s_nT, nT, s_XT)
                rel_rstd2(n)
                end_links(a1)
                end_links(a2)
            m = GROUPS - 1
            causal_rstd(m)
            triple(a2, m)
            spread_queries(a2, m)
            causal_rstd2(m)
            keep_T(m, s_nT, nT, s_XT)

            def cos_rstd(n):
                pool.wait_ge(ln["s_stat"], n + 1)
                nc.gpsimd.tensor_tensor(ln["va"][:], ln["mv"][:, 1:2], eps[:, 0:1], ALU.add).then_inc(ln["s_pool"], 1)
                pool.wait_ge(ln["s_pool"], n + 1)
                pow_half(ln["rs"][:], ln["va"][:]).then_inc(ln["s_rstd"], 1)
                nc.gpsimd.tensor_tensor(ln["hold"][:], of_group(H, n), row("l_bo"), ALU.add).then_inc(ln["s_bias_in"], 1)

            def cos_squares(n):
                pool.wait_ge(ln["s_qkv"], n + 1)
                nc.gpsimd.tensor_tensor(ln["sq"][:], ln["q"][:, 0:2, :], ln["q"][:, 0:2, :], ALU.mult).then_inc(ln["s_squares"], 1)

            def gqa_rstd(n):
                pool.wait_ge(a3["s_stat"], a3["at"] + n + 1)
                link(a3, n, nc.gpsimd.tensor_tensor(a3["va"][:, 0:1], a3["mv"][:, 1:2], eps[:, 0:1], ALU.add))
                pow_half(a3["rs"][:, 0:1], a3["va"][:, 0:1]).then_inc(a3["s_rstd"], 1)
                pool.wait_ge(a3["s_xin"], a3["at"] + n + 1)
                nc.gpsimd.tensor_tensor(a3["hold"][:], a3["xin"][:], row("g_ob"), ALU.add).then_inc(a3["s_bias_in"], 1)

            def gqa_rstd2(n):
                pool.wait_ge(a3["s_stat2"], a3["at"] + n + 1)
                link(a3, n, nc.gpsimd.tensor_tensor(a3["rs"][:, 1:2], a3["va2"][:], eps[:, 2:3], ALU.add))
                pow_half(a3["rs2"][:], a3["rs"][:, 1:2]).then_inc(a3["s_rstd2"], 1)

            cos_rstd(0)
            cos_squares(0)
            with pool.Fori(1, GROUPS) as n:
                m = n - 1
                gqa_rstd(m)
                cos_rstd(n)
                triple(a3, m)
                spread_queries(a3, m)
                cos_squares(n)
                gqa_rstd2(m)
                keep_T(m, s_gT, gT, s_GXT)
                end_links(a3)
            m = GROUPS - 1
            gqa_rstd(m)
            triple(a3, m)
            spread_queries(a3, m)
            gqa_rstd2(m)
            keep_T(m, s_gT, gT, s_GXT)
            pool.wait_ge(s_fin_stat, 1)
            nc.gpsimd.tensor_scalar(fin["va"][:], fin["va"][:], EPS_R, None, ALU.add).then_inc(s_fin_pool, 1)
            pool.wait_ge(s_fin_pool, 1)
            nc.gpsimd.tensor_tensor(fin["rs"][:], fin["va"][:], half[:, 0:1].to_broadcast([TOK, GROUPS]), ALU.pow)\
                .then_inc(s_fin_rstd, 1)


def _by_tile(w):
    return w.reshape(w.shape[0] // 128, 128, -1).transpose(1, 0, 2)


def _layout(i):
    f = np.float32
    a = {}
    x = i["x"].reshape(IMAGES, 3, SIDE, PATCH, SIDE, PATCH).transpose(1, 3, 5, 0, 2, 4)
    x = x.reshape(PK * 128, IMAGES, SIDE * SIDE)
    xt = np.zeros((PK * 128, GROUPS * PER, SEQ), f)
    xt[:, :IMAGES, 1:] = x
    a["xT"] = np.ascontiguousarray(xt.reshape(PK, 128, GROUPS, TOK).transpose(2, 1, 0, 3))
    base = np.empty((PER, SEQ, E), f)
    base[:, 0] = i["cls_tok"].reshape(E)
    base[:, 1:] = i["L0_tok_b"]
    a["base"] = base.reshape(TOK, E)
    a["wtok"] = _by_tile(i["L0_tok_W"])
    per_kv = HEADS // (i["L1_ffn_kw"].shape[1] // HD)

    def spread(w):
        return np.repeat(w.reshape(w.shape[:-1] + (-1, HD)), per_kv, axis=-2).reshape(w.shape[:-1] + (E,))

    mats = {f"{p}_W{w}": i[f"{l}_W{w}"] for p, l in (("a", "L0_attn"), ("f", "L0_ffn"), ("l", "L1_attn"))
            for w in "qkvo"}
    mats |= {"g_Wq": i["L1_ffn_qw"], "g_Wk": spread(i["L1_ffn_kw"]), "g_Wv": spread(i["L1_ffn_vw"]),
             "g_Wo": i["L1_ffn_ow"]}
    a["mats"] = np.stack([_by_tile(mats[n]) for n in MATS], 1)
    rows = {"a_bo": i["L0_attn_bo"], "a_g": i["L0_attn_ln_gamma"], "a_b": i["L0_attn_ln_beta"],
            "f_bo": i["L0_ffn_bo"], "l_bq": i["L1_attn_bq"], "l_bk": i["L1_attn_bk"], "l_bv": i["L1_attn_bv"],
            "l_bo": i["L1_attn_bo"], "g_ob": i["L1_ffn_ob"], "g_n1": i["L1_ffn_norm1_w"],
            "g_n2": i["L1_ffn_norm2_w"]}
    a["rows"] = np.stack([rows[n] for n in ROWS])
    cols = {f"{p}_b{w}": i[f"{l}_b{w}"] for p, l in (("a", "L0_attn"), ("f", "L0_ffn")) for w in "qkv"}
    cols |= {"f_g1": i["L0_ffn_ln1_g"], "f_b1": i["L0_ffn_ln1_b"], "f_g2": i["L0_ffn_ln2_g"],
             "f_b2": i["L0_ffn_ln2_b"], "g_qb": i["L1_ffn_qb"], "g_kb": spread(i["L1_ffn_kb"]),
             "g_vb": spread(i["L1_ffn_vb"]), "l_m": np.repeat(i["L1_attn_m"], HD)}
    a["cols"] = np.stack([cols[n].reshape(CT, 128).T for n in COLS], 1)
    emb = i["L0_attn_dist_emb"]
    last = emb.shape[0] // 2
    near = emb[last - (SEQ - 1):last + SEQ]
    for n, t in (("relq", near[::-1]), ("relk", near)):
        wide = np.zeros((HC, HD, REL, HC), f)
        for h in range(HC):
            wide[h, :, :, h] = t.T
        a[n] = wide.reshape(128, REL, HC)
    a["wr0"], a["wr1"] = _by_tile(i["L0_ffn_Wr"]), _by_tile(i["L1_ffn_gate_w"])
    a["br0"] = i["L0_ffn_br"]
    a["eb1"] = i["L0_ffn_e_b1"].reshape(EXPERTS, F0 // 128, 128).transpose(0, 2, 1)
    a["eb2"] = i["L0_ffn_e_b2"]
    for n, w in (("e_w1", "L0_ffn_e_w1"), ("e_w2", "L0_ffn_e_w2"), ("g_w1", "L1_ffn_w1"), ("g_w2", "L1_ffn_w2")):
        w = i[w]
        a[n] = w.reshape(EXPERTS, w.shape[1] // 128, 128, -1).transpose(0, 2, 1, 3).reshape(EXPERTS, 128, -1)
    p, t = np.arange(128), np.arange(TOK)
    a["c_ident"] = np.eye(128, dtype=f)
    a["c_head_of_row"] = (p[:, None] // HD == np.arange(HC)).astype(f)
    a["c_third"] = (t[:, None] // SEQ == np.arange(HEADS) % HPC).astype(f)
    a["c_causal"] = np.where(np.arange(SEQ) > t[:, None] % SEQ, f(MASKED), f(0))
    a["c_of_image"] = (t[:, None] // SEQ == np.arange(PER)).astype(f)
    a["c_same_head"] = (p[:, None] // HD == p // HD).astype(f)
    a["c_before"] = (t[:, None] < t).astype(f)
    a["c_rev8"] = np.broadcast_to((EXPERTS - np.arange(EXPERTS)).astype(f), (TOK, EXPERTS))
    return {n: np.ascontiguousarray(v) for n, v in a.items()}


def kernel(**inputs):
    import concourse.bacc as bacc
    from concourse.bass_utils import run_bass_kernel_spmd

    arrays = _layout({n: np.asarray(v) for n, v in inputs.items()})
    nc = bacc.Bacc("TRN2", target_bir_lowering=False, num_devices=1)
    A = {n: nc.dram_tensor("in_" + n, v.shape, mybir.dt.from_np(v.dtype), kind="ExternalInput").ap()
         for n, v in arrays.items()}
    A["out"] = nc.dram_tensor("out", (TOK, GROUPS * E), F32, kind="ExternalOutput").ap()
    build_tower(nc, A)
    r = run_bass_kernel_spmd(nc, [{"in_" + n: v for n, v in arrays.items()}], core_ids=[0])
    out = r.results[0]["out"].reshape(PER, SEQ, GROUPS, E).transpose(2, 0, 1, 3)
    return np.ascontiguousarray(out.reshape(GROUPS * PER, SEQ, E)[:IMAGES])
```

```python
from contextlib import ExitStack

import numpy as np

import concourse.bass as bass
from concourse import mybir

F32 = mybir.dt.float32
I32, U32 = mybir.dt.int32, mybir.dt.uint32
ALU = mybir.AluOpType
ACT = mybir.ActivationFunctionType
AX = mybir.AxisListType

IMAGES, PER = 32, 3
GROUPS = -(-IMAGES // PER)
PATCH, SIDE = 16, 6
SEQ = SIDE * SIDE + 1
TOK = PER * SEQ
E, HEADS, HD = 256, 16, 16
CT = E // 128
HC = HEADS // CT
PK = 3 * PATCH * PATCH // 128
K0, K1 = (SEQ + 1) // 2, SEQ // 2
HS = SEQ * HEADS
REL = 2 * SEQ - 1
REL_CUTS = (0, 25, 49, 73)
HPC = 3
CHUNKS = -(-HEADS // HPC)
EXPERTS = 8
F0, F1 = 1024, 512
CAPACITY = int(1.25 * IMAGES * SEQ * 2 / EXPERTS)
LAST_REAL = (IMAGES - (GROUPS - 1) * PER) * SEQ
TILE = 128
TILES = (-(-IMAGES * SEQ // TILE), -(-CAPACITY // TILE))
AHEAD = 4
SLOTS = tuple(n * TILE for n in TILES)
FAR = 2 ** 20
EPS, EPS_A, EPS_R = 1e-5, 1e-12, 1e-6
MASKED = -1e30

ROWS = ["a_bo", "a_g", "a_b", "f_bo", "l_bq", "l_bk", "l_bv", "l_bo", "g_ob", "g_n1", "g_n2"]
COLS = ["a_bq", "a_bk", "a_bv", "f_g1", "f_b1", "f_g2", "f_b2", "f_bq", "f_bk", "f_bv",
        "g_qb", "g_kb", "g_vb", "l_m"]
MATS = ["a_Wq", "a_Wk", "a_Wv", "a_Wo", "f_Wq", "f_Wk", "f_Wv", "f_Wo", "l_Wq", "l_Wk", "l_Wv",
        "l_Wo", "g_Wq", "g_Wk", "g_Wv", "g_Wo"]


def build_tower(nc, A):
    ctx = ExitStack()
    with ctx:
        def sb(name, shape, dtype=F32):
            return ctx.enter_context(nc.sbuf_tensor("sb_" + name, shape, dtype))

        def sem(name):
            return ctx.enter_context(nc.semaphore(name))

        bank = [ctx.enter_context(nc.psum_tensor(f"bank{i}", [128, 512], F32)) for i in range(8)]

        ident = sb("ident", [128, 128])
        head_of_row = sb("head_of_row", [128, HC])
        third_of_head = sb("third_of_head", [TOK, HEADS])
        causal = sb("causal", [TOK, SEQ])
        of_image = sb("of_image", [TOK, PER])
        same_head = sb("same_head", [128, 128])
        before = sb("before", [TOK, TOK])
        ones = sb("ones", [TOK, TOK])
        half = sb("half", [TOK, 1])
        idle = sb("idle", [1, 128])
        eps = sb("eps", [TOK, 3])
        rev8 = sb("rev8", [TOK, EXPERTS])
        slot_base = sb("slot_base", [TOK, 2, EXPERTS])
        real = sb("real", [TOK, 1])
        fulls = sb("fulls", [1, TILES[0] - 1])
        row_step = sb("row_step", [1, 2, EXPERTS])
        rows = sb("rows", [TOK, len(ROWS), E])
        cols = sb("cols", [128, len(COLS), CT])
        mats = sb("mats", [128, len(MATS), CT, E])
        wtok = sb("wtok", [128, PK, E])
        base = sb("base", [TOK, E])
        relq = sb("relq", [128, REL, HC])
        relk = sb("relk", [128, REL, HC])
        wr0 = sb("wr0", [128, CT, EXPERTS])
        wr1 = sb("wr1", [128, CT, EXPERTS])
        br0 = sb("br0", [TOK, EXPERTS])
        b_up = [sb(f"b_up{i}", [128, F0 // 128]) for i in range(2)]
        b_dn = [sb(f"b_dn{i}", [TILE, E]) for i in range(2)]
        inv_scale = sb("inv_scale", [128, 2, CT])

        def row(name):
            return rows[:, ROWS.index(name), :]

        def col(name, c):
            return cols[:, COLS.index(name), c:c + 1]

        def mat(name, c, lo=0, hi=E):
            return mats[:, MATS.index(name), c, lo:hi]

        H = sb("H", [TOK, GROUPS * E])
        SRC_all = sb("SRC", [128, GROUPS * E])
        SRC = SRC_all[0:TOK, :]
        LOGITS = sb("LOGITS", [TOK, GROUPS, EXPERTS])
        GATE = sb("GATE", [TOK, GROUPS, EXPERTS])
        slot = sb("slot", [TOK, EXPERTS, GROUPS], U32)
        entry = sb("entry", [TOK, EXPERTS, GROUPS, 2])
        plan_f = sb("plan_f", [1, 2, 3, EXPERTS + 1])
        plan = sb("plan", [1, 2, 3, EXPERTS + 1], I32)
        ties_f = sb("ties_f", [1, 1])
        ties = sb("ties", [1, 1], I32)
        over = sb("over", [1, EXPERTS, TILES[0] - 1])
        in_list = sb("in_list", [TILE, 2])
        out_list = sb("out_list", [TILE, 2])
        x_rows = sb("x_rows", [TILE, E])
        x_T = sb("x_T", [128, CT, TILE])
        y_sum = sb("y_sum", [TILE, E])
        y_rows = sb("y_rows", [TILE, E])
        w_up = [sb(f"w_up{i}", [128, CT * F0]) for i in range(2)]
        w_dn = [sb(f"w_dn{i}", [128, F0 // 128 * E]) for i in range(2)]
        mid_flat = sb("mid", [128, 2 * REL * HEADS + 2 * HS])
        mid = mid_flat[:, 0:F0 // 128 * TILE].rearrange("p (f t) -> p f t", t=TILE)
        X_dram = nc.dram_tensor("X_dram", [GROUPS * TOK + TILE, E], F32, kind="Internal").ap()
        SUM_dram = nc.dram_tensor("SUM_dram", [GROUPS * TOK + TILE, E], F32, kind="Internal").ap()
        LIST_dram = [nc.dram_tensor(f"LIST_dram{i}", [EXPERTS * SLOTS[i], 2], F32, kind="Internal").ap()
                     for i in range(2)]
        rel_scratch = {n: nc.dram_tensor("scratch_" + n, [2, TOK, REL * HEADS], F32, kind="Internal").ap()
                       for n in ("q", "k")}

        def of_group(t, g, width=E):
            return t[:, bass.ds(g * width, width)]

        DVE_LINKS = {"rel": 10, "causal": 7, "gqa": 8}
        POOL_LINKS = {"rel": 2, "causal": 2, "gqa": 2}

        def attention(tag, banks, same_buffers=None):
            L = dict(tag=tag, b=banks, at=0, dve_at=0, pool_at=0)
            if same_buffers:
                L.update(same_buffers)
                L["tag"], L["at"] = tag, GROUPS
                L["dve_at"], L["pool_at"] = (GROUPS * k[same_buffers["tag"]] for k in (DVE_LINKS, POOL_LINKS))
                return L
            for n, shape in dict(
                    xin=[TOK, E], res=[TOK, E], hold=[TOK, E], work=[TOK, E], work2=[TOK, E],
                    xT=[128, CT, TOK], qT=[128, CT, TOK], kT=[128, CT, TOK], qM=[128, CT, PER, TOK],
                    kB=[128, CT, TOK, HC], vB=[TOK, PER, E], sc=[TOK, HS], pr=[TOK, HS],
                    mx=[TOK, HEADS], sm=[TOK, HEADS], pT=[128, CHUNKS, TOK], cx=[SEQ, PER, E],
                    cT=[128, CT, TOK], st=[TOK, 6], mv=[TOK, 2], va=[TOK, 2], rs=[TOK, 2],
                    st2=[TOK, 6], mv2=[TOK, 2], va2=[TOK, 1], rs2=[TOK, 1]).items():
                L[n] = sb(f"{tag}_{n}", shape)
            L["x3"] = L["pT"][:].rearrange("p t q -> p (t q)").rearrange("p (c j r k) -> p c j (r k)", c=CT, j=PER, r=HPC)
            for n in ("x3", "xin", "xT_psum", "xT", "qk_psum", "v_psum", "qT", "kT", "qM", "kB", "vB", "s_psum",
                      "shifted", "exped", "probs", "pT_psum", "pT", "c_psum", "cx", "cT_psum", "cT", "o_psum",
                      "stat", "rstd", "stat2", "rstd2", "in2", "bias_in", "done", "dve", "pool"):
                L["s_" + n] = sem(f"{tag}_{n}")
            return L

        a1 = attention("rel", bank[0:4])
        a2 = attention("causal", bank[4:8])
        a3 = attention("gqa", bank[4:8], same_buffers=a2)
        s_zeroed = sem("s_zeroed")

        patches = SRC_all[:, 0:PK * TOK].rearrange("p (k t) -> p k t", t=TOK)
        qe = mid_flat[0:TOK, 0:2 * REL * HEADS].rearrange("p (i r) -> p i r", i=2)
        relb = mid_flat[0:TOK, 2 * REL * HEADS:2 * REL * HEADS + 2 * HS].rearrange("p (i r) -> p i r", i=2)
        nT = sb("nT", [128, CT, TOK])
        gT = sb("gT", [128, CT, TOK])

        ln = dict(b=bank[0:4])
        kb_flat = a1["kB"][:].rearrange("p c t h -> p (c t h)")
        ln.update(xin=a1["xin"], hold=a1["hold"], xT=a1["xT"], q=a1["vB"], qT=a1["qT"], cT=a1["cT"],
                           sq=a1["sc"][:, 0:2 * E].rearrange("p (i e) -> p i e", i=2),
                           km=kb_flat[0:TOK, 0:PER * E].rearrange("p (j e) -> p j e", j=PER),
                           kv=kb_flat[:, PER * E:2 * PER * E].rearrange("p (c j d) -> p c j d", c=CT, j=PER))
        for n, shape in dict(ss=[TOK, 2, HEADS], ri=[TOK, 2, HEADS], st=[TOK, 6], mv=[TOK, 2],
                             va=[TOK, 1], rs=[TOK, 1]).items():
            ln[n] = sb("cos_" + n, shape)
        for n in ("stat", "rstd", "xin", "xT_psum", "xT", "qkv_psum", "qkv", "squares", "norm2", "norm", "qn",
                  "km", "qT_psum", "qT", "kv_psum", "kv", "cT_psum", "cT", "o_psum", "bias_in", "done", "dve",
                  "act", "pool"):
            ln["s_" + n] = sem("cos_" + n)
        LN_LINKS = 3

        s_const = sem("s_const")
        s_patch = sem("s_patch")
        s_tok = sem("s_tok")
        s_qe_psum = sem("s_qe_psum")
        s_qe = sem("s_qe")
        s_qe_out = [sem(f"s_qe_out{i}") for i in range(2)]
        s_rel_in = sem("s_rel_in")
        s_relsum = sem("s_relsum")
        s_nT_psum = sem("s_nT_psum")
        s_nT = sem("s_nT")
        s_log = sem("s_log")
        s_lg = sem("s_lg")
        s_scale = sem("s_scale")
        s_scale2 = sem("s_scale2")
        s_gT_psum = sem("s_gT_psum")
        s_gT = sem("s_gT")
        s_glog = sem("s_glog")
        s_glg = sem("s_glg")

        s_rows = sem("s_rows")
        s_idle = sem("s_idle")
        s_init = sem("s_init")
        s_weights = [sem(f"s_weights{i}") for i in range(2)]
        s_back = [sem(f"s_back{i}") for i in range(2)]
        s_tie_links = sem("s_tie_links")
        s_tie_entries = sem("s_tie_entries")
        s_tie_listed = sem("s_tie_listed")

        def mixture(i, width):
            M = dict(i=i, tag=f"moe{i}", width=width, nf=width // 128, tiles=TILES[i], slots=SLOTS[i])
            for n in ("exp", "chosen", "rank_psum", "plan", "entries", "listed", "up", "act",
                      "in_list", "x_rows", "xT_psum", "x_T", "down", "out_list", "y", "added"):
                M["s_" + n] = sem(f"moe{i}_{n}")
            return M

        m0, m1 = mixture(0, F0), mixture(1, F1)
        s_shifted0 = sem("s_shifted0")
        s_y_sum = sem("s_y_sum")
        s_links = sem("s_links")
        RING = 4
        tmp8 = [sb(f"tmp8_{i}", [TOK, GROUPS, EXPERTS]) for i in range(6)]
        order = sb("order", [TOK, GROUPS, EXPERTS])
        picked = sb("picked", [TOK, GROUPS, EXPERTS])
        tmp1 = [sb(f"tmp1_{i}", [TOK, GROUPS]) for i in range(3)]
        top8 = sb("top8", [TOK, GROUPS, 8])
        s_fin_stat = sem("s_fin_stat")
        s_fin_rstd = sem("s_fin_rstd")
        s_fin = sem("s_fin")
        s_out = sem("s_out")
        s_fin_pool = sem("s_fin_pool")
        fin = dict(st=sb("fin_st", [TOK, GROUPS, 6]), mv=sb("fin_mv", [TOK, GROUPS, 2]),
                              va=sb("fin_va", [TOK, GROUPS]), rs=sb("fin_rs", [TOK, GROUPS]))

        loads = [(ident, A["c_ident"]), (head_of_row, A["c_head_of_row"]), (third_of_head, A["c_third"]),
                 (causal, A["c_causal"]), (of_image, A["c_of_image"]), (same_head, A["c_same_head"]),
                 (before, A["c_before"]), (rev8, A["c_rev8"]),
                 (slot_base, A["c_slot_base"]), (real, A["c_real"]), (fulls, A["c_fulls"]),
                 (row_step, A["c_row_step"]), (entry, A["c_entry"]), (base, A["base"]), (wtok, A["wtok"]),
                 (cols, A["cols"]), (relq, A["relq"]), (relk, A["relk"]), (wr0, A["wr0"]), (wr1, A["wr1"]),
                 (mats, A["mats"])]
        N_LOADS = len(loads) + 2

        carriers = [0]

        def idle_element():
            carriers[0] += 1
            return idle[0:1, carriers[0] - 1:carriers[0]]

        def carry_dve():
            nc.vector.memset(idle_element(), 0.0)

        def carry_pool():
            nc.gpsimd.tensor_tensor(idle_element(), half[0:1, :], half[0:1, :], ALU.add)

        def carry_pe(free):
            nc.tensor.matmul(free[0:1, 0:1], ident[:, 0:1], ident[:, 0:1], start=True, stop=True)

        def walk(eng, M, tile, expert=None):
            i_ = M["i"]
            with eng.Fori(0, EXPERTS // 2) as i:
                for b in range(2):
                    e = 2 * i + b
                    n = eng.value_load(plan[0:1, i_, 0, bass.ds(e, 1)], min_val=1, max_val=M["tiles"])
                    at = eng.value_load(plan[0:1, i_, 1, bass.ds(e, 1)], min_val=0, max_val=M["tiles"] * EXPERTS)
                    if expert:
                        expert(i, b, e, at)
                    tile(i, b, e, 0, at)
                    for t in range(1, min(AHEAD, M["tiles"])):
                        with eng.If(n > t):
                            tile(i, b, e, t, at + t)
                    if M["tiles"] > AHEAD:
                        with eng.If(n > AHEAD):
                            with eng.Fori(AHEAD, M["tiles"]) as t:
                                with eng.If(n > t):
                                    tile(i, b, e, t, at + t)
                                eng.nop()
                            eng.nop()

        def tiles_so_far(eng, M):
            return eng.value_load(plan[0:1, M["i"], 1, EXPERTS:EXPERTS + 1], min_val=EXPERTS,
                                  max_val=M["tiles"] * EXPERTS)

        def after_first(eng, i, b, t, what):
            if b == 0 and isinstance(t, int) and t == 0:
                with eng.If(i > 0):
                    what()
            else:
                what()

        block = ctx.enter_context(nc.Block())

        LOADS = (4, 2)

        def weights_there(M, i):
            return 16 * (LOADS[0] * (i + 1) if M is m0 else LOADS[0] * EXPERTS // 2 + LOADS[1] * (i + 1))

        def load_expert(eng, M, e, b):
            up, down = (A["e_w1"], A["e_w2"]) if M is m0 else (A["g_w1"], A["g_w2"])
            for dst, src in ((w_up[b][:, 0:CT * M["width"]], up), (w_dn[b][:, 0:M["nf"] * E], down)):
                eng.dma_start(dst, src[bass.ds(e, 1)].rearrange("o p n -> p (o n)")).then_inc(s_weights[b], 16)
            if M is m0:
                eng.dma_start(b_up[b][:], A["eb1"][bass.ds(e, 1)].rearrange("o p n -> p (o n)"))\
                    .then_inc(s_weights[b], 16)
                eng.dma_start(b_dn[b][:], A["eb2"][bass.ds(e, 1)].rearrange("o n -> (o n)").partition_broadcast(TILE))\
                    .then_inc(s_weights[b], 16)

        @block.sync
        def _(sp):
            for dst, src in loads:
                sp.dma_start(dst[:], src[:]).then_inc(s_const, 16)
            sp.dma_start(rows[:].rearrange("p r e -> p (r e)"),
                         A["rows"].rearrange("r e -> (r e)").partition_broadcast(TOK)).then_inc(s_const, 16)
            sp.dma_start(br0[:], A["br0"].partition_broadcast(TOK)).then_inc(s_const, 16)

            def send_relative(n):
                for i, way in enumerate(("q", "k")):
                    sp.wait_ge(s_qe, 6 * n + 3 * i + 3)
                    dst = rel_scratch[way][0]
                    sp.dma_start(dst, qe[:, i, :]).then_inc(s_qe_out[i], 16)
                for i, way in enumerate(("q", "k")):
                    sp.wait_ge(s_qe_out[i], 16 * (n + 1))
                    src = rel_scratch[way]
                    wide = REL * HEADS
                    for j in range(PER):
                        at = src.offset + j * SEQ * wide + (SEQ - 1) * HEADS
                        if way == "q":
                            ap = [[wide - HEADS, SEQ], [1, HS]]
                        else:
                            ap = [[HEADS, SEQ], [wide - HEADS, SEQ], [1, HEADS]]
                        dst = relb[j * SEQ:(j + 1) * SEQ, i, :]
                        if way == "k":
                            dst = dst.rearrange("p (r h) -> p r h", h=HEADS)
                        sp.dma_start(dst, bass.AP(tensor=src.tensor, offset=at, ap=ap)).then_inc(s_rel_in, 16)

            sp.dma_start(patches, A["xT"][0]).then_inc(s_patch, 16)
            load_expert(sp, m0, 0, 0)
            send_relative(0)
            with sp.Fori(1, GROUPS) as n:
                sp.wait_ge(s_tok, n)
                sp.dma_start(patches, A["xT"][bass.ds(n, 1)].rearrange("o p k t -> p (o k) t"))\
                    .then_inc(s_patch, 16)
                send_relative(n)

            def lists(M):
                i_ = M["i"]
                sp.wait_ge(M["s_plan"], 1)
                sp.wait_ge(M["s_listed"], 16 * 2 * GROUPS)
                if M is m0:
                    more = sp.value_load(ties[0:1, 0:1], min_val=0, max_val=EXPERTS * IMAGES * SEQ)
                    with sp.If(more > 0):
                        sp.wait_ge(s_tie_listed, 16 * (EXPERTS - 2) * GROUPS)
                    sp.nop()

                def out_of(u, slot_):
                    sp.wait_ge(M["s_added"], 16 * u)
                    sp.dma_start(out_list[:], LIST_dram[i_][bass.ds(slot_, TILE)]).then_inc(M["s_out_list"], 16)

                def tile(i, b, e, t, u):
                    sp.wait_ge(M["s_xT_psum"], u + 1)
                    sp.dma_start(in_list[:], LIST_dram[i_][bass.ds(e * M["slots"] + t * TILE, TILE)])\
                        .then_inc(M["s_in_list"], 16)

                    def before_it():
                        if isinstance(t, int) and t == 0:
                            out_of(u, sp.value_load(plan[0:1, i_, 2, bass.ds(e, 1)], min_val=0,
                                                    max_val=EXPERTS * M["slots"] - TILE))
                        else:
                            out_of(u, e * M["slots"] + (t - 1) * TILE)
                    after_first(sp, i, b, t, before_it)

                walk(sp, M, tile)
                u = tiles_so_far(sp, M)
                out_of(u, sp.value_load(plan[0:1, i_, 2, EXPERTS:EXPERTS + 1], min_val=0,
                                        max_val=EXPERTS * M["slots"] - TILE))
                sp.wait_ge(M["s_added"], 16 * (u + 1))

            def sum_rows(lo, hi):
                return SUM_dram[lo * TOK:hi * TOK].rearrange("(g t) e -> t g e", t=TOK)

            def groups_of(t, lo, hi):
                return t[:, lo * E:hi * E].rearrange("t (g e) -> t g e", e=E)

            lists(m0)
            sp.dma_start(groups_of(H, 0, 1), sum_rows(0, 1)).then_inc(s_back[0], 16)
            sp.dma_start(groups_of(H, 1, GROUPS), sum_rows(1, GROUPS)).then_inc(s_back[1], 16)
            load_expert(sp, m1, 0, 0)
            lists(m1)
            sp.dma_start(groups_of(SRC, 0, GROUPS), sum_rows(0, GROUPS)).then_inc(s_back[0], 16)
            sp.wait_ge(s_fin, GROUPS)
            sp.dma_start(A["out"], H[:]).then_inc(s_out, 16)
            sp.wait_ge(s_out, 16)

        @block.tensor
        def _(pe):
            def transpose_in(L, n):
                pe.wait_ge(L["s_xin"], L["at"] + n + 1)
                for c in range(CT):
                    last = nc.tensor.transpose(L["b"][0][:, c * TOK:(c + 1) * TOK], L["xin"][:, c * 128:(c + 1) * 128],
                                               ident[0:TOK, 0:TOK])
                last.then_inc(L["s_xT_psum"], 1)

            def project(L, n, p):
                pe.wait_ge(L["s_xT"], L["at"] + n + 1)
                for w, dst in (("q", L["b"][1]), ("k", L["b"][2])):
                    for m in range(CT):
                        for c in range(CT):
                            last = nc.tensor.matmul(dst[:, m * TOK:(m + 1) * TOK],
                                                    mat(f"{p}_W{w}", c, m * 128, (m + 1) * 128), L["xT"][:, c, :],
                                                    start=(c == 0), stop=(c == CT - 1))
                last.then_inc(L["s_qk_psum"], 1)
                pe.wait_ge(L["s_x3"], L["at"] + n + 1)
                for j in range(PER):
                    dst = (L["b"][0][0:TOK, j * E:(j + 1) * E] if j < 2 else L["b"][3][0:TOK, 0:E])
                    for c in range(CT):
                        last = nc.tensor.matmul(dst, L["x3"][:, c, j, :], mat(f"{p}_Wv", c), start=(c == 0), stop=(c == CT - 1))
                last.then_inc(L["s_v_psum"], 1)

            def scores(L, n):
                pe.wait_ge(L["s_kB"], L["at"] + n + 1)
                pe.wait_ge(L["s_qM"], L["at"] + n + 1)
                for b, (lo, hi) in enumerate(((0, K0), (K0, SEQ))):
                    dst = L["b"][1 + b][0:TOK, 0:(hi - lo) * HEADS].rearrange("p (k h) -> p k h", h=HEADS)
                    for j in range(PER):
                        for c in range(CT):
                            last = nc.tensor.matmul(dst[:, :, c * HC:(c + 1) * HC], L["qM"][:, c, j, :],
                                                    L["kB"][:, c, j * SEQ + lo:j * SEQ + hi, :],
                                                    start=(j == 0 and c == 0), stop=(j == PER - 1 and c == CT - 1),
                                                    skip_group_check=True)
                last.then_inc(L["s_s_psum"], 1)

            def transpose_probs(L, n):
                pe.wait_ge(L["s_probs"], L["at"] + n + 1)
                for t in range(CHUNKS):
                    w = min(HPC * SEQ, HS - t * HPC * SEQ)
                    dst = L["b"][0 if t < 3 else 3][0:w, (t % 3) * TOK:(t % 3 + 1) * TOK]
                    last = nc.tensor.transpose(dst, L["pr"][:, t * HPC * SEQ:t * HPC * SEQ + w], ident[0:TOK, 0:TOK])
                last.then_inc(L["s_pT_psum"], 1)

            def contexts(L, n):
                pe.wait_ge(L["s_pT"], L["at"] + n + 1)
                for j in range(PER):
                    dst = L["b"][1][0:SEQ, j * E:(j + 1) * E] if j < 2 else L["b"][2][0:SEQ, 0:E]
                    for t in range(CHUNKS):
                        h = min(HPC, HEADS - t * HPC)
                        at = t * HPC * HD
                        last = nc.tensor.matmul(dst[:, at:at + h * HD],
                                                L["pT"][0:h * SEQ, t, j * SEQ:(j + 1) * SEQ],
                                                L["vB"][0:h * SEQ, j, at:at + h * HD],
                                                start=True, stop=True)
                last.then_inc(L["s_c_psum"], 1)

            def transpose_ctx(L, n):
                pe.wait_ge(L["s_cx"], L["at"] + n + 1)
                carry_pe(L["b"][0])
                for c in range(CT):
                    for j in range(PER):
                        at = c * TOK + j * SEQ
                        last = nc.tensor.transpose(L["b"][0][:, at:at + SEQ], L["cx"][:, j, c * 128:(c + 1) * 128],
                                                   ident[0:SEQ, 0:SEQ])
                last.then_inc(L["s_cT_psum"], 1)

            def output(L, n, p):
                pe.wait_ge(L["s_cT"], L["at"] + n + 1)
                for c in range(CT):
                    last = nc.tensor.matmul(L["b"][3][0:TOK, 0:E], L["cT"][:, c, :], mat(f"{p}_Wo", c),
                                            start=(c == 0), stop=(c == CT - 1))
                last.then_inc(L["s_o_psum"], 1)

            def embed(n, first=False):
                pe.wait_ge(s_patch, 16 * (n + 1))
                if not first:
                    pe.wait_ge(a1["s_done"], n)
                for k in range(PK):
                    last = nc.tensor.matmul(bank[1][0:TOK, 0:E], patches[:, k, :], wtok[:, k, :],
                                            start=(k == 0), stop=(k == PK - 1))
                last.then_inc(s_tok, 1)

            def distances(n):
                pe.wait_ge(a1["s_qT"], n + 1)
                pe.wait_ge(a1["s_kT"], n + 1)
                pe.wait_ge(a1["s_vB"], n + 1)
                for i, (x, table) in enumerate(((a1["qT"], relq), (a1["kT"], relk))):
                    for part in range(3):
                        u = 3 * i + part
                        lo, hi = REL_CUTS[part], REL_CUTS[part + 1]
                        if u >= 2:
                            pe.wait_ge(s_qe, 6 * n + u - 1)
                        dst = a1["b"][0 if u % 2 == 0 else 3][0:TOK, 0:(hi - lo) * HEADS]
                        dst = dst.rearrange("p (r h) -> p r h", h=HEADS)
                        for c in range(CT):
                            last = nc.tensor.matmul(dst[:, :, c * HC:(c + 1) * HC], x[:, c, :],
                                                    table[:, lo:hi, :], start=(c == 0), stop=(c == CT - 1),
                                                    skip_group_check=True)
                        last.then_inc(s_qe_psum, 1)

            def router(L, n, s_in, src, s_psum, s_T, dstT, w, s_logit):
                pe.wait_ge(s_in, L["at"] + n + 1)
                for c in range(CT):
                    last = nc.tensor.transpose(L["b"][0][:, c * TOK:(c + 1) * TOK], src[:, c * 128:(c + 1) * 128],
                                               ident[0:TOK, 0:TOK])
                last.then_inc(s_psum, 1)
                pe.wait_ge(s_T, n + 1)
                for c in range(CT):
                    last = nc.tensor.matmul(L["b"][1][0:TOK, 0:EXPERTS], dstT[:, c, :], w[:, c, :],
                                            start=(c == 0), stop=(c == CT - 1))
                last.then_inc(s_logit, 1)

            def rel_first(n, first=False):
                embed(n, first)
                transpose_in(a1, n)
                project(a1, n, "a")

            def rel_block(n, first=False):
                rel_first(n, first)
                distances(n)
                scores(a1, n)
                transpose_probs(a1, n)
                contexts(a1, n)
                transpose_ctx(a1, n)
                output(a1, n, "a")

            def causal_block(n):
                transpose_in(a2, n)
                project(a2, n, "f")
                scores(a2, n)
                transpose_probs(a2, n)
                contexts(a2, n)
                transpose_ctx(a2, n)
                output(a2, n, "f")
                router(a2, n, a2["s_in2"], a2["work2"], s_nT_psum, s_nT, nT, wr0, s_log)

            pe.wait_ge(s_const, 16 * N_LOADS)
            rel_block(0, first=True)
            with pe.Fori(1, GROUPS) as n:
                embed(n)
                transpose_in(a2, n - 1)
                transpose_in(a1, n)
                project(a2, n - 1, "f")
                project(a1, n, "a")
                scores(a2, n - 1)
                distances(n)
                scores(a1, n)
                transpose_probs(a2, n - 1)
                contexts(a2, n - 1)
                transpose_ctx(a2, n - 1)
                transpose_probs(a1, n)
                output(a2, n - 1, "f")
                contexts(a1, n)
                router(a2, n - 1, a2["s_in2"], a2["work2"], s_nT_psum, s_nT, nT, wr0, s_log)
                transpose_ctx(a1, n)
                output(a1, n, "a")
            causal_block(GROUPS - 1)

            def rank(M):
                pe.wait_ge(M["s_chosen"], 1)
                flat = "p g e -> p (g e)"
                n = GROUPS * EXPERTS
                nc.tensor.matmul(bank[0][0:TOK, 0:n], before[:, :], tmp8[1][:].rearrange(flat), start=True, stop=False)
                nc.tensor.matmul(bank[0][0:TOK, 0:n], ones[:, :], tmp8[2][:].rearrange(flat), start=False, stop=True)
                nc.tensor.matmul(bank[0][0:TOK, n:n + EXPERTS], ones[:, :], tmp8[1][:, GROUPS - 1, :], start=True, stop=False)
                nc.tensor.matmul(bank[0][0:TOK, n:n + EXPERTS], ones[:, :], tmp8[2][:, GROUPS - 1, :], start=False, stop=True)\
                    .then_inc(M["s_rank_psum"], 1)

            def experts(M):
                nf, width = M["nf"], M["width"]
                pe.wait_ge(M["s_plan"], 1)

                def down(u, f, b):
                    pe.wait_ge(M["s_act"], RING + u * nf + f + 1)
                    return nc.tensor.matmul(bank[5][:, 0:E], mid[:, f, :], w_dn[b][:, f * E:(f + 1) * E],
                                            start=(f == 0), stop=(f == nf - 1))

                def tail(u, b):
                    down(u, nf - 2, b)
                    down(u, nf - 1, b).then_inc(M["s_down"], 1)

                def tile(i, b, e, t, u):
                    pe.wait_ge(M["s_x_rows"], 16 * (u + 1))
                    carry_pe(bank[4])
                    pe.wait_ge(M["s_x_T"], u + 1)
                    carry_pe(bank[4])
                    for c in range(CT):
                        last = nc.tensor.transpose(bank[4][:, c * TILE:(c + 1) * TILE], x_rows[:, c * 128:(c + 1) * 128],
                                                   ident[:, :])
                    last.then_inc(M["s_xT_psum"], 1)
                    start = isinstance(t, int) and t == 0
                    after_first(pe, i, b, t, lambda: tail(u - 1, 1 - b if start else b))
                    if start:
                        pe.wait_ge(s_weights[b], weights_there(M, i))
                    pe.wait_ge(M["s_x_T"], u + 2)
                    for f in range(nf):
                        pe.wait_ge(M["s_act"], RING + u * nf + f - 3)
                        for c in range(CT):
                            at = c * width + f * 128
                            last = nc.tensor.matmul(bank[f % RING][:, 0:TILE], w_up[b][:, at:at + 128], x_T[:, c, :],
                                                    start=(c == 0), stop=(c == CT - 1))
                        last.then_inc(M["s_up"], 1)
                        if f == 2:
                            pe.wait_ge(M["s_y"], u + 1)
                        if f >= 2:
                            down(u, f - 2, b)

                pe.sem_inc(M["s_xT_psum"], 1)
                pe.sem_inc(M["s_down"], 1)
                walk(pe, M, tile)
                tail(tiles_so_far(pe, M) - 1, 1)

            rank(m0)
            experts(m0)

            def cos_block_1(n):
                pe.wait_ge(ln["s_xin"], n + 1)
                for c in range(CT):
                    last = nc.tensor.transpose(ln["b"][0][:, c * TOK:(c + 1) * TOK], ln["xin"][:, c * 128:(c + 1) * 128],
                                               ident[0:TOK, 0:TOK])
                last.then_inc(ln["s_xT_psum"], 1)

            def cos_block_2(n):
                pe.wait_ge(ln["s_xT"], n + 1)
                for i, w in enumerate("qkv"):
                    for c in range(CT):
                        last = nc.tensor.matmul(ln["b"][1 + i][0:TOK, 0:E], ln["xT"][:, c, :], mat(f"l_W{w}", c),
                                                start=(c == 0), stop=(c == CT - 1))
                last.then_inc(ln["s_qkv_psum"], 1)

            def cos_block_3(n):
                pe.wait_ge(ln["s_qn"], n + 1)
                for c in range(CT):
                    last = nc.tensor.transpose(ln["b"][0][:, c * TOK:(c + 1) * TOK], ln["q"][:, 0, c * 128:(c + 1) * 128],
                                               ident[0:TOK, 0:TOK])
                last.then_inc(ln["s_qT_psum"], 1)
                pe.wait_ge(ln["s_km"], n + 1)
                for c in range(CT):
                    for j in range(PER):
                        last = nc.tensor.matmul(ln["b"][1 + c][:, j * 128:(j + 1) * 128],
                                                ln["km"][:, j, c * 128:(c + 1) * 128],
                                                ln["q"][:, 2, c * 128:(c + 1) * 128], start=True, stop=True)
                last.then_inc(ln["s_kv_psum"], 1)

            def cos_block_4(n):
                pe.wait_ge(ln["s_qT"], n + 1)
                pe.wait_ge(ln["s_kv"], n + 1)
                for c in range(CT):
                    for j in range(PER):
                        at = c * TOK + j * SEQ
                        last = nc.tensor.matmul(ln["b"][3][:, at:at + SEQ], ln["kv"][:, c, j, :],
                                                ln["qT"][:, c, j * SEQ:(j + 1) * SEQ], start=True, stop=True)
                last.then_inc(ln["s_cT_psum"], 1)

            def cos_block_5(n):
                pe.wait_ge(ln["s_cT"], n + 1)
                for c in range(CT):
                    last = nc.tensor.matmul(ln["b"][0][0:TOK, 0:E], ln["cT"][:, c, :], mat("l_Wo", c),
                                            start=(c == 0), stop=(c == CT - 1))
                last.then_inc(ln["s_o_psum"], 1)

            cos_block_1(0)
            cos_block_2(0)
            cos_block_3(0)
            cos_block_4(0)
            cos_block_5(0)
            with pe.Fori(1, GROUPS) as n:
                transpose_in(a3, n - 1)
                cos_block_1(n)
                project(a3, n - 1, "g")
                cos_block_2(n)
                scores(a3, n - 1)
                cos_block_3(n)
                transpose_probs(a3, n - 1)
                cos_block_4(n)
                contexts(a3, n - 1)
                cos_block_5(n)
                transpose_ctx(a3, n - 1)
                output(a3, n - 1, "g")
                router(a3, n - 1, a3["s_in2"], a3["work2"], s_gT_psum, s_gT, gT, wr1, s_glog)
            n = GROUPS - 1
            transpose_in(a3, n)
            project(a3, n, "g")
            scores(a3, n)
            transpose_probs(a3, n)
            contexts(a3, n)
            transpose_ctx(a3, n)
            output(a3, n, "g")
            router(a3, n, a3["s_in2"], a3["work2"], s_gT_psum, s_gT, gT, wr1, s_glog)

            rank(m1)
            experts(m1)

        @block.scalar
        def _(act):
            def copy_scaled(L, n, p=None):
                act.wait_ge(L["s_xT_psum"], L["at"] + n + 1)
                if p is None:
                    nc.scalar.activation(L["xT"][:].rearrange("p c t -> p (c t)"), L["b"][0][:, 0:CT * TOK], ACT.Copy)\
                        .then_inc(L["s_xT"], 1)
                    return
                for c in range(CT):
                    last = nc.scalar.activation(L["xT"][:, c, :], L["b"][0][:, c * TOK:(c + 1) * TOK], ACT.Identity,
                                                bias=col(p + "_b1", c), scale=col(p + "_g1", c))
                last.then_inc(L["s_xT"], 1)

            def queries_keys(L, n, bq, bk):
                act.wait_ge(L["s_qk_psum"], L["at"] + n + 1)
                for src, dst, bias, s in ((L["b"][1], L["qT"], bq, L["s_qT"]), (L["b"][2], L["kT"], bk, L["s_kT"])):
                    for c in range(CT):
                        last = nc.scalar.activation(dst[:, c, :], src[:, c * TOK:(c + 1) * TOK], ACT.Identity,
                                                    bias=col(bias, c))
                    last.then_inc(s, 1)

            def exps(L, n):
                act.wait_ge(L["s_shifted"], L["at"] + n + 1)
                nc.scalar.activation(L["pr"][:].rearrange("p (h k) -> p k h", h=HEADS),
                                     L["sc"][:].rearrange("p (k h) -> p k h", h=HEADS), ACT.Exp, scale=HD ** -0.5)\
                    .then_inc(L["s_exped"], 1)

            def probs_T(L, n):
                act.wait_ge(L["s_pT_psum"], L["at"] + n + 1)
                full = HPC * SEQ
                nc.scalar.activation(L["pT"][0:full, 0:3, :].rearrange("p t q -> p (t q)"), L["b"][0][0:full, 0:3 * TOK], ACT.Copy)
                nc.scalar.activation(L["pT"][0:full, 3:5, :].rearrange("p t q -> p (t q)"), L["b"][3][0:full, 0:2 * TOK], ACT.Copy)
                nc.scalar.activation(L["pT"][0:SEQ, 5, :], L["b"][3][0:SEQ, 2 * TOK:3 * TOK], ACT.Copy)\
                    .then_inc(L["s_pT"], 1)

            def ctx_out(L, n):
                act.wait_ge(L["s_c_psum"], L["at"] + n + 1)
                nc.scalar.activation(L["cx"][:, 0:2, :].rearrange("p j e -> p (j e)"), L["b"][1][0:SEQ, 0:2 * E], ACT.Copy)
                nc.scalar.activation(L["cx"][:, 2, :], L["b"][2][0:SEQ, 0:E], ACT.Copy).then_inc(L["s_cx"], 1)

            def ctx_T(L, n, bv):
                act.wait_ge(L["s_cT_psum"], L["at"] + n + 1)
                for c in range(CT):
                    last = nc.scalar.activation(L["cT"][:, c, :], L["b"][0][:, c * TOK:(c + 1) * TOK], ACT.Identity,
                                                bias=col(bv, c))
                last.then_inc(L["s_cT"], 1)

            def distances(n):
                for i in range(2):
                    for part in range(3):
                        u = 3 * i + part
                        lo, hi = REL_CUTS[part], REL_CUTS[part + 1]
                        act.wait_ge(s_qe_psum, 6 * n + u + 1)
                        nc.scalar.activation(qe[:, i, lo * HEADS:hi * HEADS],
                                             a1["b"][0 if u % 2 == 0 else 3][0:TOK, 0:(hi - lo) * HEADS], ACT.Copy)\
                            .then_inc(s_qe, 1)

            def normed_T(n, first=False):
                act.wait_ge(s_nT_psum, n + 1)
                for c in range(CT):
                    last = nc.scalar.activation(nT[:, c, :], a2["b"][0][:, c * TOK:(c + 1) * TOK], ACT.Identity,
                                                bias=col("f_b2", c), scale=col("f_g2", c))
                last.then_inc(s_nT, 1)
                act.wait_ge(a2["s_in2"], n + 1)
                act.dma_start(X_dram[bass.ds(n * TOK, TOK)], a2["work2"][:]).then_inc(s_rows, 16)
                act.wait_ge(a2["s_done"], n + 1)
                act.dma_start(SUM_dram[bass.ds(n * TOK, TOK)], of_group(H, n)).then_inc(s_rows, 16)

            act.dma_start(LIST_dram[0], A["c_list0"]).then_inc(s_init, 16)
            act.dma_start(LIST_dram[1], A["c_list1"]).then_inc(s_init, 16)
            act.wait_ge(s_const, 16 * N_LOADS)
            copy_scaled(a1, 0)
            queries_keys(a1, 0, "a_bq", "a_bk")
            distances(0)
            exps(a1, 0)
            probs_T(a1, 0)
            ctx_out(a1, 0)
            ctx_T(a1, 0, "a_bv")
            with act.Fori(1, GROUPS) as n:
                m = n - 1
                copy_scaled(a2, m, "f")
                copy_scaled(a1, n)
                queries_keys(a2, m, "f_bq", "f_bk")
                queries_keys(a1, n, "a_bq", "a_bk")
                distances(n)
                exps(a2, m)
                probs_T(a2, m)
                ctx_out(a2, m)
                exps(a1, n)
                ctx_T(a2, m, "f_bv")
                probs_T(a1, n)
                ctx_out(a1, n)
                normed_T(m)
                ctx_T(a1, n, "a_bv")
            m = GROUPS - 1
            copy_scaled(a2, m, "f")
            queries_keys(a2, m, "f_bq", "f_bk")
            exps(a2, m)
            probs_T(a2, m)
            ctx_out(a2, m)
            ctx_T(a2, m, "f_bv")
            normed_T(m)

            act.wait_ge(s_shifted0, 1)
            nc.scalar.activation(tmp8[1][:], tmp8[0][:], ACT.Exp).then_inc(m0["s_exp"], 1)

            def gelus(M, norm, bias):
                nf = M["nf"]
                act.sem_inc(M["s_act"], RING)
                act.wait_ge(M["s_plan"], 1)

                def tile(i, b, e, t, u):
                    start = isinstance(t, int) and t == 0
                    if start and bias:
                        act.wait_ge(s_weights[b], weights_there(M, i))
                    act.wait_ge(M["s_xT_psum"], u + 2)
                    for c in range(CT):
                        kw = dict(bias=col("f_b2", c), scale=col("f_g2", c)) if norm else {}
                        last = nc.scalar.activation(x_T[:, c, :], bank[4][:, c * TILE:(c + 1) * TILE],
                                                    ACT.Identity if norm else ACT.Copy, **kw)
                    last.then_inc(M["s_x_T"], 1)
                    for f in range(nf):
                        act.wait_ge(M["s_up"], u * nf + f + 1)
                        kw = dict(bias=b_up[b][:, f:f + 1]) if bias else {}
                        nc.scalar.activation(mid[:, f, :], bank[f % RING][:, 0:TILE], ACT.Gelu, **kw)\
                            .then_inc(M["s_act"], 1)
                        if f == 2 and start:
                            def load_next():
                                act.wait_ge(M["s_down"], u + 1)
                                act.wait_ge(M["s_y"], u + 1)
                                load_expert(act, M, nc.s_assert_within(e + 1, 1, EXPERTS - 1), 1 - b)
                            if b == 0:
                                load_next()
                            else:
                                with act.If(i < EXPERTS // 2 - 1):
                                    load_next()

                act.sem_inc(M["s_x_T"], 1)
                walk(act, M, tile)

            gelus(m0, True, True)

            nc.scalar.activation(inv_scale[:, 0, :], cols[:, COLS.index("l_m"), :], ACT.Sigmoid)\
                .then_inc(s_scale, 1)
            act.wait_ge(s_scale, 1)
            nc.scalar.activation(inv_scale[:, 1, :], inv_scale[:, 0, :], ACT.Exp, scale=-float(np.log(SEQ)))\
                .then_inc(s_scale2, 1)

            def cos_1(n):
                act.wait_ge(ln["s_xT_psum"], n + 1)
                nc.scalar.activation(ln["xT"][:].rearrange("p c t -> p (c t)"), ln["b"][0][:, 0:CT * TOK], ACT.Copy)\
                    .then_inc(ln["s_xT"], 1)

            def cos_2(n):
                act.wait_ge(ln["s_norm2"], n + 1)
                nc.scalar.activation(ln["ri"][:], ln["ss"][:], ACT.Ln).then_inc(ln["s_act"], 1)
                act.wait_ge(ln["s_act"], n + 1)
                nc.scalar.activation(ln["ss"][:], ln["ri"][:], ACT.Exp, scale=0.5).then_inc(ln["s_norm"], 1)

            def cos_3(n):
                act.wait_ge(ln["s_qT_psum"], n + 1)
                nc.scalar.activation(ln["qT"][:].rearrange("p c t -> p (c t)"), ln["b"][0][:, 0:CT * TOK], ACT.Copy)\
                    .then_inc(ln["s_qT"], 1)

            def cos_4(n):
                act.wait_ge(ln["s_cT_psum"], n + 1)
                nc.scalar.activation(ln["cT"][:].rearrange("p c t -> p (c t)"), ln["b"][3][:, 0:CT * TOK], ACT.Copy)\
                    .then_inc(ln["s_cT"], 1)

            def src_T(n):
                act.wait_ge(s_gT_psum, n + 1)
                nc.scalar.activation(gT[:].rearrange("p c t -> p (c t)"), a3["b"][0][:, 0:CT * TOK], ACT.Copy)\
                    .then_inc(s_gT, 1)
                act.wait_ge(a3["s_in2"], a3["at"] + n + 1)
                act.dma_start(X_dram[bass.ds(n * TOK, TOK)], a3["work2"][:]).then_inc(s_rows, 16)
                act.dma_start(SUM_dram[bass.ds(n * TOK, TOK)], a3["work2"][:]).then_inc(s_rows, 16)

            for st in (cos_1, cos_2, cos_3, cos_4):
                st(0)
            with act.Fori(1, GROUPS) as n:
                m = n - 1
                copy_scaled(a3, m)
                cos_1(n)
                queries_keys(a3, m, "g_qb", "g_kb")
                cos_2(n)
                exps(a3, m)
                cos_3(n)
                probs_T(a3, m)
                cos_4(n)
                ctx_out(a3, m)
                ctx_T(a3, m, "g_vb")
                src_T(m)
            m = GROUPS - 1
            copy_scaled(a3, m)
            queries_keys(a3, m, "g_qb", "g_kb")
            exps(a3, m)
            probs_T(a3, m)
            ctx_out(a3, m)
            ctx_T(a3, m, "g_vb")
            src_T(m)
            act.wait_ge(s_glg, GROUPS)
            nc.scalar.activation(tmp8[0][:], LOGITS[:], ACT.Sigmoid).then_inc(m1["s_exp"], 1)
            gelus(m1, False, False)

        @block.vector
        def _(dve):
            link_no = {}

            def link(L, n, ins):
                k = link_no[L["tag"]] = link_no.get(L["tag"], 0) + 1
                ins.then_inc(L["s_dve"], 1)
                dve.wait_ge(L["s_dve"], L["dve_at"] + n * DVE_LINKS[L["tag"]] + k)

            def end_links(L):
                assert link_no[L["tag"]] == DVE_LINKS[L["tag"]], (L["tag"], link_no[L["tag"]])
                link_no[L["tag"]] = 0

            def normed(out, x, mean, rstd):
                return nc.vector.tensor_scalar(out, x, mean, rstd, ALU.subtract, ALU.mult)

            def rel_pre(n, first=False):
                dve.wait_ge(s_tok, n + 1)
                link(a1, n, nc.vector.tensor_tensor(a1["hold"][:], bank[1][0:TOK, 0:E], base[:], ALU.add))
                link(a1, n, nc.vector.bn_stats(a1["st"][:], a1["hold"][:]))
                carry_dve()
                nc.vector.bn_aggr(a1["mv"][:], a1["st"][:]).then_inc(a1["s_stat"], 1)
                dve.wait_ge(a1["s_rstd"], n + 1)
                normed(a1["xin"][:], a1["hold"][:], a1["mv"][:, 0:1], a1["rs"][:, 0:1]).then_inc(a1["s_xin"], 1)

            def causal_pre(n, first=False):
                dve.wait_ge(a1["s_done"], n + 1)
                link(a2, n, nc.vector.bn_stats(a2["st"][:], of_group(H, n)))
                carry_dve()
                nc.vector.bn_aggr(a2["mv"][:], a2["st"][:]).then_inc(a2["s_stat"], 1)
                dve.wait_ge(a2["s_rstd"], n + 1)
                normed(a2["xin"][:], of_group(H, n), a2["mv"][:, 0:1], a2["rs"][:, 1:2])
                normed(a2["res"][:], of_group(H, n), a2["mv"][:, 0:1], a2["rs"][:, 0:1]).then_inc(a2["s_xin"], 1)

            def keys(L, n):
                dve.wait_ge(L["s_kT"], L["at"] + n + 1)
                k = L["kT"][:].rearrange("p c t -> p (c t)")
                nc.vector.tensor_tensor(
                    L["kB"][:].rearrange("p c t h -> p (c t) h"), k[:, :, None].to_broadcast([128, CT * TOK, HC]),
                    head_of_row[:, None, :].to_broadcast([128, CT * TOK, HC]), ALU.mult).then_inc(L["s_kB"], 1)

            def values(L, n):
                dve.wait_ge(L["s_v_psum"], L["at"] + n + 1)
                for lo, hi, src in ((0, 2, L["b"][0]), (2, 3, L["b"][3])):
                    w = (hi - lo)
                    v = src[0:TOK, 0:w * E].rearrange("p (j h d) -> p j h d", j=w, h=HEADS)
                    m_ = third_of_head[:, None, :, None].to_broadcast([TOK, w, HEADS, HD])
                    last = nc.vector.tensor_tensor(L["vB"][:, lo:hi, :].rearrange("p j (h d) -> p j h d", h=HEADS),
                                                   v, m_, ALU.mult)
                last.then_inc(L["s_vB"], 1)

            def shift(L, n, extra):
                dve.wait_ge(L["s_s_psum"], L["at"] + n + 1)
                for b, (lo, hi) in enumerate(((0, K0), (K0, SEQ))):
                    s = L["b"][1 + b][0:TOK, 0:(hi - lo) * HEADS].rearrange("p (k h) -> p k h", h=HEADS)
                    o = L["sc"][:, lo * HEADS:hi * HEADS].rearrange("p (k h) -> p k h", h=HEADS)
                    if extra == "rel":
                        ins = nc.vector.tensor_tensor(o, s, relb[:, 0, lo * HEADS:hi * HEADS]
                                                      .rearrange("p (k h) -> p k h", h=HEADS), ALU.add)
                    elif extra == "causal":
                        ins = nc.vector.tensor_tensor(o, s, causal[:, lo:hi, None].to_broadcast(
                            [TOK, hi - lo, HEADS]), ALU.add)
                    else:
                        ins = nc.vector.tensor_copy(o, s)
                link(L, n, ins)
                link(L, n, nc.vector.tensor_reduce(L["mx"][:], L["sc"][:].rearrange("p (k h) -> p h k", h=HEADS),
                                                   AX.X, ALU.max))
                s = L["sc"][:].rearrange("p (k h) -> p k h", h=HEADS)
                nc.vector.tensor_tensor(s, s, L["mx"][:, None, :].to_broadcast([TOK, SEQ, HEADS]), ALU.subtract)\
                    .then_inc(L["s_shifted"], 1)

            def normalise(L, n):
                dve.wait_ge(L["s_exped"], L["at"] + n + 1)
                p = L["pr"][:].rearrange("p (h k) -> p h k", h=HEADS)
                link(L, n, nc.vector.tensor_reduce(L["sm"][:], p, AX.X, ALU.add))
                link(L, n, nc.vector.reciprocal(L["sm"][:], L["sm"][:]))
                nc.vector.tensor_tensor(p, p, L["sm"][:, :, None].to_broadcast([TOK, HEADS, SEQ]), ALU.mult)\
                    .then_inc(L["s_probs"], 1)

            def rel_post(n):
                dve.wait_ge(a1["s_o_psum"], n + 1)
                dve.wait_ge(a1["s_bias_in"], n + 1)
                link(a1, n, nc.vector.tensor_tensor(a1["work"][:], a1["b"][3][0:TOK, 0:E], a1["res"][:], ALU.add))
                link(a1, n, nc.vector.bn_stats(a1["st2"][:], a1["work"][:]))
                carry_dve()
                nc.vector.bn_aggr(a1["mv2"][:], a1["st2"][:]).then_inc(a1["s_stat2"], 1)
                dve.wait_ge(a1["s_rstd2"], n + 1)
                link(a1, n, normed(a1["work2"][:], a1["work"][:], a1["mv2"][:, 0:1], a1["rs2"][:, 0:1]))
                link(a1, n, nc.vector.tensor_tensor(a1["work2"][:], a1["work2"][:], row("a_g"), ALU.mult))
                nc.vector.tensor_tensor(of_group(H, n), a1["work2"][:], a1["hold"][:], ALU.add).then_inc(a1["s_done"], 1)
                end_links(a1)

            def causal_post(n):
                dve.wait_ge(a2["s_o_psum"], n + 1)
                dve.wait_ge(a2["s_bias_in"], n + 1)
                link(a2, n, nc.vector.tensor_tensor(a2["work"][:], a2["b"][3][0:TOK, 0:E], a2["hold"][:], ALU.add))

            def gqa_pre(n, first=False):
                dve.wait_ge(ln["s_done"], n + 1)
                link(a3, n, nc.vector.bn_stats(a3["st"][:], of_group(H, n)))
                carry_dve()
                nc.vector.bn_aggr(a3["mv"][:], a3["st"][:]).then_inc(a3["s_stat"], 1)
                dve.wait_ge(a3["s_rstd"], a3["at"] + n + 1)
                normed(a3["xin"][:], of_group(H, n), a3["mv"][:, 0:1], a3["rs"][:, 0:1]).then_inc(a3["s_xin"], 1)

            def logits_in(n, s_in, s_done_, src, bias):
                dve.wait_ge(s_in, n + 1)
                dst = LOGITS[:].rearrange("p g e -> p (g e)")[:, bass.ds(n * EXPERTS, EXPERTS)]
                if bias:
                    nc.vector.tensor_tensor(dst, src[0:TOK, 0:EXPERTS], br0[:], ALU.add).then_inc(s_done_, 1)
                else:
                    nc.vector.tensor_copy(dst, src[0:TOK, 0:EXPERTS]).then_inc(s_done_, 1)

            def causal_norm(n, first=False):
                link(a2, n, nc.vector.bn_stats(a2["st2"][:], a2["work"][:]))
                carry_dve()
                nc.vector.bn_aggr(a2["mv2"][:], a2["st2"][:]).then_inc(a2["s_stat2"], 1)
                nc.vector.tensor_tensor(of_group(H, n), of_group(H, n), a2["work"][:], ALU.add).then_inc(a2["s_done"], 1)
                dve.wait_ge(a2["s_rstd2"], n + 1)
                if not first:
                    dve.wait_ge(s_rows, 32 * n)
                normed(a2["work2"][:], a2["work"][:], a2["mv2"][:, 0:1], a2["rs2"][:, 0:1]).then_inc(a2["s_in2"], 1)
                end_links(a2)

            def gqa_post(n):
                dve.wait_ge(a3["s_o_psum"], a3["at"] + n + 1)
                dve.wait_ge(a3["s_bias_in"], a3["at"] + n + 1)
                link(a3, n, nc.vector.tensor_tensor(a3["work"][:], a3["b"][3][0:TOK, 0:E], a3["hold"][:], ALU.add))
                link(a3, n, nc.vector.bn_stats(a3["st2"][:], a3["work"][:]))
                carry_dve()
                link(a3, n, nc.vector.bn_aggr(a3["mv2"][:], a3["st2"][:]))
                nc.vector.scalar_tensor_tensor(a3["va2"][:], a3["mv2"][:, 0:1], a3["mv2"][:, 0:1], a3["mv2"][:, 1:2],
                                               ALU.mult, ALU.add).then_inc(a3["s_stat2"], 1)
                dve.wait_ge(a3["s_rstd2"], a3["at"] + n + 1)
                dve.wait_ge(s_rows, 32 * (GROUPS + n))
                nc.vector.scalar_tensor_tensor(a3["work2"][:], a3["work"][:], a3["rs2"][:, 0:1], row("g_n1"),
                                               ALU.mult, ALU.mult).then_inc(a3["s_in2"], 1)
                end_links(a3)

            dve.wait_ge(s_const, 16 * N_LOADS)
            rel_pre(0, True)
            keys(a1, 0)
            values(a1, 0)
            dve.wait_ge(s_relsum, 1)
            shift(a1, 0, "rel")
            normalise(a1, 0)
            rel_post(0)
            with dve.Fori(1, GROUPS) as n:
                m = n - 1
                rel_pre(n)
                causal_pre(m)
                keys(a2, m)
                values(a2, m)
                keys(a1, n)
                values(a1, n)
                shift(a2, m, "causal")
                normalise(a2, m)
                dve.wait_ge(s_relsum, n + 1)
                shift(a1, n, "rel")
                normalise(a1, n)
                causal_post(m)
                causal_norm(m)
                logits_in(m, s_log, s_lg, a2["b"][1], True)
                rel_post(n)
            m = GROUPS - 1
            causal_pre(m)
            keys(a2, m)
            values(a2, m)
            shift(a2, m, "causal")
            normalise(a2, m)
            causal_post(m)
            causal_norm(m)
            logits_in(m, s_log, s_lg, a2["b"][1], True)

            moe_links = [0]
            chosen, prefix = tmp8[1], tmp8[2]

            def mlink(ins):
                moe_links[0] += 1
                ins.then_inc(s_links, 1)
                dve.wait_ge(s_links, moe_links[0])

            def wide1(x):
                return x[:, :, None].to_broadcast([TOK, GROUPS, EXPERTS])

            dve.wait_ge(s_lg, GROUPS)
            for g in range(GROUPS):
                last = nc.vector.max(top8[:, g, :], LOGITS[:, g, :])
            mlink(last)
            nc.vector.tensor_tensor(tmp8[0][:], LOGITS[:], top8[:, :, 0:1].to_broadcast([TOK, GROUPS, EXPERTS]),
                                    ALU.subtract).then_inc(s_shifted0, 1)
            mlink(nc.vector.tensor_tensor(tmp8[4][:], LOGITS[:],
                                              top8[:, :, 1:2].to_broadcast([TOK, GROUPS, EXPERTS]), ALU.is_ge))
            dve.wait_ge(m0["s_exp"], 1)
            mlink(nc.vector.tensor_tensor(tmp8[3][:], tmp8[1][:], tmp8[4][:], ALU.mult))
            mlink(nc.vector.tensor_copy(chosen[:], tmp8[4][:]))
            mlink(nc.vector.tensor_reduce(tmp1[0][:], tmp8[3][:], AX.X, ALU.add))
            mlink(nc.vector.reciprocal(tmp1[0][:], tmp1[0][:]))
            mlink(nc.vector.tensor_tensor(GATE[:], tmp8[3][:], wide1(tmp1[0]), ALU.mult))

            def entries(link_, k):
                link_(nc.vector.scalar_tensor_tensor(picked[:], order[:], float(k), tmp8[4][:], ALU.is_equal, ALU.mult))
                link_(nc.vector.tensor_tensor(tmp8[3][:], picked[:], tmp8[5][:], ALU.mult))
                link_(nc.vector.tensor_reduce(tmp1[0][:], tmp8[3][:], AX.X, ALU.add))
                link_(nc.vector.tensor_scalar(slot[:, k, :], tmp1[0][:], float(FAR), None, ALU.add))
                link_(nc.vector.tensor_tensor(picked[:], picked[:], GATE[:], ALU.mult))
                return nc.vector.tensor_reduce(entry[:, k, :, 1], picked[:], AX.X, ALU.add)

            def route(M):
                i_ = M["i"]

                def lk(ins):
                    mlink(ins)

                lk(nc.vector.tensor_scalar(chosen[:, GROUPS - 1, :], chosen[:, GROUPS - 1, :], real[:, 0:1], None, ALU.mult))
                lk(nc.vector.memset(prefix[:, 0, :], 0.0))
                for g in range(1, GROUPS):
                    ins = nc.vector.tensor_tensor(prefix[:, g, :], prefix[:, g - 1, :], chosen[:, g - 1, :], ALU.add)
                    if g < GROUPS - 1:
                        lk(ins)
                ins.then_inc(M["s_chosen"], 1)
                dve.wait_ge(M["s_chosen"], 1)
                lk(nc.vector.memset(order[:, :, 0:1], 0.0))
                for e in range(1, EXPERTS):
                    lk(nc.vector.tensor_tensor(order[:, :, e:e + 1], order[:, :, e - 1:e], chosen[:, :, e - 1:e], ALU.add))
                dve.wait_ge(M["s_rank_psum"], 1)
                n = GROUPS * EXPERTS
                rank = bank[0][0:TOK, 0:n].rearrange("p (g e) -> p g e", e=EXPERTS)
                lk(nc.vector.tensor_tensor(tmp8[5][:], rank,
                                           slot_base[:, i_, None, :].to_broadcast([TOK, GROUPS, EXPERTS]), ALU.add))
                if M is m1:
                    lk(nc.vector.scalar_tensor_tensor(tmp8[4][:], rank, float(CAPACITY), chosen[:], ALU.is_lt, ALU.mult))
                else:
                    lk(nc.vector.tensor_copy(tmp8[4][:], chosen[:]))
                for k in range(2):
                    ins = entries(lk, k)
                    if k == 0:
                        lk(ins)
                ins.then_inc(M["s_entries"], 1)
                whole = M["tiles"] - 1
                count = bank[0][0:1, n:n + EXPERTS]
                tiles, at, last = (plan_f[0:1, i_, j, :] for j in range(3))
                lk(nc.vector.tensor_tensor(over[:, :, 0:whole], count[:, :, None].to_broadcast([1, EXPERTS, whole]),
                                           fulls[:, None, 0:whole].to_broadcast([1, EXPERTS, whole]), ALU.is_gt))
                lk(nc.vector.tensor_reduce(tiles[:, 0:EXPERTS], over[:, :, 0:whole], AX.X, ALU.add))
                lk(nc.vector.scalar_tensor_tensor(last[:, 1:EXPERTS + 1], tiles[:, 0:EXPERTS], float(TILE),
                                                  row_step[:, i_, :], ALU.mult, ALU.add))
                lk(nc.vector.tensor_scalar(tiles[:, 0:EXPERTS], tiles[:, 0:EXPERTS], 1.0, None, ALU.add))
                lk(nc.vector.memset(tiles[:, EXPERTS:EXPERTS + 1], 0.0))
                lk(nc.vector.memset(last[:, 0:1], 0.0))
                lk(nc.vector.memset(at[:, 0:1], 0.0))
                if M is m0:
                    lk(nc.vector.tensor_reduce(ties_f[:], count, AX.X, ALU.add))
                    lk(nc.vector.tensor_scalar(ties[:], ties_f[:], -2.0 * IMAGES * SEQ, None, ALU.add))
                for e in range(EXPERTS):
                    lk(nc.vector.tensor_tensor(at[:, e + 1:e + 2], at[:, e:e + 1], tiles[:, e:e + 1], ALU.add))
                nc.vector.tensor_copy(plan[0:1, i_, :, :], plan_f[0:1, i_, :, :]).then_inc(M["s_plan"], 1)
                dve.wait_ge(M["s_plan"], 1)
                if M is m0:
                    links = [0]

                    def tie_link(ins):
                        links[0] += 1
                        ins.then_inc(s_tie_links, 1)
                        dve.wait_ge(s_tie_links, links[0])

                    more = dve.value_load(ties[0:1, 0:1], min_val=0, max_val=EXPERTS * IMAGES * SEQ)
                    with dve.If(more > 0):
                        for k in range(2, EXPERTS):
                            ins = entries(tie_link, k)
                            if k < EXPERTS - 1:
                                tie_link(ins)
                        ins.then_inc(s_tie_entries, 1)
                        dve.wait_ge(s_tie_entries, 1)
                    dve.nop()

            def weigh(M, bias):
                def out_of(u, b):
                    dve.wait_ge(M["s_down"], u + 1)
                    dve.wait_ge(M["s_out_list"], 16 * u)
                    src = bank[5][:, 0:E]
                    if bias:
                        nc.vector.tensor_tensor(y_sum[:], src, b_dn[b][:], ALU.add).then_inc(s_y_sum, 1)
                        dve.wait_ge(s_y_sum, u)
                        src = y_sum[:]
                    nc.vector.tensor_scalar(y_rows[:], src, out_list[:, 1:2], None, ALU.mult).then_inc(M["s_y"], 1)

                def tile(i, b, e, t, u):
                    start = isinstance(t, int) and t == 0
                    after_first(dve, i, b, t, lambda: out_of(u, 1 - b if start else b))
                    if start and bias:
                        dve.wait_ge(s_weights[b], weights_there(M, i))
                        carry_dve()

                dve.sem_inc(M["s_y"], 1)
                walk(dve, M, tile)
                out_of(tiles_so_far(dve, M), 1)

            route(m0)
            weigh(m0, True)
            dve.wait_ge(s_back[0], 16)
            dve.wait_ge(s_back[1], 16)

            def cos_pre(n, first=False):
                if not first:
                    dve.wait_ge(ln["s_done"], n)
                nc.vector.bn_stats(ln["st"][:], of_group(H, n)).then_inc(ln["s_dve"], 1)
                dve.wait_ge(ln["s_dve"], n * LN_LINKS + 1)
                carry_dve()
                nc.vector.bn_aggr(ln["mv"][:], ln["st"][:]).then_inc(ln["s_stat"], 1)
                dve.wait_ge(ln["s_rstd"], n + 1)
                normed(ln["xin"][:], of_group(H, n), ln["mv"][:, 0:1], ln["rs"][:, 0:1]).then_inc(ln["s_xin"], 1)

            def cos_qkv(n):
                dve.wait_ge(ln["s_qkv_psum"], n + 1)
                for i, b in enumerate(("l_bq", "l_bk", "l_bv")):
                    last = nc.vector.tensor_tensor(ln["q"][:, i, :], ln["b"][1 + i][0:TOK, 0:E], row(b), ALU.add)
                last.then_inc(ln["s_qkv"], 1)
                dve.wait_ge(ln["s_squares"], n + 1)
                nc.vector.tensor_reduce(ln["ss"][:], ln["sq"][:].rearrange("p i (h d) -> p i h d", h=HEADS), AX.X, ALU.add)\
                    .then_inc(ln["s_norm2"], 1)

            def cos_norm(n):
                dve.wait_ge(ln["s_norm"], n + 1)
                nc.vector.tensor_scalar(ln["ri"][:], ln["ss"][:], EPS_A, None, ALU.max).then_inc(ln["s_dve"], 1)
                dve.wait_ge(ln["s_dve"], n * LN_LINKS + 2)
                nc.vector.reciprocal(ln["ri"][:], ln["ri"][:]).then_inc(ln["s_dve"], 1)
                dve.wait_ge(ln["s_dve"], n * LN_LINKS + 3)
                qk = ln["q"][:, 0:2, :].rearrange("p i (h d) -> p i h d", h=HEADS)
                nc.vector.tensor_tensor(qk, qk, ln["ri"][:, :, :, None].to_broadcast([TOK, 2, HEADS, HD]), ALU.mult)\
                    .then_inc(ln["s_qn"], 1)
                dve.wait_ge(ln["s_qn"], n + 1)
                nc.vector.tensor_tensor(ln["km"][:], ln["q"][:, 1:2, :].to_broadcast([TOK, PER, E]),
                                        of_image[:, :, None].to_broadcast([TOK, PER, E]), ALU.mult)\
                    .then_inc(ln["s_km"], 1)

            def cos_kv(n):
                dve.wait_ge(ln["s_kv_psum"], n + 1)
                for c in range(CT):
                    last = nc.vector.scalar_tensor_tensor(
                        ln["kv"][:, c, :, :], ln["b"][1 + c][:, 0:PER * 128].rearrange("p (j d) -> p j d", j=PER),
                        inv_scale[:, 1, c:c + 1], same_head[:, None, :].to_broadcast([128, PER, 128]),
                        ALU.mult, ALU.mult)
                last.then_inc(ln["s_kv"], 1)

            def cos_post(n):
                dve.wait_ge(ln["s_o_psum"], n + 1)
                dve.wait_ge(ln["s_bias_in"], n + 1)
                nc.vector.tensor_tensor(of_group(H, n), ln["b"][0][0:TOK, 0:E], ln["hold"][:], ALU.add).then_inc(ln["s_done"], 1)

            dve.wait_ge(s_scale2, 1)
            cos_pre(0, True)
            cos_qkv(0)
            cos_norm(0)
            cos_kv(0)
            cos_post(0)

            with dve.Fori(1, GROUPS) as n:
                m = n - 1
                gqa_pre(m)
                cos_pre(n)
                keys(a3, m)
                cos_qkv(n)
                values(a3, m)
                cos_norm(n)
                shift(a3, m, "none")
                cos_kv(n)
                normalise(a3, m)
                cos_post(n)
                gqa_post(m)
                logits_in(m, s_glog, s_glg, a3["b"][1], False)
            m = GROUPS - 1
            gqa_pre(m)
            keys(a3, m)
            values(a3, m)
            shift(a3, m, "none")
            normalise(a3, m)
            gqa_post(m)
            logits_in(m, s_glog, s_glg, a3["b"][1], False)

            p, left, first, eq, score = tmp8[0], tmp8[3], tmp8[4], tmp8[5], tmp8[2]
            dve.wait_ge(m1["s_exp"], 1)
            rev = rev8[:, None, :].to_broadcast([TOK, GROUPS, EXPERTS])

            def pick(src, out):
                mlink(nc.vector.tensor_reduce(tmp1[0][:], src[:], AX.X, ALU.max))
                mlink(nc.vector.tensor_tensor(eq[:], src[:], wide1(tmp1[0]), ALU.is_ge))
                mlink(nc.vector.tensor_tensor(score[:], eq[:], rev, ALU.mult))
                mlink(nc.vector.tensor_reduce(tmp1[1][:], score[:], AX.X, ALU.max))
                mlink(nc.vector.tensor_tensor(out[:], score[:], wide1(tmp1[1]), ALU.is_equal))

            pick(p, first)
            mlink(nc.vector.scalar_tensor_tensor(left[:], first[:], -2.0, p[:], ALU.mult, ALU.add))
            pick(left, chosen)
            mlink(nc.vector.tensor_tensor(chosen[:], chosen[:], first[:], ALU.add))
            mlink(nc.vector.tensor_tensor(left[:], p[:], chosen[:], ALU.mult))
            mlink(nc.vector.tensor_reduce(tmp1[0][:], left[:], AX.X, ALU.add))
            mlink(nc.vector.tensor_scalar(tmp1[0][:], tmp1[0][:], EPS_R, None, ALU.add))
            mlink(nc.vector.reciprocal(tmp1[1][:], tmp1[0][:]))
            mlink(nc.vector.tensor_tensor(GATE[:], left[:], wide1(tmp1[1]), ALU.mult))
            route(m1)
            weigh(m1, False)

            dve.wait_ge(s_back[0], 32)
            for g in range(GROUPS):
                last = nc.vector.bn_stats(fin["st"][:, g, :], SRC[:, g * E:(g + 1) * E])
            mlink(last)
            for g in range(GROUPS):
                last = nc.vector.bn_aggr(fin["mv"][:, g, :], fin["st"][:, g, :])
            mlink(last)
            mlink(nc.vector.tensor_tensor(fin["va"][:], fin["mv"][:, :, 0], fin["mv"][:, :, 0], ALU.mult))
            nc.vector.tensor_tensor(fin["va"][:], fin["va"][:], fin["mv"][:, :, 1], ALU.add).then_inc(s_fin_stat, 1)
            dve.wait_ge(s_fin_rstd, 1)
            for g in range(GROUPS):
                s = SRC[:, g * E:(g + 1) * E]
                nc.vector.scalar_tensor_tensor(s, s, fin["rs"][:, g:g + 1], row("g_n2"), ALU.mult, ALU.mult)\
                    .then_inc(s_links, 1)
            for g in range(GROUPS):
                h = H[:, g * E:(g + 1) * E]
                dve.wait_ge(s_links, moe_links[0] + g + 1)
                nc.vector.tensor_tensor(h, h, SRC[:, g * E:(g + 1) * E], ALU.add).then_inc(s_fin, 1)

        @block.gpsimd
        def _(pool):
            link_no = {}

            def link(L, n, ins):
                k = link_no[L["tag"]] = link_no.get(L["tag"], 0) + 1
                ins.then_inc(L["s_pool"], 1)
                pool.wait_ge(L["s_pool"], L["pool_at"] + n * POOL_LINKS[L["tag"]] + k)

            def end_links(L):
                assert link_no[L["tag"]] == POOL_LINKS[L["tag"]], (L["tag"], link_no[L["tag"]])
                link_no[L["tag"]] = 0

            def pow_half(out, x):
                return nc.gpsimd.tensor_tensor(out, x, half[:, 0:1], ALU.pow)

            def rel_rstd(n):
                pool.wait_ge(a1["s_stat"], n + 1)
                link(a1, n, nc.gpsimd.tensor_tensor(a1["va"][:, 0:1], a1["mv"][:, 1:2], eps[:, 0:1], ALU.add))
                pow_half(a1["rs"][:, 0:1], a1["va"][:, 0:1]).then_inc(a1["s_rstd"], 1)
                pool.wait_ge(a1["s_xin"], n + 1)
                nc.gpsimd.tensor_tensor(a1["res"][:], a1["xin"][:], row("a_bo"), ALU.add)
                nc.gpsimd.tensor_tensor(a1["hold"][:], a1["hold"][:], row("a_b"), ALU.add).then_inc(a1["s_bias_in"], 1)

            def triple(L, n):
                pool.wait_ge(L["s_xT"], L["at"] + n + 1)
                carry_pool()
                nc.gpsimd.tensor_copy(
                    L["x3"].rearrange("p c j (r k) -> p (c j) r k", r=HPC),
                    L["xT"][:].rearrange("p c (j k) -> p (c j) k", j=PER)[:, :, None, :]
                    .to_broadcast([128, CT * PER, HPC, SEQ])).then_inc(L["s_x3"], 1)

            def spread_queries(L, n):
                pool.wait_ge(L["s_qT"], L["at"] + n + 1)
                carry_pool()
                for j in range(PER):
                    last = nc.gpsimd.tensor_copy(L["qM"][:, :, j, j * SEQ:(j + 1) * SEQ],
                                                 L["qT"][:, :, j * SEQ:(j + 1) * SEQ])
                last.then_inc(L["s_qM"], 1)

            def rel_sum(n):
                pool.wait_ge(s_rel_in, 96 * (n + 1))
                nc.gpsimd.tensor_tensor(relb[:, 0, :], relb[:, 0, :], relb[:, 1, :], ALU.add).then_inc(s_relsum, 1)

            def rel_rstd2(n):
                pool.wait_ge(a1["s_stat2"], n + 1)
                link(a1, n, nc.gpsimd.tensor_tensor(a1["va2"][:], a1["mv2"][:, 1:2], eps[:, 1:2], ALU.add))
                pow_half(a1["rs2"][:], a1["va2"][:]).then_inc(a1["s_rstd2"], 1)

            def causal_rstd(n):
                pool.wait_ge(a2["s_stat"], n + 1)
                nc.gpsimd.tensor_tensor(a2["va"][:, 0:1], a2["mv"][:, 1:2], eps[:, 0:1], ALU.add)
                link(a2, n, nc.gpsimd.tensor_scalar(a2["va"][:, 1:2], a2["mv"][:, 1:2], 1.0 + EPS, EPS * EPS,
                                                    ALU.mult, ALU.add))
                nc.gpsimd.tensor_tensor(a2["rs"][:], a2["va"][:], half[:, 0:1].to_broadcast([TOK, 2]), ALU.pow)\
                    .then_inc(a2["s_rstd"], 1)
                pool.wait_ge(a2["s_xin"], n + 1)
                nc.gpsimd.tensor_tensor(a2["hold"][:], a2["res"][:], row("f_bo"), ALU.add).then_inc(a2["s_bias_in"], 1)

            def causal_rstd2(n):
                pool.wait_ge(a2["s_stat2"], n + 1)
                link(a2, n, nc.gpsimd.tensor_tensor(a2["va2"][:], a2["mv2"][:, 1:2], eps[:, 0:1], ALU.add))
                pow_half(a2["rs2"][:], a2["va2"][:]).then_inc(a2["s_rstd2"], 1)

            def add_rows(M):
                i_ = M["i"]

                def list_tokens(k, done):
                    for g in range(GROUPS):
                        pool.indirect_dma_start(
                            out=LIST_dram[i_], out_offset=bass.IndirectOffsetOnAxis(ap=slot[:, k, g:g + 1], axis=0),
                            in_=entry[:, k, g, :], in_offset=None, bounds_check=EXPERTS * M["slots"] - 1,
                            oob_is_err=False).then_inc(done, 16)

                pool.wait_ge(s_init, 16 * 2)
                def wait_alone():
                    pool.sem_inc(s_idle, 1)

                pool.wait_ge(m0["s_added"], 16)
                pool.wait_ge(m1["s_added"], 16)
                pool.wait_ge(M["s_entries"], 1)
                for k in range(2):
                    list_tokens(k, M["s_listed"])
                pool.wait_ge(M["s_plan"], 1)
                if M is m0:
                    more = pool.value_load(ties[0:1, 0:1], min_val=0, max_val=EXPERTS * IMAGES * SEQ)
                    with pool.If(more > 0):
                        pool.wait_ge(s_tie_entries, 1)
                        for k in range(2, EXPERTS):
                            list_tokens(k, s_tie_listed)
                    pool.nop()
                pool.wait_ge(s_rows, 32 * GROUPS * (i_ + 1))

                def out_of(u):
                    pool.wait_ge(M["s_y"], u + 1)
                    wait_alone()
                    pool.indirect_dma_start(
                        out=SUM_dram, out_offset=bass.IndirectOffsetOnAxis(ap=out_list[:, 0:1].bitcast(U32), axis=0),
                        in_=y_rows[:], in_offset=None, compute_op=ALU.add, bounds_check=GROUPS * TOK + TILE - 1,
                        oob_is_err=True).then_inc(M["s_added"], 16)

                def tile(i, b, e, t, u):
                    pool.wait_ge(M["s_in_list"], 16 * (u + 1))
                    wait_alone()
                    pool.wait_ge(M["s_xT_psum"], u + 1)
                    wait_alone()
                    pool.indirect_dma_start(
                        out=x_rows[:], out_offset=None, in_=X_dram,
                        in_offset=bass.IndirectOffsetOnAxis(ap=in_list[:, 0:1].bitcast(U32), axis=0))\
                        .then_inc(M["s_x_rows"], 16)
                    after_first(pool, i, b, t, lambda: out_of(u))

                walk(pool, M, tile)
                out_of(tiles_so_far(pool, M))

            pool.dma_start(X_dram[GROUPS * TOK:], A["c_spare"]).then_inc(m0["s_added"], 16)
            pool.dma_start(SUM_dram[GROUPS * TOK:], A["c_spare"]).then_inc(m1["s_added"], 16)
            nc.gpsimd.memset(half[:], -0.5)
            for i, value in enumerate((EPS, EPS_A, EPS_R)):
                nc.gpsimd.memset(eps[:, i:i + 1], value)
            nc.gpsimd.memset(ones[:], 1.0)
            nc.gpsimd.memset(a2["qM"][:], 0.0)
            nc.gpsimd.memset(a1["qM"][:], 0.0).then_inc(s_zeroed, 1)
            pool.wait_ge(s_zeroed, 1)
            pool.wait_ge(s_const, 16 * N_LOADS)
            rel_rstd(0)
            triple(a1, 0)
            spread_queries(a1, 0)
            rel_sum(0)
            rel_rstd2(0)
            end_links(a1)
            with pool.Fori(1, GROUPS) as n:
                m = n - 1
                rel_rstd(n)
                causal_rstd(m)
                triple(a2, m)
                spread_queries(a2, m)
                triple(a1, n)
                spread_queries(a1, n)
                rel_sum(n)
                causal_rstd2(m)
                rel_rstd2(n)
                end_links(a1)
                end_links(a2)
            m = GROUPS - 1
            causal_rstd(m)
            triple(a2, m)
            spread_queries(a2, m)
            causal_rstd2(m)
            add_rows(m0)

            def cos_rstd(n):
                pool.wait_ge(ln["s_stat"], n + 1)
                nc.gpsimd.tensor_tensor(ln["va"][:], ln["mv"][:, 1:2], eps[:, 0:1], ALU.add).then_inc(ln["s_pool"], 1)
                pool.wait_ge(ln["s_pool"], n + 1)
                pow_half(ln["rs"][:], ln["va"][:]).then_inc(ln["s_rstd"], 1)
                nc.gpsimd.tensor_tensor(ln["hold"][:], of_group(H, n), row("l_bo"), ALU.add).then_inc(ln["s_bias_in"], 1)

            def cos_squares(n):
                pool.wait_ge(ln["s_qkv"], n + 1)
                nc.gpsimd.tensor_tensor(ln["sq"][:], ln["q"][:, 0:2, :], ln["q"][:, 0:2, :], ALU.mult).then_inc(ln["s_squares"], 1)

            def gqa_rstd(n):
                pool.wait_ge(a3["s_stat"], a3["at"] + n + 1)
                link(a3, n, nc.gpsimd.tensor_tensor(a3["va"][:, 0:1], a3["mv"][:, 1:2], eps[:, 0:1], ALU.add))
                pow_half(a3["rs"][:, 0:1], a3["va"][:, 0:1]).then_inc(a3["s_rstd"], 1)
                pool.wait_ge(a3["s_xin"], a3["at"] + n + 1)
                nc.gpsimd.tensor_tensor(a3["hold"][:], a3["xin"][:], row("g_ob"), ALU.add).then_inc(a3["s_bias_in"], 1)

            def gqa_rstd2(n):
                pool.wait_ge(a3["s_stat2"], a3["at"] + n + 1)
                link(a3, n, nc.gpsimd.tensor_tensor(a3["rs"][:, 1:2], a3["va2"][:], eps[:, 2:3], ALU.add))
                pow_half(a3["rs2"][:], a3["rs"][:, 1:2]).then_inc(a3["s_rstd2"], 1)

            cos_rstd(0)
            cos_squares(0)
            with pool.Fori(1, GROUPS) as n:
                m = n - 1
                gqa_rstd(m)
                cos_rstd(n)
                triple(a3, m)
                spread_queries(a3, m)
                cos_squares(n)
                gqa_rstd2(m)
                end_links(a3)
            m = GROUPS - 1
            gqa_rstd(m)
            triple(a3, m)
            spread_queries(a3, m)
            gqa_rstd2(m)
            add_rows(m1)
            pool.wait_ge(s_fin_stat, 1)
            nc.gpsimd.tensor_scalar(fin["va"][:], fin["va"][:], EPS_R, None, ALU.add).then_inc(s_fin_pool, 1)
            pool.wait_ge(s_fin_pool, 1)
            nc.gpsimd.tensor_tensor(fin["rs"][:], fin["va"][:], half[:, 0:1].to_broadcast([TOK, GROUPS]), ALU.pow)\
                .then_inc(s_fin_rstd, 1)


def _by_tile(w):
    return w.reshape(w.shape[0] // 128, 128, -1).transpose(1, 0, 2)


def _layout(i):
    f = np.float32
    a = {}
    x = i["x"].reshape(IMAGES, 3, SIDE, PATCH, SIDE, PATCH).transpose(1, 3, 5, 0, 2, 4)
    x = x.reshape(PK * 128, IMAGES, SIDE * SIDE)
    xt = np.zeros((PK * 128, GROUPS * PER, SEQ), f)
    xt[:, :IMAGES, 1:] = x
    a["xT"] = np.ascontiguousarray(xt.reshape(PK, 128, GROUPS, TOK).transpose(2, 1, 0, 3))
    base = np.empty((PER, SEQ, E), f)
    base[:, 0] = i["cls_tok"].reshape(E)
    base[:, 1:] = i["L0_tok_b"]
    a["base"] = base.reshape(TOK, E)
    a["wtok"] = _by_tile(i["L0_tok_W"])
    per_kv = HEADS // (i["L1_ffn_kw"].shape[1] // HD)

    def spread(w):
        return np.repeat(w.reshape(w.shape[:-1] + (-1, HD)), per_kv, axis=-2).reshape(w.shape[:-1] + (E,))

    mats = {f"{p}_W{w}": i[f"{l}_W{w}"] for p, l in (("a", "L0_attn"), ("f", "L0_ffn"), ("l", "L1_attn"))
            for w in "qkvo"}
    mats |= {"g_Wq": i["L1_ffn_qw"], "g_Wk": spread(i["L1_ffn_kw"]), "g_Wv": spread(i["L1_ffn_vw"]),
             "g_Wo": i["L1_ffn_ow"]}
    a["mats"] = np.stack([_by_tile(mats[n]) for n in MATS], 1)
    rows = {"a_bo": i["L0_attn_bo"], "a_g": i["L0_attn_ln_gamma"], "a_b": i["L0_attn_ln_beta"],
            "f_bo": i["L0_ffn_bo"], "l_bq": i["L1_attn_bq"], "l_bk": i["L1_attn_bk"], "l_bv": i["L1_attn_bv"],
            "l_bo": i["L1_attn_bo"], "g_ob": i["L1_ffn_ob"], "g_n1": i["L1_ffn_norm1_w"],
            "g_n2": i["L1_ffn_norm2_w"]}
    a["rows"] = np.stack([rows[n] for n in ROWS])
    cols = {f"{p}_b{w}": i[f"{l}_b{w}"] for p, l in (("a", "L0_attn"), ("f", "L0_ffn")) for w in "qkv"}
    cols |= {"f_g1": i["L0_ffn_ln1_g"], "f_b1": i["L0_ffn_ln1_b"], "f_g2": i["L0_ffn_ln2_g"],
             "f_b2": i["L0_ffn_ln2_b"], "g_qb": i["L1_ffn_qb"], "g_kb": spread(i["L1_ffn_kb"]),
             "g_vb": spread(i["L1_ffn_vb"]), "l_m": np.repeat(i["L1_attn_m"], HD)}
    a["cols"] = np.stack([cols[n].reshape(CT, 128).T for n in COLS], 1)
    emb = i["L0_attn_dist_emb"]
    last = emb.shape[0] // 2
    near = emb[last - (SEQ - 1):last + SEQ]
    for n, t in (("relq", near[::-1]), ("relk", near)):
        wide = np.zeros((HC, HD, REL, HC), f)
        for h in range(HC):
            wide[h, :, :, h] = t.T
        a[n] = wide.reshape(128, REL, HC)
    a["wr0"], a["wr1"] = _by_tile(i["L0_ffn_Wr"]), _by_tile(i["L1_ffn_gate_w"])
    a["br0"] = i["L0_ffn_br"]
    a["eb1"] = i["L0_ffn_e_b1"].reshape(EXPERTS, F0 // 128, 128).transpose(0, 2, 1)
    a["eb2"] = i["L0_ffn_e_b2"]
    for n, w in (("e_w1", "L0_ffn_e_w1"), ("e_w2", "L0_ffn_e_w2"), ("g_w1", "L1_ffn_w1"), ("g_w2", "L1_ffn_w2")):
        w = i[w]
        a[n] = w.reshape(EXPERTS, w.shape[1] // 128, 128, -1).transpose(0, 2, 1, 3).reshape(EXPERTS, 128, -1)
    p, t = np.arange(128), np.arange(TOK)
    a["c_ident"] = np.eye(128, dtype=f)
    a["c_head_of_row"] = (p[:, None] // HD == np.arange(HC)).astype(f)
    a["c_third"] = (t[:, None] // SEQ == np.arange(HEADS) % HPC).astype(f)
    a["c_causal"] = np.where(np.arange(SEQ) > t[:, None] % SEQ, f(MASKED), f(0))
    a["c_of_image"] = (t[:, None] // SEQ == np.arange(PER)).astype(f)
    a["c_same_head"] = (p[:, None] // HD == p // HD).astype(f)
    a["c_before"] = (t[:, None] < t).astype(f)
    expert = np.arange(EXPERTS)
    a["c_row_step"] = np.stack([expert * n for n in SLOTS]).astype(f)[None]
    a["c_slot_base"] = np.broadcast_to(a["c_row_step"] - f(FAR), (TOK, 2, EXPERTS))
    a["c_real"] = (t[:, None] < LAST_REAL).astype(f)
    a["c_fulls"] = (np.arange(1, TILES[0]) * TILE).astype(f)[None]
    entry = np.zeros((TOK, EXPERTS, GROUPS, 2), np.int32)
    entry[..., 0] = t[:, None, None] + TOK * np.arange(GROUPS)
    a["c_entry"] = entry.view(f)
    for k, n in enumerate(SLOTS):
        empty = np.zeros((EXPERTS * n, 2), np.int32)
        empty[:, 0] = GROUPS * TOK + np.arange(EXPERTS * n) % TILE
        a[f"c_list{k}"] = empty.view(f)
    a["c_spare"] = np.zeros((TILE, E), f)
    a["c_rev8"] = np.broadcast_to((EXPERTS - np.arange(EXPERTS)).astype(f), (TOK, EXPERTS))
    return {n: np.ascontiguousarray(v) for n, v in a.items()}


def kernel(**inputs):
    import concourse.bacc as bacc
    from concourse.bass_utils import run_bass_kernel_spmd

    arrays = _layout({n: np.asarray(v) for n, v in inputs.items()})
    nc = bacc.Bacc("TRN2", target_bir_lowering=False, num_devices=1)
    A = {n: nc.dram_tensor("in_" + n, v.shape, mybir.dt.from_np(v.dtype), kind="ExternalInput").ap()
         for n, v in arrays.items()}
    A["out"] = nc.dram_tensor("out", (TOK, GROUPS * E), F32, kind="ExternalOutput").ap()
    build_tower(nc, A)
    r = run_bass_kernel_spmd(nc, [{"in_" + n: v for n, v in arrays.items()}], core_ids=[0])
    out = r.results[0]["out"].reshape(PER, SEQ, GROUPS, E).transpose(2, 0, 1, 3)
    return np.ascontiguousarray(out.reshape(GROUPS * PER, SEQ, E)[:IMAGES])
```

```python
from contextlib import ExitStack

import numpy as np

import concourse.bass as bass
from concourse import mybir

F32 = mybir.dt.float32
I32, U32 = mybir.dt.int32, mybir.dt.uint32
ALU = mybir.AluOpType
ACT = mybir.ActivationFunctionType
AX = mybir.AxisListType

IMAGES, PER = 32, 3
GROUPS = -(-IMAGES // PER)
PATCH, SIDE = 16, 6
SEQ = SIDE * SIDE + 1
TOK = PER * SEQ
E, HEADS, HD = 256, 16, 16
CT = E // 128
HC = HEADS // CT
PK = 3 * PATCH * PATCH // 128
K0, K1 = (SEQ + 1) // 2, SEQ // 2
HS = SEQ * HEADS
REL = 2 * SEQ - 1
REL_CUTS = (0, 25, 49, 73)
HPC = 3
CHUNKS = -(-HEADS // HPC)
EXPERTS = 8
F0, F1 = 1024, 512
CAPACITY = int(1.25 * IMAGES * SEQ * 2 / EXPERTS)
LAST_REAL = (IMAGES - (GROUPS - 1) * PER) * SEQ
TILE = 128
TILES = (-(-IMAGES * SEQ // TILE), -(-CAPACITY // TILE))
AHEAD = 4
BUFS = 3
SLOTS = tuple(n * TILE for n in TILES)
SPANS = ((0, 4), (4, 8), (8, 11))
PARTS = ((0, GROUPS - 1), (GROUPS - 1, GROUPS))
FAR = 2 ** 20
EPS, EPS_A, EPS_R = 1e-5, 1e-12, 1e-6
MASKED = -1e30

ROWS = ["a_bo", "a_g", "a_b", "f_bo", "l_bq", "l_bk", "l_bv", "l_bo", "g_ob", "g_n1", "g_n2"]
COLS = ["a_bq", "a_bk", "a_bv", "f_g1", "f_b1", "f_g2", "f_b2", "f_bq", "f_bk", "f_bv",
        "g_qb", "g_kb", "g_vb", "l_m"]
MATS = ["a_Wq", "a_Wk", "a_Wv", "a_Wo", "f_Wq", "f_Wk", "f_Wv", "f_Wo", "l_Wq", "l_Wk", "l_Wv",
        "l_Wo", "g_Wq", "g_Wk", "g_Wv", "g_Wo"]


def build_tower(nc, A):
    ctx = ExitStack()
    with ctx:
        def sb(name, shape, dtype=F32):
            return ctx.enter_context(nc.sbuf_tensor("sb_" + name, shape, dtype))

        def sem(name):
            return ctx.enter_context(nc.semaphore(name))

        bank = [ctx.enter_context(nc.psum_tensor(f"bank{i}", [128, 512], F32)) for i in range(8)]

        ident = sb("ident", [128, 128])
        head_of_row = sb("head_of_row", [128, HC])
        third_of_head = sb("third_of_head", [TOK, HEADS])
        causal = sb("causal", [TOK, SEQ])
        of_image = sb("of_image", [TOK, PER])
        same_head = sb("same_head", [128, 128])
        before = sb("before", [TOK, TOK])
        ones = sb("ones", [TOK, TOK])
        half = sb("half", [TOK, 1])
        idle = sb("idle", [1, 160])
        eps = sb("eps", [TOK, 3])
        rev8 = sb("rev8", [TOK, EXPERTS])
        slot_base = sb("slot_base", [TOK, 2, EXPERTS])
        real = sb("real", [TOK, 1])
        fulls = sb("fulls", [1, TILES[0] - 1])
        rows = sb("rows", [TOK, len(ROWS), E])
        cols = sb("cols", [128, len(COLS), CT])
        mats = sb("mats", [128, len(MATS), CT, E])
        wtok = sb("wtok", [128, PK, E])
        base = sb("base", [TOK, E])
        relq = sb("relq", [128, REL, HC])
        relk = sb("relk", [128, REL, HC])
        wr0 = sb("wr0", [128, CT, EXPERTS])
        wr1 = sb("wr1", [128, CT, EXPERTS])
        br0 = sb("br0", [TOK, EXPERTS])
        b_up = [sb(f"b_up{i}", [128, F0 // 128]) for i in range(BUFS)]
        b_dn = [sb(f"b_dn{i}", [TILE, E]) for i in range(BUFS)]
        inv_scale = sb("inv_scale", [128, 2, CT])

        def row(name):
            return rows[:, ROWS.index(name), :]

        def col(name, c):
            return cols[:, COLS.index(name), c:c + 1]

        def mat(name, c, lo=0, hi=E):
            return mats[:, MATS.index(name), c, lo:hi]

        H_all = sb("H", [128, GROUPS * E])
        H = H_all[0:TOK, :]
        SRC_all = sb("SRC", [128, GROUPS * E])
        SRC = SRC_all[0:TOK, :]
        LOGITS = sb("LOGITS", [TOK, GROUPS, EXPERTS])
        GATE = sb("GATE", [TOK, GROUPS, EXPERTS])
        slot = sb("slot", [TOK, EXPERTS, GROUPS], U32)
        entry = sb("entry", [TOK, EXPERTS, GROUPS, 2])
        plan_f = sb("plan_f", [1, 2, 3, EXPERTS + 1])
        plan = sb("plan", [1, 2, 3, EXPERTS + 1], I32)
        ties_f = sb("ties_f", [1, 1])
        ties = sb("ties", [1, 1], I32)
        over = sb("over", [1, EXPERTS, TILES[0] - 1])
        lists_in = sb("lists", [TILE, EXPERTS * TILES[0] * 2])
        list_now = [sb(f"list{i}", [TILE, TILES[0] * 2]) for i in range(BUFS)]
        out_row = sb("out_row", [TILE, 1])
        x_T = sb("x_T", [128, CT, TILE])
        w_up = [sb(f"w_up{i}", [128, CT * F0]) for i in range(2)]
        w_dn = [sb(f"w_dn{i}", [128, F0 // 128 * E]) for i in range(2)]
        up3, dn3 = (H_all, SRC_all[:, F1 * CT:]), (SRC_all, SRC_all)
        mid_flat = sb("mid", [128, 2 * REL * HEADS + 2 * HS])
        mid = mid_flat[:, 0:F0 // 128 * TILE].rearrange("p (f t) -> p f t", t=TILE)
        X_dram = nc.dram_tensor("X_dram", [GROUPS * TOK + TILE, E], F32, kind="Internal").ap()
        SUM_dram = nc.dram_tensor("SUM_dram", [GROUPS * TOK + TILE, E], F32, kind="Internal").ap()
        LIST_dram = [nc.dram_tensor(f"LIST_dram{i}", [EXPERTS * SLOTS[i], 2], F32, kind="Internal").ap()
                     for i in range(2)]
        rel_scratch = {n: nc.dram_tensor("scratch_" + n, [2, TOK, REL * HEADS], F32, kind="Internal").ap()
                       for n in ("q", "k")}

        def of_group(t, g, width=E):
            return t[:, bass.ds(g * width, width)]

        DVE_LINKS = {"rel": 10, "causal": 7, "gqa": 8}
        POOL_LINKS = {"rel": 2, "causal": 2, "gqa": 2}

        def attention(tag, banks, same_buffers=None):
            L = dict(tag=tag, b=banks, at=0, dve_at=0, pool_at=0)
            L["v2_psum"] = banks[3][0:TOK, 0:E]
            L["in_psum"] = (bank[6] if tag == "rel" else banks[0])[:, 0:CT * TOK]
            if same_buffers:
                L.update(same_buffers)
                L["tag"], L["at"], L["in_psum"] = tag, GROUPS, bank[0][:, E:E + CT * TOK]
                L["v2_psum"] = bank[3][0:TOK, 0:E]
                L["dve_at"], L["pool_at"] = (GROUPS * k[same_buffers["tag"]] for k in (DVE_LINKS, POOL_LINKS))
                return L
            for n, shape in dict(
                    xin=[TOK, E], h0=[TOK, E], res=[TOK, E], hold=[TOK, E], work=[TOK, E], work2=[TOK, E],
                    xT=[128, CT, TOK], qT=[128, CT, TOK], kT=[128, CT, TOK], qM=[128, CT, PER, TOK],
                    kB=[128, CT, TOK, HC], vB=[TOK, PER, E], sc=[TOK, HS], pr=[TOK, HS],
                    mx=[TOK, HEADS], sm=[TOK, HEADS], pT=[128, CHUNKS, TOK], cx=[SEQ, PER, E],
                    cT=[128, CT, TOK], st=[TOK, 6], mv=[TOK, 2], va=[TOK, 2], rs=[TOK, 2],
                    st2=[TOK, 6], mv2=[TOK, 2], va2=[TOK, 1], rs2=[TOK, 1]).items():
                L[n] = sb(f"{tag}_{n}", shape)
            L["x3"] = L["pT"][:].rearrange("p t q -> p (t q)").rearrange("p (c j r k) -> p c j (r k)", c=CT, j=PER, r=HPC)
            for n in ("x3", "xin", "xT_psum", "xT", "qk_psum", "v_psum", "qT", "kT", "qM", "kB", "vB", "s_psum",
                      "shifted", "exped", "probs", "pT_psum", "pT", "c_psum", "cx", "cT_psum", "cT", "o_psum",
                      "stat", "rstd", "stat2", "rstd2", "in2", "bias_in", "done", "dve", "pool"):
                if (tag, n) not in (("rel", "in2"), ("causal", "qT")):
                    L["s_" + n] = sem(f"{tag}_{n}")
            return L

        a1 = attention("rel", bank[0:4])
        a2 = attention("causal", bank[4:8])
        a3 = attention("gqa", bank[4:8], same_buffers=a2)
        tokens_psum = bank[0][0:TOK, 0:E]
        logits0_psum = bank[5][0:TOK, 0:EXPERTS]
        logits1_psum = bank[0][0:TOK, 480:480 + EXPERTS]
        s_zeroed = sem("s_zeroed")
        rows_flat = a1["kB"][:].rearrange("p c t h -> p (c t h)")
        x_rows = [[rows_flat[:, (2 * i + j) * E:(2 * i + j + 1) * E] for j in range(2)] for i in range(BUFS)]
        y_flat = a1["qM"][:].rearrange("p c j t -> p (c j t)")
        y_sum, y_rows = y_flat[:, 0:E], y_flat[:, E:2 * E]

        patches = SRC_all[:, 0:PK * TOK].rearrange("p (k t) -> p k t", t=TOK)
        qe = mid_flat[0:TOK, 0:2 * REL * HEADS].rearrange("p (i r) -> p i r", i=2)
        relb = mid_flat[0:TOK, 2 * REL * HEADS:2 * REL * HEADS + 2 * HS].rearrange("p (i r) -> p i r", i=2)
        nT = sb("nT", [128, CT, TOK])
        gT = sb("gT", [128, CT, TOK])

        ln = dict(b=bank[0:4])
        kb_flat = a1["kB"][:].rearrange("p c t h -> p (c t h)")
        ln.update(xin=a1["xin"], hold=a1["hold"], xT=a1["xT"], q=a1["vB"], qT=a1["qT"], cT=a1["cT"],
                           sq=a1["sc"][:, 0:2 * E].rearrange("p (i e) -> p i e", i=2),
                           km=kb_flat[0:TOK, 0:PER * E].rearrange("p (j e) -> p j e", j=PER),
                           kv=kb_flat[:, PER * E:2 * PER * E].rearrange("p (c j d) -> p c j d", c=CT, j=PER))
        for n, shape in dict(ss=[TOK, 2, HEADS], ri=[TOK, 2, HEADS], st=[TOK, 6], mv=[TOK, 2],
                             va=[TOK, 1], rs=[TOK, 1]).items():
            ln[n] = sb("cos_" + n, shape)
        for n in ("stat", "rstd", "xin", "xT_psum", "xT", "qkv_psum", "qkv", "squares", "norm2", "norm", "qn",
                  "km", "qT_psum", "qT", "kv_psum", "kv", "cT_psum", "cT", "o_psum", "bias_in", "done", "dve",
                  "pool"):
            ln["s_" + n] = sem("cos_" + n)
        LN_LINKS = 2

        s_wtok = sem("s_wtok")
        s_const = sem("s_const")
        s_rest = sem("s_rest")
        s_patch = sem("s_patch")
        s_tok = sem("s_tok")
        s_qe_psum = sem("s_qe_psum")
        s_qe = sem("s_qe")
        s_qe_out = [sem(f"s_qe_out{i}") for i in range(2)]
        s_rel_in = sem("s_rel_in")
        s_relsum = sem("s_relsum")
        s_nT_psum = sem("s_nT_psum")
        s_nT = sem("s_nT")
        s_log = sem("s_log")
        s_lg = sem("s_lg")
        s_scale = sem("s_scale")
        s_gT_psum = sem("s_gT_psum")
        s_gT = sem("s_gT")
        s_glog = sem("s_glog")
        s_glg = sem("s_glg")

        s_rows = sem("s_rows")
        s_idle = sem("s_idle")
        s_init = sem("s_init")
        s_list_now = sem("s_list_now")
        s_lists = sem("s_lists")
        s_weights = [sem(f"s_weights{i}") for i in range(BUFS)]
        s_back = [sem(f"s_back{i}") for i in range(2 + len(SPANS))]
        s_tie_links = sem("s_tie_links")
        TIE_LINKS = 6 * (EXPERTS - 2)
        s_tie_listed = sem("s_tie_listed")

        def mixture(i, width):
            M = dict(i=i, tag=f"moe{i}", width=width, nf=width // 128, tiles=TILES[i], slots=SLOTS[i])
            for n in ("exp", "chosen", "rank_psum", "plan", "entries", "listed", "up", "act",
                      "x_rows", "xT_psum", "x_T", "down", "y", "added"):
                M["s_" + n] = sem(f"moe{i}_{n}")
            return M

        m0, m1 = mixture(0, F0), mixture(1, F1)
        s_shifted0 = sem("s_shifted0")
        s_y_sum = sem("s_y_sum")
        s_links = sem("s_links")
        RING = 4
        tmp8 = [sb(f"tmp8_{i}", [TOK, GROUPS, EXPERTS]) for i in range(6)]
        order = sb("order", [TOK, GROUPS, EXPERTS])
        picked = sb("picked", [TOK, GROUPS, EXPERTS])
        tmp1 = [sb(f"tmp1_{i}", [TOK, GROUPS]) for i in range(3)]
        top8 = sb("top8", [TOK, GROUPS, 8])
        s_fin_stat = sem("s_fin_stat")
        s_fin_rstd = sem("s_fin_rstd")
        s_fin_rows = sem("s_fin_rows")
        s_fin = sem("s_fin")
        s_out = sem("s_out")
        fin = dict(st=sb("fin_st", [TOK, GROUPS, 6]), mv=sb("fin_mv", [TOK, GROUPS, 2]),
                              va=sb("fin_va", [TOK, GROUPS]), rs=sb("fin_rs", [TOK, GROUPS]))

        A_MATS, F_MATS = 4, 8
        rows_in = A["rows"].rearrange("r e -> (r e)").partition_broadcast(TOK)
        embed_loads = [(wtok[:], A["wtok"])]
        rel_loads = [(ident[:], A["c_ident"]), (base[:], A["base"]), (cols[:], A["cols"]),
                     (mats[:, 0:A_MATS], A["mats"][:, 0:A_MATS]), (relq[:], A["relq"]), (relk[:], A["relk"]),
                     (head_of_row[:], A["c_head_of_row"]), (third_of_head[:], A["c_third"]),
                     (rows[:].rearrange("p r e -> p (r e)"), rows_in)]
        causal_loads = [(mats[:, A_MATS:F_MATS], A["mats"][:, A_MATS:F_MATS]), (causal[:], A["c_causal"]),
                        (wr0[:], A["wr0"]), (br0[:], A["br0"].partition_broadcast(TOK))]
        late_loads = [(mats[:, F_MATS:], A["mats"][:, F_MATS:]), (of_image[:], A["c_of_image"]),
                      (same_head[:], A["c_same_head"]), (before[:], A["c_before"]), (rev8[:], A["c_rev8"]),
                      (slot_base[:], A["c_slot_base"]), (real[:], A["c_real"]), (fulls[:], A["c_fulls"]),
                      (entry[:], A["c_entry"]), (wr1[:], A["wr1"])]
        N_CONST, N_REST = len(rel_loads), len(causal_loads) + len(late_loads)

        carriers = [0]

        def idle_element():
            carriers[0] += 1
            return idle[0:1, carriers[0] - 1:carriers[0]]

        def carry_dve():
            nc.vector.memset(idle_element(), 0.0)

        def carry_pool():
            nc.gpsimd.tensor_tensor(idle_element(), half[0:1, :], half[0:1, :], ALU.add)

        def carry_pe(free):
            nc.tensor.matmul(free[0:1, 0:1], ident[:, 0:1], ident[:, 0:1], start=True, stop=True)

        def walk(eng, M, tile, unroll=False):
            i_ = M["i"]

            def expert(i, b):
                e = BUFS * i + b
                if b > 1:
                    e = nc.s_assert_within(e, 0, EXPERTS - 1)
                n = eng.value_load(plan[0:1, i_, 0, bass.ds(e, 1)], min_val=1, max_val=M["tiles"])
                at = eng.value_load(plan[0:1, i_, 1, bass.ds(e, 1)], min_val=0, max_val=M["tiles"] * EXPERTS)
                tile(i, b, e, 0, 0, at)
                for t in range(1, min(AHEAD, M["tiles"])):
                    with eng.If(n > t):
                        tile(i, b, e, t, t % 2, at + t)
                if M["tiles"] > AHEAD:
                    with eng.If(n > AHEAD):
                        if unroll:
                            for t in range(AHEAD, M["tiles"]):
                                with eng.If(n > t):
                                    tile(i, b, e, t, t % 2, at + t)
                        else:
                            with eng.Fori(AHEAD, M["tiles"], 2) as t:
                                for k in range(2):
                                    with eng.If(n > t + k):
                                        tile(i, b, e, t + k, k, at + (t + k))
                                eng.nop()
                        eng.nop()

            with eng.Fori(0, -(-EXPERTS // BUFS)) as i:
                for b in range(BUFS):
                    if b < EXPERTS % BUFS:
                        expert(i, b)
                    else:
                        with eng.If(i < EXPERTS // BUFS):
                            expert(i, b)
                eng.nop()

        def is_first(t):
            return isinstance(t, int) and t == 0

        def tiles_so_far(eng, M):
            return eng.value_load(plan[0:1, M["i"], 1, EXPERTS:EXPERTS + 1], min_val=EXPERTS,
                                  max_val=M["tiles"] * EXPERTS)

        def after_first(eng, i, b, t, what):
            if b == 0 and is_first(t):
                with eng.If(i > 0):
                    what()
            else:
                what()

        block = ctx.enter_context(nc.Block())

        LOADS = (4, 2)

        def weights_there(M, i, b):
            before_ = 0 if M is m0 else LOADS[0] * len(range(b, EXPERTS, BUFS))
            return 16 * (before_ + LOADS[M["i"]] * (i + 1))

        def up_of(M, b):
            return w_up[b] if b < 2 else up3[M["i"]]

        def down_of(M, b):
            return w_dn[b] if b < 2 else dn3[M["i"]]

        def load_expert(eng, M, e, b):
            up, down = (A["e_w1"], A["e_w2"]) if M is m0 else (A["g_w1"], A["g_w2"])
            for dst, src in ((up_of(M, b)[:, 0:CT * M["width"]], up), (down_of(M, b)[:, 0:M["nf"] * E], down)):
                eng.dma_start(dst, src[bass.ds(e, 1)].rearrange("o p n -> p (o n)")).then_inc(s_weights[b], 16)
            if M is m0:
                eng.dma_start(b_up[b][:], A["eb1"][bass.ds(e, 1)].rearrange("o p n -> p (o n)"))\
                    .then_inc(s_weights[b], 16)
                eng.dma_start(b_dn[b][:], A["eb2"][bass.ds(e, 1)].rearrange("o n -> (o n)").partition_broadcast(TILE))\
                    .then_inc(s_weights[b], 16)

        @block.sync
        def _(sp):
            def load(pairs, done):
                for dst, src in pairs:
                    sp.dma_start(dst, src).then_inc(done, 16)

            def send_relative(n):
                for i, way in enumerate(("q", "k")):
                    sp.wait_ge(s_qe, 6 * n + 3 * i + 3)
                    dst = rel_scratch[way][0]
                    sp.dma_start(dst, qe[:, i, :]).then_inc(s_qe_out[i], 16)
                for i, way in enumerate(("q", "k")):
                    sp.wait_ge(s_qe_out[i], 16 * (n + 1))
                    src = rel_scratch[way]
                    wide = REL * HEADS
                    for j in range(PER):
                        at = src.offset + j * SEQ * wide + (SEQ - 1) * HEADS
                        if way == "q":
                            ap = [[wide - HEADS, SEQ], [1, HS]]
                        else:
                            ap = [[HEADS, SEQ], [wide - HEADS, SEQ], [1, HEADS]]
                        dst = relb[j * SEQ:(j + 1) * SEQ, i, :]
                        if way == "k":
                            dst = dst.rearrange("p (r h) -> p r h", h=HEADS)
                        sp.dma_start(dst, bass.AP(tensor=src.tensor, offset=at, ap=ap)).then_inc(s_rel_in, 16)

            def relative_block(n, last=False):
                if not last:
                    sp.wait_ge(s_tok, n + 1)
                    at = bass.ds(n + 1, 1)
                    sp.dma_start(patches, A["xT"][at].rearrange("o p k t -> p (o k) t")).then_inc(s_patch, 16)
                send_relative(n)

            sp.dma_start(patches, A["xT"][0]).then_inc(s_patch, 16)
            load(embed_loads, s_wtok)
            load(rel_loads, s_const)
            load(causal_loads, s_rest)
            relative_block(0)
            load(late_loads, s_rest)
            load_expert(sp, m0, 0, 0)
            load_expert(sp, m0, 1, 1)
            with sp.Fori(1, GROUPS - 1) as n:
                relative_block(n)
            relative_block(GROUPS - 1, last=True)

            def lists(M):
                i_ = M["i"]
                sp.wait_ge(M["s_plan"], 1)
                sp.wait_ge(M["s_listed"], 16 * 2 * GROUPS)
                if M is m0:
                    more = sp.value_load(ties[0:1, 0:1], min_val=0, max_val=EXPERTS * IMAGES * SEQ)
                    with sp.If(more > 0):
                        sp.wait_ge(s_tie_listed, 16 * (EXPERTS - 2) * GROUPS)
                    sp.nop()

                sp.dma_start(lists_in[:, 0:EXPERTS * M["tiles"] * 2].rearrange("p (n w) -> p n w", w=2),
                             LIST_dram[i_].rearrange("(n p) w -> p n w", p=TILE)).then_inc(s_lists, 16)
                u = tiles_so_far(sp, M)
                sp.wait_ge(M["s_added"], 16 * (u + 1))

            def sum_rows(lo, hi):
                return SUM_dram[lo * TOK:hi * TOK].rearrange("(g t) e -> t g e", t=TOK)

            def groups_of(t, lo, hi):
                return t[:, lo * E:hi * E].rearrange("t (g e) -> t g e", e=E)

            lists(m0)
            sp.dma_start(groups_of(H, 0, 1), sum_rows(0, 1)).then_inc(s_back[0], 16)
            sp.dma_start(groups_of(H, 1, GROUPS), sum_rows(1, GROUPS)).then_inc(s_back[1], 16)
            load_expert(sp, m1, 0, 0)
            load_expert(sp, m1, 1, 1)
            lists(m1)
            for k, (lo, hi) in enumerate(SPANS):
                sp.dma_start(groups_of(SRC, lo, hi), sum_rows(lo, hi)).then_inc(s_back[2 + k], 16)
            for lo, hi in SPANS:
                sp.wait_ge(s_fin, hi)
                sp.dma_start(A["out"][:, lo * E:hi * E], H[:, lo * E:hi * E]).then_inc(s_out, 16)
            sp.wait_ge(s_out, 16 * len(SPANS))

        @block.tensor
        def _(pe):
            def transpose_in(L, n):
                pe.wait_ge(L["s_xin"], L["at"] + n + 1)
                for c in range(CT):
                    last = nc.tensor.transpose(L["in_psum"][:, c * TOK:(c + 1) * TOK], L["xin"][:, c * 128:(c + 1) * 128],
                                               ident[0:TOK, 0:TOK])
                last.then_inc(L["s_xT_psum"], 1)

            def project(L, n, p):
                pe.wait_ge(L["s_xT"], L["at"] + n + 1)
                for w, dst in (("q", L["b"][1]), ("k", L["b"][2])):
                    for m in range(CT):
                        for c in range(CT):
                            last = nc.tensor.matmul(dst[:, m * TOK:(m + 1) * TOK],
                                                    mat(f"{p}_W{w}", c, m * 128, (m + 1) * 128), L["xT"][:, c, :],
                                                    start=(c == 0), stop=(c == CT - 1))
                last.then_inc(L["s_qk_psum"], 1)

            def project_values(L, n, p):
                pe.wait_ge(L["s_x3"], L["at"] + n + 1)
                for j in range(PER):
                    dst = (L["b"][0][0:TOK, j * E:(j + 1) * E] if j < 2 else L["v2_psum"])
                    for c in range(CT):
                        last = nc.tensor.matmul(dst, L["x3"][:, c, j, :], mat(f"{p}_Wv", c), start=(c == 0), stop=(c == CT - 1))
                last.then_inc(L["s_v_psum"], 1)

            def scores(L, n):
                pe.wait_ge(L["s_qM"], L["at"] + n + 1)
                for c in range(CT):
                    pe.wait_ge(L["s_kB"], CT * (L["at"] + n) + c + 1)
                    for b, (lo, hi) in enumerate(((0, K0), (K0, SEQ))):
                        dst = L["b"][1 + b][0:TOK, 0:(hi - lo) * HEADS].rearrange("p (k h) -> p k h", h=HEADS)
                        for j in range(PER):
                            last = nc.tensor.matmul(dst[:, :, c * HC:(c + 1) * HC], L["qM"][:, c, j, :],
                                                    L["kB"][:, c, j * SEQ + lo:j * SEQ + hi, :],
                                                    start=(j == 0 and c == 0), stop=(j == PER - 1 and c == CT - 1),
                                                    skip_group_check=True)
                last.then_inc(L["s_s_psum"], 1)

            def transpose_probs(L, n):
                pe.wait_ge(L["s_probs"], L["at"] + n + 1)
                for t in range(CHUNKS):
                    w = min(HPC * SEQ, HS - t * HPC * SEQ)
                    dst = L["b"][0 if t < 3 else 3][0:w, (t % 3) * TOK:(t % 3 + 1) * TOK]
                    last = nc.tensor.transpose(dst, L["pr"][:, t * HPC * SEQ:t * HPC * SEQ + w], ident[0:TOK, 0:TOK])
                last.then_inc(L["s_pT_psum"], 1)

            def contexts(L, n):
                pe.wait_ge(L["s_pT"], L["at"] + n + 1)
                for j in range(PER):
                    dst = L["b"][1][0:SEQ, j * E:(j + 1) * E] if j < 2 else L["b"][2][0:SEQ, 0:E]
                    for t in range(CHUNKS):
                        h = min(HPC, HEADS - t * HPC)
                        at = t * HPC * HD
                        last = nc.tensor.matmul(dst[:, at:at + h * HD],
                                                L["pT"][0:h * SEQ, t, j * SEQ:(j + 1) * SEQ],
                                                L["vB"][0:h * SEQ, j, at:at + h * HD],
                                                start=True, stop=True)
                last.then_inc(L["s_c_psum"], 1)

            def transpose_ctx(L, n):
                pe.wait_ge(L["s_cx"], L["at"] + n + 1)
                carry_pe(L["b"][0])
                for c in range(CT):
                    for j in range(PER):
                        at = c * TOK + j * SEQ
                        last = nc.tensor.transpose(L["b"][0][:, at:at + SEQ], L["cx"][:, j, c * 128:(c + 1) * 128],
                                                   ident[0:SEQ, 0:SEQ])
                last.then_inc(L["s_cT_psum"], 1)

            def output(L, n, p):
                pe.wait_ge(L["s_cT"], L["at"] + n + 1)
                for c in range(CT):
                    last = nc.tensor.matmul(L["b"][3][0:TOK, 0:E], L["cT"][:, c, :], mat(f"{p}_Wo", c),
                                            start=(c == 0), stop=(c == CT - 1))
                last.then_inc(L["s_o_psum"], 1)

            def embed(n, first=False):
                pe.wait_ge(s_patch, 16 * (n + 1))
                if not first:
                    pe.wait_ge(a1["s_vB"], n)
                for k in range(PK):
                    last = nc.tensor.matmul(tokens_psum, patches[:, k, :], wtok[:, k, :],
                                            start=(k == 0), stop=(k == PK - 1))
                last.then_inc(s_tok, 1)

            def distances(n):
                for i, (x, table) in enumerate(((a1["qT"], relq), (a1["kT"], relk))):
                    for part in range(3):
                        u = 3 * i + part
                        lo, hi = REL_CUTS[part], REL_CUTS[part + 1]
                        if u == 0:
                            pe.wait_ge(a1["s_qT"], n + 1)
                        if u == 1:
                            pe.wait_ge(a1["s_kT"], CT * (n + 1))
                        if u >= 2:
                            pe.wait_ge(s_qe, 6 * n + u - 1)
                        dst = a1["b"][1 + u % 2][0:TOK, 0:(hi - lo) * HEADS]
                        dst = dst.rearrange("p (r h) -> p r h", h=HEADS)
                        for c in range(CT):
                            last = nc.tensor.matmul(dst[:, :, c * HC:(c + 1) * HC], x[:, c, :],
                                                    table[:, lo:hi, :], start=(c == 0), stop=(c == CT - 1),
                                                    skip_group_check=True)
                        last.then_inc(s_qe_psum, 1)

            def router_T(L, dst, n, s_in, src, s_psum):
                pe.wait_ge(s_in, L["at"] + n + 1)
                for c in range(CT):
                    last = nc.tensor.transpose(dst[:, c * TOK:(c + 1) * TOK], src[:, c * 128:(c + 1) * 128],
                                               ident[0:TOK, 0:TOK])
                last.then_inc(s_psum, 1)

            def router(logits_psum, n, s_T, dstT, w, s_logit):
                pe.wait_ge(s_T, n + 1)
                for c in range(CT):
                    last = nc.tensor.matmul(logits_psum, dstT[:, c, :], w[:, c, :],
                                            start=(c == 0), stop=(c == CT - 1))
                last.then_inc(s_logit, 1)

            def rank(M, part):
                lo, hi = PARTS[part]
                pe.wait_ge(M["s_chosen"], part + 1)

                def flat(x):
                    return x[:, lo:hi, :].rearrange("p g e -> p (g e)")
                dst = bank[0][0:TOK, lo * EXPERTS:hi * EXPERTS]
                nc.tensor.matmul(dst, before[:, :], flat(tmp8[1]), start=True, stop=False)
                last = nc.tensor.matmul(dst, ones[:, :], flat(tmp8[2]), start=False, stop=True)
                if part:
                    dst = bank[0][0:TOK, hi * EXPERTS:(hi + 1) * EXPERTS]
                    nc.tensor.matmul(dst, ones[:, :], flat(tmp8[1]), start=True, stop=False)
                    last = nc.tensor.matmul(dst, ones[:, :], flat(tmp8[2]), start=False, stop=True)
                last.then_inc(M["s_rank_psum"], 1)

            def first_layer(n, causal=True, last=False):
                m = n - 1
                distances(n)
                if causal:
                    pe.wait_ge(a1["s_done"], n)
                    transpose_in(a2, m)
                project_values(a1, n, "a")
                if causal:
                    project(a2, m, "f")
                    project_values(a2, m, "f")
                    scores(a2, m)
                pe.wait_ge(s_qe, 6 * n + 6)
                scores(a1, n)
                if not last:
                    embed(n + 1)
                if causal:
                    transpose_probs(a2, m)
                    contexts(a2, m)
                    transpose_ctx(a2, m)
                transpose_probs(a1, n)
                if causal:
                    output(a2, m, "f")
                contexts(a1, n)
                if not last:
                    transpose_in(a1, n + 1)
                transpose_ctx(a1, n)
                if causal:
                    router_T(a2, bank[4], m, a2["s_in2"], a2["work2"], s_nT_psum)
                output(a1, n, "a")
                if not last:
                    project(a1, n + 1, "a")
                if causal:
                    router(logits0_psum, m, s_nT, nT, wr0, s_log)

            pe.wait_ge(s_wtok, 16)
            embed(0, first=True)
            pe.wait_ge(s_const, 16 * N_CONST)
            transpose_in(a1, 0)
            project(a1, 0, "a")
            first_layer(0, causal=False)
            pe.wait_ge(s_rest, 16 * N_REST)
            with pe.Fori(1, GROUPS - 1) as n:
                first_layer(n)
            first_layer(GROUPS - 1, last=True)
            m = GROUPS - 1
            transpose_in(a2, m)
            project(a2, m, "f")
            rank(m0, 0)
            project_values(a2, m, "f")
            scores(a2, m)
            transpose_probs(a2, m)
            contexts(a2, m)
            transpose_ctx(a2, m)
            output(a2, m, "f")
            router_T(a2, bank[4], m, a2["s_in2"], a2["work2"], s_nT_psum)
            router(logits0_psum, m, s_nT, nT, wr0, s_log)

            def experts(M):
                nf, width = M["nf"], M["width"]
                pe.wait_ge(M["s_plan"], 1)

                def down(u, f, b):
                    pe.wait_ge(M["s_act"], RING + u * nf + f + 1)
                    return nc.tensor.matmul(bank[5][:, 0:E], mid[:, f, :], down_of(M, b)[:, f * E:(f + 1) * E],
                                            start=(f == 0), stop=(f == nf - 1))

                def tail(u, b):
                    down(u, nf - 2, b)
                    down(u, nf - 1, b).then_inc(M["s_down"], 1)

                def tile(i, b, e, t, parity, u):
                    pe.wait_ge(M["s_x_rows"], 16 * (u + 1))
                    carry_pe(bank[4])
                    pe.wait_ge(M["s_x_T"], u + 1)
                    carry_pe(bank[4])
                    for c in range(CT):
                        last = nc.tensor.transpose(bank[4][:, c * TILE:(c + 1) * TILE],
                                                   x_rows[b][parity][:, c * 128:(c + 1) * 128], ident[:, :])
                    last.then_inc(M["s_xT_psum"], 1)
                    after_first(pe, i, b, t, lambda: tail(u - 1, (b - 1) % BUFS if is_first(t) else b))
                    if is_first(t):
                        pe.wait_ge(s_weights[b], weights_there(M, i, b))
                    pe.wait_ge(M["s_x_T"], u + 2)
                    for f in range(nf):
                        pe.wait_ge(M["s_act"], RING + u * nf + f - 3)
                        for c in range(CT):
                            at = c * width + f * 128
                            last = nc.tensor.matmul(bank[f % RING][:, 0:TILE], up_of(M, b)[:, at:at + 128], x_T[:, c, :],
                                                    start=(c == 0), stop=(c == CT - 1))
                        last.then_inc(M["s_up"], 1)
                        if f == 2:
                            pe.wait_ge(M["s_y"], u + 1)
                        if f >= 2:
                            down(u, f - 2, b)

                pe.sem_inc(M["s_xT_psum"], 2)
                pe.sem_inc(M["s_down"], 1)
                walk(pe, M, tile)
                tail(tiles_so_far(pe, M) - 1, (EXPERTS - 1) % BUFS)

            rank(m0, 1)
            experts(m0)

            def cos_block_1(n, first=False):
                if not first:
                    pe.wait_ge(ln["s_done"], n)
                pe.wait_ge(ln["s_xin"], n + 1)
                for c in range(CT):
                    last = nc.tensor.transpose(ln["b"][0][:, c * TOK:(c + 1) * TOK], ln["xin"][:, c * 128:(c + 1) * 128],
                                               ident[0:TOK, 0:TOK])
                last.then_inc(ln["s_xT_psum"], 1)

            def cos_block_2(n):
                pe.wait_ge(ln["s_xT"], n + 1)
                for i, w in enumerate("qkv"):
                    for c in range(CT):
                        last = nc.tensor.matmul(ln["b"][1 + i][0:TOK, 0:E], ln["xT"][:, c, :], mat(f"l_W{w}", c),
                                                start=(c == 0), stop=(c == CT - 1))
                last.then_inc(ln["s_qkv_psum"], 1)

            def cos_block_3(n):
                pe.wait_ge(ln["s_qn"], n + 1)
                for c in range(CT):
                    last = nc.tensor.transpose(ln["b"][0][:, c * TOK:(c + 1) * TOK], ln["q"][:, 0, c * 128:(c + 1) * 128],
                                               ident[0:TOK, 0:TOK])
                last.then_inc(ln["s_qT_psum"], 1)
                pe.wait_ge(ln["s_km"], n + 1)
                for c in range(CT):
                    for j in range(PER):
                        last = nc.tensor.matmul(ln["b"][1 + c][:, j * 128:(j + 1) * 128],
                                                ln["km"][:, j, c * 128:(c + 1) * 128],
                                                ln["q"][:, 2, c * 128:(c + 1) * 128], start=True, stop=True)
                last.then_inc(ln["s_kv_psum"], 1)

            def cos_block_4(n):
                pe.wait_ge(ln["s_qT"], n + 1)
                pe.wait_ge(ln["s_kv"], n + 1)
                for c in range(CT):
                    for j in range(PER):
                        at = c * TOK + j * SEQ
                        last = nc.tensor.matmul(ln["b"][3][:, at:at + SEQ], ln["kv"][:, c, j, :],
                                                ln["qT"][:, c, j * SEQ:(j + 1) * SEQ], start=True, stop=True)
                last.then_inc(ln["s_cT_psum"], 1)

            def cos_block_5(n):
                pe.wait_ge(ln["s_cT"], n + 1)
                for c in range(CT):
                    last = nc.tensor.matmul(ln["b"][0][0:TOK, 0:E], ln["cT"][:, c, :], mat("l_Wo", c),
                                            start=(c == 0), stop=(c == CT - 1))
                last.then_inc(ln["s_o_psum"], 1)

            def gqa_router(m):
                router_T(a3, bank[0], m, a3["s_in2"], a3["work2"], s_gT_psum)
                pe.wait_ge(s_glg, m + 1)
                router(logits1_psum, m, s_gT, gT, wr1, s_glog)

            def second_layer(n, gqa=True, last=False):
                m = n - 1
                if gqa:
                    scores(a3, m)
                    project_values(a3, m, "g")
                cos_block_3(n)
                if gqa:
                    transpose_probs(a3, m)
                cos_block_4(n)
                if gqa:
                    contexts(a3, m)
                cos_block_5(n)
                if gqa:
                    transpose_ctx(a3, m)
                if not last:
                    cos_block_1(n + 1)
                    cos_block_2(n + 1)
                transpose_in(a3, n)
                if gqa:
                    output(a3, m, "g")
                project(a3, n, "g")
                if gqa:
                    pe.wait_ge(a3["s_x3"], a3["at"] + n + 1)
                    gqa_router(m)

            cos_block_1(0, first=True)
            cos_block_2(0)
            second_layer(0, gqa=False)
            with pe.Fori(1, GROUPS - 1) as n:
                second_layer(n)
            second_layer(GROUPS - 1, last=True)
            n = GROUPS - 1
            rank(m1, 0)
            scores(a3, n)
            project_values(a3, n, "g")
            transpose_probs(a3, n)
            contexts(a3, n)
            transpose_ctx(a3, n)
            output(a3, n, "g")
            gqa_router(n)

            rank(m1, 1)
            experts(m1)

        @block.scalar
        def _(act):
            def copy_in(L, n):
                act.wait_ge(L["s_xT_psum"], L["at"] + n + 1)
                nc.scalar.activation(L["xT"][:].rearrange("p c t -> p (c t)"), L["in_psum"], ACT.Copy)\
                    .then_inc(L["s_xT"], 1)

            def copy_three(L, n):
                nc.scalar.activation(
                    L["x3"].rearrange("p c j (r k) -> p (c j) r k", r=HPC),
                    L["in_psum"].rearrange("p (cj k) -> p cj k", k=SEQ)[:, :, None, :]
                    .to_broadcast([128, CT * PER, HPC, SEQ]), ACT.Copy).then_inc(L["s_x3"], 1)

            def copy_scaled(L, n, p):
                act.wait_ge(L["s_xT_psum"], L["at"] + n + 1)
                src = L["in_psum"]
                for c in range(CT):
                    last = nc.scalar.activation(L["xT"][:, c, :], src[:, c * TOK:(c + 1) * TOK], ACT.Identity,
                                                bias=col(p + "_b1", c), scale=col(p + "_g1", c))
                last.then_inc(L["s_xT"], 1)
                for c in range(CT):
                    last = nc.scalar.activation(
                        L["x3"][:, c].rearrange("p j (r k) -> p j r k", r=HPC),
                        src[:, c * TOK:(c + 1) * TOK].rearrange("p (j k) -> p j k", k=SEQ)[:, :, None, :]
                        .to_broadcast([128, PER, HPC, SEQ]), ACT.Identity,
                        bias=col(p + "_b1", c), scale=col(p + "_g1", c))
                last.then_inc(L["s_x3"], 1)

            def own_rows(L):
                blocks = L["qM"][:].rearrange("p c j (i k) -> p c (j i) k", k=SEQ)
                return blocks[:, :, 0:PER * PER:PER + 1, :]

            def queries_keys(L, n, bq, bk):
                act.wait_ge(L["s_qk_psum"], L["at"] + n + 1)
                if L is a1:
                    for c in range(CT):
                        last = nc.scalar.activation(L["qT"][:, c, :], L["b"][1][:, c * TOK:(c + 1) * TOK], ACT.Identity,
                                                    bias=col(bq, c))
                    last.then_inc(L["s_qT"], 1)
                for c in range(CT):
                    nc.scalar.activation(L["kT"][:, c, :], L["b"][2][:, c * TOK:(c + 1) * TOK], ACT.Identity,
                                         bias=col(bk, c)).then_inc(L["s_kT"], 1)
                if L is not a1:
                    for c in range(CT):
                        last = nc.scalar.activation(own_rows(L)[:, c],
                                                    L["b"][1][:, c * TOK:(c + 1) * TOK].rearrange("p (j k) -> p j k", k=SEQ),
                                                    ACT.Identity, bias=col(bq, c))
                    last.then_inc(L["s_qM"], 1)

            def spread_queries(L, n):
                act.wait_ge(L["s_qT"], n + 1)
                nc.scalar.activation(own_rows(L), L["qT"][:].rearrange("p c (j k) -> p c j k", k=SEQ), ACT.Copy)\
                    .then_inc(L["s_qM"], 1)

            def exps(L, n):
                act.wait_ge(L["s_shifted"], L["at"] + n + 1)
                nc.scalar.activation(L["pr"][:].rearrange("p (h k) -> p k h", h=HEADS),
                                     L["sc"][:].rearrange("p (k h) -> p k h", h=HEADS), ACT.Exp, scale=HD ** -0.5)\
                    .then_inc(L["s_exped"], 1)

            def probs_T(L, n):
                act.wait_ge(L["s_pT_psum"], L["at"] + n + 1)
                full = HPC * SEQ
                nc.scalar.activation(L["pT"][0:full, 0:3, :].rearrange("p t q -> p (t q)"), L["b"][0][0:full, 0:3 * TOK], ACT.Copy)
                nc.scalar.activation(L["pT"][0:full, 3:5, :].rearrange("p t q -> p (t q)"), L["b"][3][0:full, 0:2 * TOK], ACT.Copy)
                nc.scalar.activation(L["pT"][0:SEQ, 5, :], L["b"][3][0:SEQ, 2 * TOK:3 * TOK], ACT.Copy)\
                    .then_inc(L["s_pT"], 1)

            def ctx_out(L, n):
                act.wait_ge(L["s_c_psum"], L["at"] + n + 1)
                nc.scalar.activation(L["cx"][:, 0:2, :].rearrange("p j e -> p (j e)"), L["b"][1][0:SEQ, 0:2 * E], ACT.Copy)
                nc.scalar.activation(L["cx"][:, 2, :], L["b"][2][0:SEQ, 0:E], ACT.Copy).then_inc(L["s_cx"], 1)

            def ctx_T(L, n, bv):
                act.wait_ge(L["s_cT_psum"], L["at"] + n + 1)
                for c in range(CT):
                    last = nc.scalar.activation(L["cT"][:, c, :], L["b"][0][:, c * TOK:(c + 1) * TOK], ACT.Identity,
                                                bias=col(bv, c))
                last.then_inc(L["s_cT"], 1)

            def distances(n):
                for i in range(2):
                    for part in range(3):
                        u = 3 * i + part
                        lo, hi = REL_CUTS[part], REL_CUTS[part + 1]
                        act.wait_ge(s_qe_psum, 6 * n + u + 1)
                        nc.scalar.activation(qe[:, i, lo * HEADS:hi * HEADS],
                                             a1["b"][1 + u % 2][0:TOK, 0:(hi - lo) * HEADS], ACT.Copy)\
                            .then_inc(s_qe, 1)

            def normed_T(n):
                act.wait_ge(s_nT_psum, n + 1)
                for c in range(CT):
                    last = nc.scalar.activation(nT[:, c, :], a2["b"][0][:, c * TOK:(c + 1) * TOK], ACT.Identity,
                                                bias=col("f_b2", c), scale=col("f_g2", c))
                last.then_inc(s_nT, 1)
                act.wait_ge(a2["s_in2"], n + 1)
                act.dma_start(X_dram[bass.ds(n * TOK, TOK)], a2["work2"][:]).then_inc(s_rows, 16)
                act.wait_ge(a2["s_done"], n + 1)
                act.dma_start(SUM_dram[bass.ds(n * TOK, TOK)], of_group(H, n)).then_inc(s_rows, 16)

            act.dma_start(LIST_dram[0], A["c_list0"]).then_inc(s_init, 16)
            act.dma_start(LIST_dram[1], A["c_list1"]).then_inc(s_init, 16)
            def first_layer(n, causal=True, last=False):
                m = n - 1
                queries_keys(a1, n, "a_bq", "a_bk")
                distances(n)
                spread_queries(a1, n)
                if causal:
                    copy_scaled(a2, m, "f")
                    queries_keys(a2, m, "f_bq", "f_bk")
                    exps(a2, m)
                    probs_T(a2, m)
                exps(a1, n)
                if causal:
                    ctx_out(a2, m)
                    ctx_T(a2, m, "f_bv")
                probs_T(a1, n)
                ctx_out(a1, n)
                if not last:
                    copy_in(a1, n + 1)
                ctx_T(a1, n, "a_bv")
                if not last:
                    copy_three(a1, n + 1)
                if causal:
                    normed_T(m)

            act.wait_ge(s_const, 16 * N_CONST)
            act.wait_ge(s_zeroed, 1)
            copy_in(a1, 0)
            copy_three(a1, 0)
            first_layer(0, causal=False)
            with act.Fori(1, GROUPS - 1) as n:
                first_layer(n)
            first_layer(GROUPS - 1, last=True)
            def gate_exps(part):
                lo, hi = PARTS[part]
                act.wait_ge(s_shifted0, part + 1)
                nc.scalar.activation(tmp8[1][:, lo:hi, :], tmp8[0][:, lo:hi, :], ACT.Exp).then_inc(m0["s_exp"], 1)

            m = GROUPS - 1
            gate_exps(0)
            copy_scaled(a2, m, "f")
            queries_keys(a2, m, "f_bq", "f_bk")
            exps(a2, m)
            probs_T(a2, m)
            ctx_out(a2, m)
            ctx_T(a2, m, "f_bv")
            normed_T(m)

            gate_exps(1)

            def gelus(M, norm, bias):
                nf = M["nf"]
                act.sem_inc(M["s_act"], RING)
                act.wait_ge(M["s_plan"], 1)

                def tile(i, b, e, t, parity, u):
                    if is_first(t) and bias:
                        act.wait_ge(s_weights[b], weights_there(M, i, b))
                    act.wait_ge(M["s_xT_psum"], u + 3)
                    for c in range(CT):
                        kw = dict(bias=col("f_b2", c), scale=col("f_g2", c)) if norm else {}
                        last = nc.scalar.activation(x_T[:, c, :], bank[4][:, c * TILE:(c + 1) * TILE],
                                                    ACT.Identity if norm else ACT.Copy, **kw)
                    last.then_inc(M["s_x_T"], 1)
                    for f in range(nf):
                        act.wait_ge(M["s_up"], u * nf + f + 1)
                        kw = dict(bias=b_up[b][:, f:f + 1]) if bias else {}
                        nc.scalar.activation(mid[:, f, :], bank[f % RING][:, 0:TILE], ACT.Gelu, **kw)\
                            .then_inc(M["s_act"], 1)
                        if f == 2 and is_first(t):
                            def load_next():
                                act.wait_ge(M["s_down"], u + 1)
                                act.wait_ge(M["s_y"], u + 1)
                                load_expert(act, M, nc.s_assert_within(e + 2, 2, EXPERTS - 1), (b + 2) % BUFS)
                            if b == BUFS - 1:
                                load_next()
                            else:
                                with act.If(i < EXPERTS // BUFS):
                                    load_next()

                act.sem_inc(M["s_x_T"], 1)
                walk(act, M, tile)

            gelus(m0, True, True)

            nc.scalar.activation(inv_scale[:, 0, :], cols[:, COLS.index("l_m"), :], ACT.Sigmoid)\
                .then_inc(s_scale, 1)
            act.wait_ge(s_scale, 1)
            nc.scalar.activation(inv_scale[:, 1, :], inv_scale[:, 0, :], ACT.Exp, scale=-float(np.log(SEQ)))\
                .then_inc(s_scale, 1)

            def cos_1(n):
                act.wait_ge(ln["s_xT_psum"], n + 1)
                nc.scalar.activation(ln["xT"][:].rearrange("p c t -> p (c t)"), ln["b"][0][:, 0:CT * TOK], ACT.Copy)\
                    .then_inc(ln["s_xT"], 1)

            def cos_2(n):
                act.wait_ge(ln["s_qkv"], n + 1)
                nc.scalar.activation(ln["sq"][:], ln["q"][:, 0:2, :], ACT.Square).then_inc(ln["s_squares"], 1)

            def cos_3(n):
                act.wait_ge(ln["s_qT_psum"], n + 1)
                nc.scalar.activation(ln["qT"][:].rearrange("p c t -> p (c t)"), ln["b"][0][:, 0:CT * TOK], ACT.Copy)\
                    .then_inc(ln["s_qT"], 1)

            def cos_4(n):
                act.wait_ge(ln["s_cT_psum"], n + 1)
                nc.scalar.activation(ln["cT"][:].rearrange("p c t -> p (c t)"), ln["b"][3][:, 0:CT * TOK], ACT.Copy)\
                    .then_inc(ln["s_cT"], 1)

            def src_T(n):
                act.wait_ge(s_gT_psum, n + 1)
                nc.scalar.activation(gT[:].rearrange("p c t -> p (c t)"), bank[0][:, 0:CT * TOK], ACT.Copy)\
                    .then_inc(s_gT, 1)
                act.wait_ge(a3["s_in2"], a3["at"] + n + 1)
                act.dma_start(X_dram[bass.ds(n * TOK, TOK)], a3["work2"][:]).then_inc(s_rows, 16)
                act.dma_start(SUM_dram[bass.ds(n * TOK, TOK)], a3["work2"][:]).then_inc(s_rows, 16)

            def second_layer(n, gqa=True, last=False):
                m = n - 1
                cos_3(n)
                if gqa:
                    exps(a3, m)
                if gqa:
                    probs_T(a3, m)
                cos_4(n)
                if gqa:
                    ctx_out(a3, m)
                if not last:
                    cos_1(n + 1)
                if gqa:
                    ctx_T(a3, m, "g_vb")
                copy_in(a3, n)
                copy_three(a3, n)
                if not last:
                    cos_2(n + 1)
                queries_keys(a3, n, "g_qb", "g_kb")
                if gqa:
                    src_T(m)

            cos_1(0)
            cos_2(0)
            second_layer(0, gqa=False)
            with act.Fori(1, GROUPS - 1) as n:
                second_layer(n)
            second_layer(GROUPS - 1, last=True)
            def sigmoid_exps(part):
                lo, hi = PARTS[part]
                act.wait_ge(s_glg, hi + 1)
                nc.scalar.activation(tmp8[0][:, lo:hi, :], LOGITS[:, lo:hi, :], ACT.Exp, scale=-1.0)\
                    .then_inc(m1["s_exp"], 1)

            m = GROUPS - 1
            sigmoid_exps(0)
            exps(a3, m)
            probs_T(a3, m)
            ctx_out(a3, m)
            ctx_T(a3, m, "g_vb")
            src_T(m)
            sigmoid_exps(1)
            gelus(m1, False, False)

        @block.vector
        def _(dve):
            link_no = {}

            def link(L, n, ins):
                k = link_no[L["tag"]] = link_no.get(L["tag"], 0) + 1
                ins.then_inc(L["s_dve"], 1)
                dve.wait_ge(L["s_dve"], L["dve_at"] + n * DVE_LINKS[L["tag"]] + k)

            def end_links(L):
                assert link_no[L["tag"]] == DVE_LINKS[L["tag"]], (L["tag"], link_no[L["tag"]])
                link_no[L["tag"]] = 0

            def normed(out, x, mean, rstd):
                return nc.vector.tensor_scalar(out, x, mean, rstd, ALU.subtract, ALU.mult)

            def rel_embed(n, body):
                dve.wait_ge(s_tok, n + 1)
                if body is not None:
                    dve.wait_ge(a1["s_bias_in"], n)
                at = 0 if body is None else body
                link(a1, at, nc.vector.tensor_tensor(a1["h0"][:], tokens_psum, base[:], ALU.add))
                link(a1, at, nc.vector.bn_stats(a1["st"][:], a1["h0"][:]))
                carry_dve()
                nc.vector.bn_aggr(a1["mv"][:], a1["st"][:]).then_inc(a1["s_stat"], 1)

            def rel_norm(n):
                dve.wait_ge(a1["s_rstd"], n + 1)
                normed(a1["xin"][:], a1["h0"][:], a1["mv"][:, 0:1], a1["rs"][:, 0:1]).then_inc(a1["s_xin"], 1)

            def causal_pre(n):
                dve.wait_ge(a1["s_done"], n + 1)
                link(a2, n, nc.vector.bn_stats(a2["st"][:], of_group(H, n)))
                carry_dve()
                nc.vector.bn_aggr(a2["mv"][:], a2["st"][:]).then_inc(a2["s_stat"], 1)
                dve.wait_ge(a2["s_rstd"], n + 1)
                normed(a2["xin"][:], of_group(H, n), a2["mv"][:, 0:1], a2["rs"][:, 1:2])
                normed(a2["res"][:], of_group(H, n), a2["mv"][:, 0:1], a2["rs"][:, 0:1]).then_inc(a2["s_xin"], 1)

            def keys(L, n):
                for c in range(CT):
                    dve.wait_ge(L["s_kT"], CT * (L["at"] + n) + c + 1)
                    nc.vector.tensor_tensor(
                        L["kB"][:, c], L["kT"][:, c, :, None].to_broadcast([128, TOK, HC]),
                        head_of_row[:, None, :].to_broadcast([128, TOK, HC]), ALU.mult).then_inc(L["s_kB"], 1)

            def values(L, n):
                dve.wait_ge(L["s_v_psum"], L["at"] + n + 1)
                for lo, hi, src in ((0, 2, L["b"][0][0:TOK, 0:2 * E]), (2, 3, L["v2_psum"])):
                    w = (hi - lo)
                    v = src.rearrange("p (j h d) -> p j h d", j=w, h=HEADS)
                    m_ = third_of_head[:, None, :, None].to_broadcast([TOK, w, HEADS, HD])
                    last = nc.vector.tensor_tensor(L["vB"][:, lo:hi, :].rearrange("p j (h d) -> p j h d", h=HEADS),
                                                   v, m_, ALU.mult)
                last.then_inc(L["s_vB"], 1)

            def shift(L, n, extra):
                dve.wait_ge(L["s_s_psum"], L["at"] + n + 1)
                for b, (lo, hi) in enumerate(((0, K0), (K0, SEQ))):
                    s = L["b"][1 + b][0:TOK, 0:(hi - lo) * HEADS].rearrange("p (k h) -> p k h", h=HEADS)
                    o = L["sc"][:, lo * HEADS:hi * HEADS].rearrange("p (k h) -> p k h", h=HEADS)
                    if extra == "rel":
                        ins = nc.vector.tensor_tensor(o, s, relb[:, 0, lo * HEADS:hi * HEADS]
                                                      .rearrange("p (k h) -> p k h", h=HEADS), ALU.add)
                    elif extra == "causal":
                        ins = nc.vector.tensor_tensor(o, s, causal[:, lo:hi, None].to_broadcast(
                            [TOK, hi - lo, HEADS]), ALU.add)
                    else:
                        ins = nc.vector.tensor_copy(o, s)
                link(L, n, ins)
                link(L, n, nc.vector.tensor_reduce(L["mx"][:], L["sc"][:].rearrange("p (k h) -> p h k", h=HEADS),
                                                   AX.X, ALU.max))
                s = L["sc"][:].rearrange("p (k h) -> p k h", h=HEADS)
                nc.vector.tensor_tensor(s, s, L["mx"][:, None, :].to_broadcast([TOK, SEQ, HEADS]), ALU.subtract)\
                    .then_inc(L["s_shifted"], 1)

            def normalise(L, n):
                dve.wait_ge(L["s_exped"], L["at"] + n + 1)
                p = L["pr"][:].rearrange("p (h k) -> p h k", h=HEADS)
                link(L, n, nc.vector.tensor_reduce(L["sm"][:], p, AX.X, ALU.add))
                link(L, n, nc.vector.reciprocal(L["sm"][:], L["sm"][:]))
                nc.vector.tensor_tensor(p, p, L["sm"][:, :, None].to_broadcast([TOK, HEADS, SEQ]), ALU.mult)\
                    .then_inc(L["s_probs"], 1)

            def rel_post(n):
                dve.wait_ge(a1["s_o_psum"], n + 1)
                dve.wait_ge(a1["s_bias_in"], n + 1)
                link(a1, n, nc.vector.tensor_tensor(a1["work"][:], a1["b"][3][0:TOK, 0:E], a1["res"][:], ALU.add))
                link(a1, n, nc.vector.bn_stats(a1["st2"][:], a1["work"][:]))
                carry_dve()
                nc.vector.bn_aggr(a1["mv2"][:], a1["st2"][:]).then_inc(a1["s_stat2"], 1)
                dve.wait_ge(a1["s_rstd2"], n + 1)
                link(a1, n, normed(a1["work2"][:], a1["work"][:], a1["mv2"][:, 0:1], a1["rs2"][:, 0:1]))
                link(a1, n, nc.vector.tensor_tensor(a1["work2"][:], a1["work2"][:], row("a_g"), ALU.mult))
                nc.vector.tensor_tensor(of_group(H, n), a1["work2"][:], a1["hold"][:], ALU.add).then_inc(a1["s_done"], 1)

            def causal_post(n):
                dve.wait_ge(a2["s_o_psum"], n + 1)
                dve.wait_ge(a2["s_bias_in"], n + 1)
                link(a2, n, nc.vector.tensor_tensor(a2["work"][:], a2["b"][3][0:TOK, 0:E], a2["hold"][:], ALU.add))

            def gqa_pre(n, body):
                dve.wait_ge(ln["s_done"], n + 1)
                carry_dve()
                link(a3, body, nc.vector.bn_stats(a3["st"][:], of_group(H, n)))
                carry_dve()
                nc.vector.bn_aggr(a3["mv"][:], a3["st"][:]).then_inc(a3["s_stat"], 1)
                dve.wait_ge(a3["s_rstd"], a3["at"] + n + 1)
                dve.wait_ge(a3["s_bias_in"], a3["at"] + n)
                normed(a3["xin"][:], of_group(H, n), a3["mv"][:, 0:1], a3["rs"][:, 0:1]).then_inc(a3["s_xin"], 1)

            def logits_in(n, s_in, s_done_, src, bias):
                dve.wait_ge(s_in, n + 1)
                dst = LOGITS[:].rearrange("p g e -> p (g e)")[:, bass.ds(n * EXPERTS, EXPERTS)]
                if bias:
                    nc.vector.tensor_tensor(dst, src, br0[:], ALU.add).then_inc(s_done_, 1)
                else:
                    nc.vector.tensor_copy(dst, src).then_inc(s_done_, 1)

            def causal_norm(n, first=False):
                link(a2, n, nc.vector.bn_stats(a2["st2"][:], a2["work"][:]))
                carry_dve()
                nc.vector.bn_aggr(a2["mv2"][:], a2["st2"][:]).then_inc(a2["s_stat2"], 1)
                nc.vector.tensor_tensor(of_group(H, n), of_group(H, n), a2["work"][:], ALU.add).then_inc(a2["s_done"], 1)
                dve.wait_ge(a2["s_rstd2"], n + 1)
                if not first:
                    dve.wait_ge(s_rows, 32 * n)
                normed(a2["work2"][:], a2["work"][:], a2["mv2"][:, 0:1], a2["rs2"][:, 0:1]).then_inc(a2["s_in2"], 1)
                end_links(a2)

            def gqa_post(n):
                dve.wait_ge(a3["s_o_psum"], a3["at"] + n + 1)
                dve.wait_ge(a3["s_bias_in"], a3["at"] + n + 1)
                link(a3, n, nc.vector.tensor_tensor(a3["work"][:], a3["b"][3][0:TOK, 0:E], a3["hold"][:], ALU.add))
                link(a3, n, nc.vector.bn_stats(a3["st2"][:], a3["work"][:]))
                carry_dve()
                link(a3, n, nc.vector.bn_aggr(a3["mv2"][:], a3["st2"][:]))
                nc.vector.scalar_tensor_tensor(a3["va2"][:], a3["mv2"][:, 0:1], a3["mv2"][:, 0:1], a3["mv2"][:, 1:2],
                                               ALU.mult, ALU.add).then_inc(a3["s_stat2"], 1)

            def gqa_normed(n):
                dve.wait_ge(a3["s_rstd2"], a3["at"] + n + 1)
                dve.wait_ge(s_rows, 32 * (GROUPS + n))
                nc.vector.scalar_tensor_tensor(a3["work2"][:], a3["work"][:], a3["rs2"][:, 0:1], row("g_n1"),
                                               ALU.mult, ALU.mult).then_inc(a3["s_in2"], 1)

            dve.wait_ge(s_const, 16 * N_CONST)
            def first_layer(n, causal=True, last=False):
                m = n - 1
                if causal:
                    causal_pre(m)
                keys(a1, n)
                values(a1, n)
                if causal:
                    keys(a2, m)
                    values(a2, m)
                    shift(a2, m, "causal")
                    normalise(a2, m)
                dve.wait_ge(s_relsum, n + 1)
                shift(a1, n, "rel")
                if not last:
                    rel_embed(n + 1, n)
                normalise(a1, n)
                if not last:
                    rel_norm(n + 1)
                if causal:
                    causal_post(m)
                    causal_norm(m)
                rel_post(n)
                if not last:
                    assert link_no["rel"] == DVE_LINKS["rel"] + 2
                    link_no["rel"] = 2
                if causal:
                    logits_in(m, s_log, s_lg, logits0_psum, True)

            rel_embed(0, None)
            rel_norm(0)
            first_layer(0, causal=False)
            dve.wait_ge(s_rest, 16 * N_REST)
            carry_dve()
            with dve.Fori(1, GROUPS - 1) as n:
                first_layer(n)
            first_layer(GROUPS - 1, last=True)
            moe_links = [0]
            chosen, prefix = tmp8[1], tmp8[2]

            def mlink(ins):
                moe_links[0] += 1
                ins.then_inc(s_links, 1)
                dve.wait_ge(s_links, moe_links[0])

            def cut_groups(part):
                lo, hi = PARTS[part]
                return (lambda x: x[:, lo:hi, :]), (lambda x: x[:, lo:hi]), \
                    (lambda x: x[:, lo:hi, None].to_broadcast([TOK, hi - lo, EXPERTS])), [TOK, hi - lo, EXPERTS]

            def choose0(part):
                lo, hi = PARTS[part]
                of, of1, wide, shape = cut_groups(part)
                dve.wait_ge(s_lg, hi)
                for g in range(lo, hi):
                    last = nc.vector.max(top8[:, g, :], LOGITS[:, g, :])
                mlink(last)
                nc.vector.tensor_tensor(of(tmp8[0]), of(LOGITS), of(top8)[:, :, 0:1].to_broadcast(shape), ALU.subtract)\
                    .then_inc(s_shifted0, 1)
                mlink(nc.vector.tensor_tensor(of(tmp8[4]), of(LOGITS), of(top8)[:, :, 1:2].to_broadcast(shape), ALU.is_ge))
                dve.wait_ge(m0["s_exp"], part + 1)
                mlink(nc.vector.tensor_tensor(of(tmp8[3]), of(tmp8[1]), of(tmp8[4]), ALU.mult))
                mlink(nc.vector.tensor_copy(of(chosen), of(tmp8[4])))
                count_before(m0, part)
                mlink(nc.vector.tensor_reduce(of1(tmp1[0]), of(tmp8[3]), AX.X, ALU.add))
                mlink(nc.vector.reciprocal(of1(tmp1[0]), of1(tmp1[0])))
                mlink(nc.vector.tensor_tensor(of(GATE), of(tmp8[3]), wide(tmp1[0]), ALU.mult))

            def choose1(part):
                of, of1, wide, shape = cut_groups(part)
                p, left, first, eq, score = tmp8[0], tmp8[3], tmp8[4], tmp8[5], picked
                rev = rev8[:, None, :].to_broadcast(shape)

                def pick(src, out):
                    mlink(nc.vector.tensor_reduce(of1(tmp1[0]), of(src), AX.X, ALU.max))
                    mlink(nc.vector.tensor_tensor(of(eq), of(src), wide(tmp1[0]), ALU.is_ge))
                    mlink(nc.vector.tensor_tensor(of(score), of(eq), rev, ALU.mult))
                    mlink(nc.vector.tensor_reduce(of1(tmp1[1]), of(score), AX.X, ALU.max))
                    mlink(nc.vector.tensor_tensor(of(out), of(score), wide(tmp1[1]), ALU.is_equal))

                dve.wait_ge(m1["s_exp"], part + 1)
                mlink(nc.vector.tensor_scalar(of(p), of(p), 1.0, None, ALU.add))
                mlink(nc.vector.reciprocal(of(p), of(p)))
                pick(p, first)
                mlink(nc.vector.scalar_tensor_tensor(of(left), of(first), -2.0, of(p), ALU.mult, ALU.add))
                pick(left, chosen)
                mlink(nc.vector.tensor_tensor(of(chosen), of(chosen), of(first), ALU.add))
                mlink(nc.vector.tensor_tensor(of(left), of(p), of(chosen), ALU.mult))
                count_before(m1, part)
                mlink(nc.vector.tensor_reduce(of1(tmp1[0]), of(left), AX.X, ALU.add))
                mlink(nc.vector.tensor_scalar(of1(tmp1[0]), of1(tmp1[0]), EPS_R, None, ALU.add))
                mlink(nc.vector.reciprocal(of1(tmp1[1]), of1(tmp1[0])))
                mlink(nc.vector.tensor_tensor(of(GATE), of(left), wide(tmp1[1]), ALU.mult))

            def count_before(M, part):
                if part:
                    nc.vector.tensor_scalar(chosen[:, GROUPS - 1, :], chosen[:, GROUPS - 1, :], real[:, 0:1], None,
                                            ALU.mult).then_inc(M["s_chosen"], 1)
                else:
                    mlink(nc.vector.memset(prefix[:, 0, :], 0.0))
                    for g in range(1, GROUPS):
                        ins = nc.vector.tensor_tensor(prefix[:, g, :], prefix[:, g - 1, :], chosen[:, g - 1, :], ALU.add)
                        if g < GROUPS - 1:
                            mlink(ins)
                    ins.then_inc(M["s_chosen"], 1)
                dve.wait_ge(M["s_chosen"], part + 1)

            def entries(link_, k, lo=0, hi=GROUPS):
                def of(x):
                    return x[:, lo:hi, :]
                link_(nc.vector.scalar_tensor_tensor(of(picked), of(order), float(k), of(tmp8[4]), ALU.is_equal, ALU.mult))
                link_(nc.vector.tensor_tensor(of(tmp8[3]), of(picked), of(tmp8[5]), ALU.mult))
                link_(nc.vector.tensor_reduce(tmp1[0][:, lo:hi], of(tmp8[3]), AX.X, ALU.add))
                link_(nc.vector.tensor_scalar(slot[:, k, lo:hi], tmp1[0][:, lo:hi], float(FAR), None, ALU.add))
                link_(nc.vector.tensor_tensor(of(picked), of(picked), of(GATE), ALU.mult))
                return nc.vector.tensor_reduce(entry[:, k, lo:hi, 1], of(picked), AX.X, ALU.add)

            def list_entries(M, part):
                lo, hi = PARTS[part]
                of, of1, wide, shape = cut_groups(part)
                i_ = M["i"]
                mlink(nc.vector.memset(of(order)[:, :, 0:1], 0.0))
                for e in range(1, EXPERTS):
                    mlink(nc.vector.tensor_tensor(of(order)[:, :, e:e + 1], of(order)[:, :, e - 1:e],
                                                  of(chosen)[:, :, e - 1:e], ALU.add))
                dve.wait_ge(M["s_rank_psum"], part + 1)
                rank = bank[0][0:TOK, lo * EXPERTS:hi * EXPERTS].rearrange("p (g e) -> p g e", e=EXPERTS)
                mlink(nc.vector.tensor_tensor(of(tmp8[5]), rank, slot_base[:, i_, None, :].to_broadcast(shape), ALU.add))
                if M is m1:
                    mlink(nc.vector.scalar_tensor_tensor(of(tmp8[4]), rank, float(CAPACITY), of(chosen), ALU.is_lt, ALU.mult))
                else:
                    mlink(nc.vector.tensor_copy(of(tmp8[4]), of(chosen)))
                for k in range(2):
                    ins = entries(mlink, k, lo, hi)
                    if k == 0:
                        mlink(ins)
                ins.then_inc(M["s_entries"], 1)
                dve.wait_ge(M["s_entries"], part + 1)

            def plan_tiles(M):
                i_ = M["i"]
                n = GROUPS * EXPERTS
                whole = M["tiles"] - 1
                count = bank[0][0:1, n:n + EXPERTS]
                tiles, at, last = (plan_f[0:1, i_, j, :] for j in range(3))
                mlink(nc.vector.tensor_tensor(over[:, :, 0:whole], count[:, :, None].to_broadcast([1, EXPERTS, whole]),
                                              fulls[:, None, 0:whole].to_broadcast([1, EXPERTS, whole]), ALU.is_gt))
                mlink(nc.vector.tensor_reduce(tiles[:, 0:EXPERTS], over[:, :, 0:whole], AX.X, ALU.add))
                mlink(nc.vector.tensor_copy(last[:, 1:EXPERTS + 1], tiles[:, 0:EXPERTS]))
                mlink(nc.vector.tensor_scalar(tiles[:, 0:EXPERTS], tiles[:, 0:EXPERTS], 1.0, None, ALU.add))
                mlink(nc.vector.memset(tiles[:, EXPERTS:EXPERTS + 1], 0.0))
                mlink(nc.vector.memset(last[:, 0:1], 0.0))
                mlink(nc.vector.memset(at[:, 0:1], 0.0))
                if M is m0:
                    mlink(nc.vector.tensor_reduce(ties_f[:], count, AX.X, ALU.add))
                    mlink(nc.vector.tensor_scalar(ties[:], ties_f[:], -2.0 * IMAGES * SEQ, None, ALU.add))
                for e in range(EXPERTS):
                    mlink(nc.vector.tensor_tensor(at[:, e + 1:e + 2], at[:, e:e + 1], tiles[:, e:e + 1], ALU.add))
                nc.vector.tensor_copy(plan[0:1, i_, :, :], plan_f[0:1, i_, :, :]).then_inc(M["s_plan"], 1)
                dve.wait_ge(M["s_plan"], 1)
                if M is m0:
                    links = [0]

                    def tie_link(ins):
                        links[0] += 1
                        ins.then_inc(s_tie_links, 1)
                        dve.wait_ge(s_tie_links, links[0])

                    more = dve.value_load(ties[0:1, 0:1], min_val=0, max_val=EXPERTS * IMAGES * SEQ)
                    with dve.If(more > 0):
                        for k in range(2, EXPERTS):
                            tie_link(entries(tie_link, k))
                        assert links[0] == TIE_LINKS
                    dve.nop()

            m = GROUPS - 1
            causal_pre(m)
            choose0(0)
            keys(a2, m)
            values(a2, m)
            list_entries(m0, 0)
            shift(a2, m, "causal")
            normalise(a2, m)
            causal_post(m)
            causal_norm(m)
            logits_in(m, s_log, s_lg, logits0_psum, True)
            choose0(1)
            list_entries(m0, 1)
            plan_tiles(m0)

            def weigh(M, bias):
                def out_of(u, b, e, t):
                    dve.wait_ge(M["s_down"], u + 1)
                    carry_dve()
                    dve.wait_ge(M["s_added"], 16 * u)
                    carry_dve()
                    at = (e * M["tiles"] + t) * 2
                    nc.vector.tensor_copy(out_row[:].bitcast(U32), lists_in[:, bass.ds(at, 1)].bitcast(U32))
                    src = bank[5][:, 0:E]
                    if bias:
                        nc.vector.tensor_tensor(y_sum[:], src, b_dn[b][:], ALU.add).then_inc(s_y_sum, 1)
                        dve.wait_ge(s_y_sum, u)
                        src = y_sum[:]
                    nc.vector.tensor_scalar(y_rows[:], src, lists_in[:, bass.ds(at + 1, 1)], None, ALU.mult)\
                        .then_inc(M["s_y"], 1)

                def last_of(e):
                    return dve.value_load(plan[0:1, M["i"], 2, e:e + 1] if isinstance(e, int) else
                                          plan[0:1, M["i"], 2, bass.ds(e, 1)], min_val=0, max_val=M["tiles"] - 1)

                def tile(i, b, e, t, parity, u):
                    if is_first(t):
                        after_first(dve, i, b, t, lambda: out_of(u, (b - 1) % BUFS, nc.s_assert_within(
                            e - 1, 0, EXPERTS - 1), last_of(e)))
                        if bias:
                            dve.wait_ge(s_weights[b], weights_there(M, i, b))
                            carry_dve()
                    else:
                        out_of(u, b, e, t - 1)

                dve.sem_inc(M["s_y"], 1)
                dve.wait_ge(s_lists, 16 * (M["i"] + 1))
                walk(dve, M, tile)
                out_of(tiles_so_far(dve, M), (EXPERTS - 1) % BUFS, EXPERTS - 1, last_of(EXPERTS))

            weigh(m0, True)
            dve.wait_ge(s_back[0], 16)

            def cos_pre(n):
                nc.vector.bn_stats(ln["st"][:], of_group(H, n)).then_inc(ln["s_dve"], 1)
                dve.wait_ge(ln["s_dve"], n * LN_LINKS + 1)
                carry_dve()
                nc.vector.bn_aggr(ln["mv"][:], ln["st"][:]).then_inc(ln["s_stat"], 1)
                dve.wait_ge(ln["s_rstd"], n + 1)
                normed(ln["xin"][:], of_group(H, n), ln["mv"][:, 0:1], ln["rs"][:, 0:1]).then_inc(ln["s_xin"], 1)

            def cos_qkv(n):
                dve.wait_ge(ln["s_qkv_psum"], n + 1)
                for i, b in enumerate(("l_bq", "l_bk", "l_bv")):
                    last = nc.vector.tensor_tensor(ln["q"][:, i, :], ln["b"][1 + i][0:TOK, 0:E], row(b), ALU.add)
                last.then_inc(ln["s_qkv"], 1)

            def cos_lengths(n):
                dve.wait_ge(ln["s_squares"], n + 1)
                nc.vector.tensor_reduce(ln["ss"][:], ln["sq"][:].rearrange("p i (h d) -> p i h d", h=HEADS), AX.X, ALU.add)\
                    .then_inc(ln["s_dve"], 1)
                dve.wait_ge(ln["s_dve"], n * LN_LINKS + 2)
                nc.vector.tensor_scalar(ln["ss"][:], ln["ss"][:], EPS_A ** 2, None, ALU.max).then_inc(ln["s_norm2"], 1)

            def cos_norm(n):
                dve.wait_ge(ln["s_norm"], n + 1)
                qk = ln["q"][:, 0:2, :].rearrange("p i (h d) -> p i h d", h=HEADS)
                nc.vector.tensor_tensor(qk, qk, ln["ri"][:, :, :, None].to_broadcast([TOK, 2, HEADS, HD]), ALU.mult)\
                    .then_inc(ln["s_qn"], 1)
                dve.wait_ge(ln["s_qn"], n + 1)
                nc.vector.tensor_tensor(ln["km"][:], ln["q"][:, 1:2, :].to_broadcast([TOK, PER, E]),
                                        of_image[:, :, None].to_broadcast([TOK, PER, E]), ALU.mult)\
                    .then_inc(ln["s_km"], 1)

            def cos_kv(n):
                dve.wait_ge(ln["s_kv_psum"], n + 1)
                for c in range(CT):
                    last = nc.vector.scalar_tensor_tensor(
                        ln["kv"][:, c, :, :], ln["b"][1 + c][:, 0:PER * 128].rearrange("p (j d) -> p j d", j=PER),
                        inv_scale[:, 1, c:c + 1], same_head[:, None, :].to_broadcast([128, PER, 128]),
                        ALU.mult, ALU.mult)
                last.then_inc(ln["s_kv"], 1)

            def cos_post(n):
                dve.wait_ge(ln["s_o_psum"], n + 1)
                dve.wait_ge(ln["s_bias_in"], n + 1)
                nc.vector.tensor_tensor(of_group(H, n), ln["b"][0][0:TOK, 0:E], ln["hold"][:], ALU.add).then_inc(ln["s_done"], 1)

            dve.wait_ge(s_scale, 2)
            def second_layer(n, gqa=True, last=False):
                m = n - 1
                cos_norm(n)
                if gqa:
                    shift(a3, m, "none")
                    values(a3, m)
                    normalise(a3, m)
                cos_kv(n)
                if not last:
                    cos_pre(n + 1)
                cos_post(n)
                gqa_pre(n, m if gqa else 0)
                if not last:
                    cos_qkv(n + 1)
                if gqa:
                    gqa_post(m)
                if not last:
                    cos_lengths(n + 1)
                if gqa:
                    gqa_normed(m)
                    assert link_no["gqa"] == DVE_LINKS["gqa"] + 1
                    link_no["gqa"] = 1
                keys(a3, n)
                if gqa:
                    logits_in(m, s_glog, s_glg, logits1_psum, False)

            dve.sem_inc(s_glg, 1)
            cos_pre(0)
            cos_qkv(0)
            cos_lengths(0)
            dve.wait_ge(s_back[1], 16)
            second_layer(0, gqa=False)
            with dve.Fori(1, GROUPS - 1) as n:
                second_layer(n)
            second_layer(GROUPS - 1, last=True)
            m = GROUPS - 1
            choose1(0)
            list_entries(m1, 0)
            shift(a3, m, "none")
            values(a3, m)
            normalise(a3, m)
            gqa_post(m)
            gqa_normed(m)
            logits_in(m, s_glog, s_glg, logits1_psum, False)
            choose1(1)
            list_entries(m1, 1)
            plan_tiles(m1)
            weigh(m1, False)

            def last_statistics(k):
                lo, hi = SPANS[k]
                dve.wait_ge(s_back[2 + k], 16)
                for g in range(lo, hi):
                    last = nc.vector.bn_stats(fin["st"][:, g, :], SRC[:, g * E:(g + 1) * E])
                mlink(last)
                for g in range(lo, hi):
                    last = nc.vector.bn_aggr(fin["mv"][:, g, :], fin["st"][:, g, :])
                mlink(last)
                mean, va = fin["mv"][:, lo:hi, 0], fin["va"][:, lo:hi]
                mlink(nc.vector.tensor_tensor(va, mean, mean, ALU.mult))
                nc.vector.tensor_tensor(va, va, fin["mv"][:, lo:hi, 1], ALU.add).then_inc(s_fin_stat, 1)

            def last_rows(k):
                lo, hi = SPANS[k]
                dve.wait_ge(s_fin_rstd, 2 * k + 2)
                for g in range(lo, hi):
                    h = H[:, g * E:(g + 1) * E]
                    dve.wait_ge(s_fin_rows, g + 1)
                    nc.vector.scalar_tensor_tensor(h, SRC[:, g * E:(g + 1) * E], fin["rs"][:, g:g + 1], h,
                                                   ALU.mult, ALU.add).then_inc(s_fin, 1)

            for k in range(len(SPANS)):
                last_statistics(k)
                if k:
                    last_rows(k - 1)
            last_rows(len(SPANS) - 1)

        @block.gpsimd
        def _(pool):
            link_no = {}

            def link(L, n, ins):
                k = link_no[L["tag"]] = link_no.get(L["tag"], 0) + 1
                ins.then_inc(L["s_pool"], 1)
                pool.wait_ge(L["s_pool"], L["pool_at"] + n * POOL_LINKS[L["tag"]] + k)

            def end_links(L):
                assert link_no[L["tag"]] == POOL_LINKS[L["tag"]], (L["tag"], link_no[L["tag"]])
                link_no[L["tag"]] = 0

            def pow_half(out, x):
                return nc.gpsimd.tensor_tensor(out, x, half[:, 0:1], ALU.pow)

            def rel_rstd(n, body=0):
                pool.wait_ge(a1["s_stat"], n + 1)
                link(a1, body, nc.gpsimd.tensor_tensor(a1["va"][:, 0:1], a1["mv"][:, 1:2], eps[:, 0:1], ALU.add))
                pow_half(a1["rs"][:, 0:1], a1["va"][:, 0:1]).then_inc(a1["s_rstd"], 1)

            def rel_biases(n):
                pool.wait_ge(a1["s_xin"], n + 1)
                nc.gpsimd.tensor_tensor(a1["res"][:], a1["xin"][:], row("a_bo"), ALU.add)
                nc.gpsimd.tensor_tensor(a1["hold"][:], a1["h0"][:], row("a_b"), ALU.add).then_inc(a1["s_bias_in"], 1)

            def rel_sum(n):
                pool.wait_ge(s_rel_in, 96 * (n + 1))
                nc.gpsimd.tensor_tensor(relb[:, 0, :], relb[:, 0, :], relb[:, 1, :], ALU.add).then_inc(s_relsum, 1)

            def rel_rstd2(n):
                pool.wait_ge(a1["s_stat2"], n + 1)
                link(a1, n, nc.gpsimd.tensor_tensor(a1["va2"][:], a1["mv2"][:, 1:2], eps[:, 1:2], ALU.add))
                pow_half(a1["rs2"][:], a1["va2"][:]).then_inc(a1["s_rstd2"], 1)

            def causal_rstd(n):
                pool.wait_ge(a2["s_stat"], n + 1)
                nc.gpsimd.tensor_tensor(a2["va"][:, 0:1], a2["mv"][:, 1:2], eps[:, 0:1], ALU.add)
                link(a2, n, nc.gpsimd.tensor_scalar(a2["va"][:, 1:2], a2["mv"][:, 1:2], 1.0 + EPS, EPS * EPS,
                                                    ALU.mult, ALU.add))
                nc.gpsimd.tensor_tensor(a2["rs"][:], a2["va"][:], half[:, 0:1].to_broadcast([TOK, 2]), ALU.pow)\
                    .then_inc(a2["s_rstd"], 1)

            def causal_bias(n):
                pool.wait_ge(a2["s_xin"], n + 1)
                nc.gpsimd.tensor_tensor(a2["hold"][:], a2["res"][:], row("f_bo"), ALU.add).then_inc(a2["s_bias_in"], 1)

            def causal_rstd2(n):
                pool.wait_ge(a2["s_stat2"], n + 1)
                link(a2, n, nc.gpsimd.tensor_tensor(a2["va2"][:], a2["mv2"][:, 1:2], eps[:, 0:1], ALU.add))
                pow_half(a2["rs2"][:], a2["va2"][:]).then_inc(a2["s_rstd2"], 1)

            def list_tokens(M, k, lo, hi, done):
                for g in range(lo, hi):
                    pool.indirect_dma_start(
                        out=LIST_dram[M["i"]], out_offset=bass.IndirectOffsetOnAxis(ap=slot[:, k, g:g + 1], axis=0),
                        in_=entry[:, k, g, :], in_offset=None, bounds_check=EXPERTS * M["slots"] - 1,
                        oob_is_err=False).then_inc(done, 16)

            def list_part(M, part):
                if part == 0:
                    pool.wait_ge(s_init, 16 * 2)
                    pool.wait_ge(m0["s_added"], 16)
                    pool.wait_ge(m1["s_added"], 16)
                pool.wait_ge(M["s_entries"], part + 1)
                for k in range(2):
                    list_tokens(M, k, *PARTS[part], M["s_listed"])

            def add_rows(M):
                i_ = M["i"]

                def wait_alone():
                    pool.sem_inc(s_idle, 1)

                list_part(M, 1)
                pool.wait_ge(M["s_plan"], 1)
                if M is m0:
                    more = pool.value_load(ties[0:1, 0:1], min_val=0, max_val=EXPERTS * IMAGES * SEQ)
                    with pool.If(more > 0):
                        pool.wait_ge(s_tie_links, TIE_LINKS)
                        for k in range(2, EXPERTS):
                            list_tokens(M, k, 0, GROUPS, s_tie_listed)
                    pool.nop()
                pool.wait_ge(s_rows, 32 * GROUPS * (i_ + 1))

                def out_of(u):
                    pool.wait_ge(M["s_y"], u)
                    wait_alone()
                    pool.indirect_dma_start(
                        out=SUM_dram, out_offset=bass.IndirectOffsetOnAxis(ap=out_row[:, 0:1].bitcast(U32), axis=0),
                        in_=y_rows[:], in_offset=None, compute_op=ALU.add, bounds_check=GROUPS * TOK + TILE - 1,
                        oob_is_err=True).then_inc(M["s_added"], 16)

                def tile(i, b, e, t, parity, u):
                    if is_first(t):
                        width = M["tiles"] * 2
                        nc.gpsimd.tensor_copy(list_now[b][:, 0:width].bitcast(U32),
                                              lists_in[:, bass.ds(e * width, width)].bitcast(U32)).then_inc(s_list_now, 1)
                        pool.wait_ge(s_list_now, i_ * EXPERTS + BUFS * i + b + 1)
                        wait_alone()
                    pool.wait_ge(M["s_xT_psum"], u + 1)
                    wait_alone()

                    def before_it():
                        pool.wait_ge(M["s_x_rows"], 16 * u)
                        wait_alone()
                    after_first(pool, i, b, t, before_it)
                    pool.indirect_dma_start(
                        out=x_rows[b][parity][:], out_offset=None, in_=X_dram,
                        in_offset=bass.IndirectOffsetOnAxis(ap=list_now[b][:, 2 * t:2 * t + 1].bitcast(U32), axis=0))\
                        .then_inc(M["s_x_rows"], 16)
                    if t < 2 and b < 2:
                        with pool.If(u > 1):
                            out_of(u)
                    else:
                        out_of(u)

                pool.wait_ge(s_lists, 16 * (i_ + 1))
                walk(pool, M, tile, unroll=True)
                u = tiles_so_far(pool, M)
                out_of(u)
                out_of(u + 1)

            pool.dma_start(X_dram[GROUPS * TOK:], A["c_spare"]).then_inc(m0["s_added"], 16)
            pool.dma_start(SUM_dram[GROUPS * TOK:], A["c_spare"]).then_inc(m1["s_added"], 16)
            nc.gpsimd.memset(half[:], -0.5)
            for i, value in enumerate((EPS, EPS_A, EPS_R)):
                nc.gpsimd.memset(eps[:, i:i + 1], value)
            nc.gpsimd.memset(ones[:], 1.0)
            nc.gpsimd.memset(a2["qM"][:], 0.0)
            nc.gpsimd.memset(a1["qM"][:], 0.0).then_inc(s_zeroed, 1)
            pool.wait_ge(s_zeroed, 1)
            pool.wait_ge(s_const, 16 * N_CONST)
            def first_layer(n, causal=True, last=False):
                m = n - 1
                if causal:
                    causal_rstd(m)
                rel_biases(n)
                if causal:
                    causal_bias(m)
                rel_sum(n)
                if not last:
                    rel_rstd(n + 1, n)
                if causal:
                    causal_rstd2(m)
                rel_rstd2(n)
                if causal:
                    end_links(a2)
                if not last:
                    assert link_no["rel"] == POOL_LINKS["rel"] + 1
                    link_no["rel"] = 1

            rel_rstd(0)
            first_layer(0, causal=False)
            with pool.Fori(1, GROUPS - 1) as n:
                first_layer(n)
            first_layer(GROUPS - 1, last=True)
            m = GROUPS - 1
            causal_rstd(m)
            causal_bias(m)
            list_part(m0, 0)
            causal_rstd2(m)
            add_rows(m0)

            def cos_rstd(n):
                pool.wait_ge(ln["s_stat"], n + 1)
                nc.gpsimd.tensor_tensor(ln["va"][:], ln["mv"][:, 1:2], eps[:, 0:1], ALU.add).then_inc(ln["s_pool"], 1)
                pool.wait_ge(ln["s_pool"], n + 1)
                pow_half(ln["rs"][:], ln["va"][:]).then_inc(ln["s_rstd"], 1)

            def cos_bias(n, first=False):
                if not first:
                    pool.wait_ge(ln["s_done"], n)
                nc.gpsimd.tensor_tensor(ln["hold"][:], of_group(H, n), row("l_bo"), ALU.add).then_inc(ln["s_bias_in"], 1)

            def cos_inverse(n):
                pool.wait_ge(ln["s_norm2"], n + 1)
                nc.gpsimd.tensor_tensor(ln["ri"][:].rearrange("p i h -> p (i h)"), ln["ss"][:].rearrange("p i h -> p (i h)"),
                                        half[:, 0:1].to_broadcast([TOK, 2 * HEADS]), ALU.pow).then_inc(ln["s_norm"], 1)

            def gqa_rstd(n, body):
                pool.wait_ge(a3["s_stat"], a3["at"] + n + 1)
                link(a3, body, nc.gpsimd.tensor_tensor(a3["va"][:, 0:1], a3["mv"][:, 1:2], eps[:, 0:1], ALU.add))
                pow_half(a3["rs"][:, 0:1], a3["va"][:, 0:1]).then_inc(a3["s_rstd"], 1)

            def gqa_bias(n):
                pool.wait_ge(a3["s_xin"], a3["at"] + n + 1)
                nc.gpsimd.tensor_tensor(a3["hold"][:], a3["xin"][:], row("g_ob"), ALU.add).then_inc(a3["s_bias_in"], 1)

            def gqa_rstd2(n):
                pool.wait_ge(a3["s_stat2"], a3["at"] + n + 1)
                link(a3, n, nc.gpsimd.tensor_tensor(a3["rs"][:, 1:2], a3["va2"][:], eps[:, 2:3], ALU.add))
                pow_half(a3["rs2"][:], a3["rs"][:, 1:2]).then_inc(a3["s_rstd2"], 1)

            def second_layer(n, gqa=True, last=False):
                m = n - 1
                cos_inverse(n)
                if gqa:
                    gqa_bias(m)
                cos_bias(n, first=not gqa)
                if not last:
                    cos_rstd(n + 1)
                gqa_rstd(n, m if gqa else 0)
                if gqa:
                    gqa_rstd2(m)
                    assert link_no["gqa"] == POOL_LINKS["gqa"] + 1
                    link_no["gqa"] = 1

            cos_rstd(0)
            second_layer(0, gqa=False)
            with pool.Fori(1, GROUPS - 1) as n:
                second_layer(n)
            second_layer(GROUPS - 1, last=True)
            m = GROUPS - 1
            gqa_bias(m)
            list_part(m1, 0)
            gqa_rstd2(m)
            add_rows(m1)
            for k, (lo, hi) in enumerate(SPANS):
                pool.wait_ge(s_fin_stat, k + 1)
                va, rs = fin["va"][:, lo:hi], fin["rs"][:, lo:hi]
                nc.gpsimd.tensor_scalar(va, va, EPS_R, None, ALU.add).then_inc(s_fin_rstd, 1)
                pool.wait_ge(s_fin_rstd, 2 * k + 1)
                nc.gpsimd.tensor_tensor(rs, va, half[:, 0:1].to_broadcast([TOK, hi - lo]), ALU.pow)\
                    .then_inc(s_fin_rstd, 1)
                for g in range(lo, hi):
                    x = SRC[:, g * E:(g + 1) * E]
                    nc.gpsimd.tensor_tensor(x, x, row("g_n2"), ALU.mult).then_inc(s_fin_rows, 1)


def _by_tile(w):
    return w.reshape(w.shape[0] // 128, 128, -1).transpose(1, 0, 2)


def _layout(i):
    f = np.float32
    a = {}
    x = i["x"].reshape(IMAGES, 3, SIDE, PATCH, SIDE, PATCH).transpose(1, 3, 5, 0, 2, 4)
    x = x.reshape(PK * 128, IMAGES, SIDE * SIDE)
    xt = np.zeros((PK * 128, GROUPS * PER, SEQ), f)
    xt[:, :IMAGES, 1:] = x
    a["xT"] = np.ascontiguousarray(xt.reshape(PK, 128, GROUPS, TOK).transpose(2, 1, 0, 3))
    base = np.empty((PER, SEQ, E), f)
    base[:, 0] = i["cls_tok"].reshape(E)
    base[:, 1:] = i["L0_tok_b"]
    a["base"] = base.reshape(TOK, E)
    a["wtok"] = _by_tile(i["L0_tok_W"])
    per_kv = HEADS // (i["L1_ffn_kw"].shape[1] // HD)

    def spread(w):
        return np.repeat(w.reshape(w.shape[:-1] + (-1, HD)), per_kv, axis=-2).reshape(w.shape[:-1] + (E,))

    mats = {f"{p}_W{w}": i[f"{l}_W{w}"] for p, l in (("a", "L0_attn"), ("f", "L0_ffn"), ("l", "L1_attn"))
            for w in "qkvo"}
    mats |= {"g_Wq": i["L1_ffn_qw"], "g_Wk": spread(i["L1_ffn_kw"]), "g_Wv": spread(i["L1_ffn_vw"]),
             "g_Wo": i["L1_ffn_ow"]}
    a["mats"] = np.stack([_by_tile(mats[n]) for n in MATS], 1)
    rows = {"a_bo": i["L0_attn_bo"], "a_g": i["L0_attn_ln_gamma"], "a_b": i["L0_attn_ln_beta"],
            "f_bo": i["L0_ffn_bo"], "l_bq": i["L1_attn_bq"], "l_bk": i["L1_attn_bk"], "l_bv": i["L1_attn_bv"],
            "l_bo": i["L1_attn_bo"], "g_ob": i["L1_ffn_ob"], "g_n1": i["L1_ffn_norm1_w"],
            "g_n2": i["L1_ffn_norm2_w"]}
    a["rows"] = np.stack([rows[n] for n in ROWS])
    cols = {f"{p}_b{w}": i[f"{l}_b{w}"] for p, l in (("a", "L0_attn"), ("f", "L0_ffn")) for w in "qkv"}
    cols |= {"f_g1": i["L0_ffn_ln1_g"], "f_b1": i["L0_ffn_ln1_b"], "f_g2": i["L0_ffn_ln2_g"],
             "f_b2": i["L0_ffn_ln2_b"], "g_qb": i["L1_ffn_qb"], "g_kb": spread(i["L1_ffn_kb"]),
             "g_vb": spread(i["L1_ffn_vb"]), "l_m": np.repeat(i["L1_attn_m"], HD)}
    a["cols"] = np.stack([cols[n].reshape(CT, 128).T for n in COLS], 1)
    emb = i["L0_attn_dist_emb"]
    last = emb.shape[0] // 2
    near = emb[last - (SEQ - 1):last + SEQ]
    for n, t in (("relq", near[::-1]), ("relk", near)):
        wide = np.zeros((HC, HD, REL, HC), f)
        for h in range(HC):
            wide[h, :, :, h] = t.T
        a[n] = wide.reshape(128, REL, HC)
    a["wr0"], a["wr1"] = _by_tile(i["L0_ffn_Wr"]), _by_tile(i["L1_ffn_gate_w"])
    a["br0"] = i["L0_ffn_br"]
    a["eb1"] = i["L0_ffn_e_b1"].reshape(EXPERTS, F0 // 128, 128).transpose(0, 2, 1)
    a["eb2"] = i["L0_ffn_e_b2"]
    for n, w in (("e_w1", "L0_ffn_e_w1"), ("e_w2", "L0_ffn_e_w2"), ("g_w1", "L1_ffn_w1"), ("g_w2", "L1_ffn_w2")):
        w = i[w]
        a[n] = w.reshape(EXPERTS, w.shape[1] // 128, 128, -1).transpose(0, 2, 1, 3).reshape(EXPERTS, 128, -1)
    p, t = np.arange(128), np.arange(TOK)
    a["c_ident"] = np.eye(128, dtype=f)
    a["c_head_of_row"] = (p[:, None] // HD == np.arange(HC)).astype(f)
    a["c_third"] = (t[:, None] // SEQ == np.arange(HEADS) % HPC).astype(f)
    a["c_causal"] = np.where(np.arange(SEQ) > t[:, None] % SEQ, f(MASKED), f(0))
    a["c_of_image"] = (t[:, None] // SEQ == np.arange(PER)).astype(f)
    a["c_same_head"] = (p[:, None] // HD == p // HD).astype(f)
    a["c_before"] = (t[:, None] < t).astype(f)
    expert = np.arange(EXPERTS)
    first_slot = np.stack([expert * n for n in SLOTS]).astype(f)
    a["c_slot_base"] = np.broadcast_to(first_slot - f(FAR), (TOK, 2, EXPERTS))
    a["c_real"] = (t[:, None] < LAST_REAL).astype(f)
    a["c_fulls"] = (np.arange(1, TILES[0]) * TILE).astype(f)[None]
    entry = np.zeros((TOK, EXPERTS, GROUPS, 2), np.int32)
    entry[..., 0] = t[:, None, None] + TOK * np.arange(GROUPS)
    a["c_entry"] = entry.view(f)
    for k, n in enumerate(SLOTS):
        empty = np.zeros((EXPERTS * n, 2), np.int32)
        empty[:, 0] = GROUPS * TOK + np.arange(EXPERTS * n) % TILE
        a[f"c_list{k}"] = empty.view(f)
    a["c_spare"] = np.zeros((TILE, E), f)
    a["c_rev8"] = np.broadcast_to((EXPERTS - np.arange(EXPERTS)).astype(f), (TOK, EXPERTS))
    return {n: np.ascontiguousarray(v) for n, v in a.items()}


def kernel(**inputs):
    import concourse.bacc as bacc
    from concourse.bass_utils import run_bass_kernel_spmd

    arrays = _layout({n: np.asarray(v) for n, v in inputs.items()})
    nc = bacc.Bacc("TRN2", target_bir_lowering=False, num_devices=1)
    A = {n: nc.dram_tensor("in_" + n, v.shape, mybir.dt.from_np(v.dtype), kind="ExternalInput").ap()
         for n, v in arrays.items()}
    A["out"] = nc.dram_tensor("out", (TOK, GROUPS * E), F32, kind="ExternalOutput").ap()
    build_tower(nc, A)
    r = run_bass_kernel_spmd(nc, [{"in_" + n: v for n, v in arrays.items()}], core_ids=[0])
    out = r.results[0]["out"].reshape(PER, SEQ, GROUPS, E).transpose(2, 0, 1, 3)
    return np.ascontiguousarray(out.reshape(GROUPS * PER, SEQ, E)[:IMAGES])
```
